# Optimizing a Trainium2 kernel written in Bass

```python
import numpy as np
import jax
import jax.numpy as jnp

def _softmax(x, axis=-1):
    return jax.nn.softmax(x, axis=axis)

def _gelu(x):
    return jax.nn.gelu(x, approximate=True)

def _silu(x):
    return jax.nn.silu(x)

def _sigmoid(x):
    return jax.nn.sigmoid(x)

def _layernorm(x, axis=-1, eps=1e-05):
    m = jnp.mean(x, axis=axis, keepdims=True)
    v = jnp.var(x, axis=axis, keepdims=True)
    return (x - m) / jnp.sqrt(v + eps)

def _scatter_add(tgt, idx, src, axis=0):
    return tgt.at[idx].add(src)

def _segment_sum(src, seg, n):
    return jax.ops.segment_sum(src, seg, n)
kernel_name = 'mk_macaron_d2_jaxref_r8_d09a91'

def setup_inputs(seed: int=0):
    np.random.seed(seed)
    _w = jnp.asarray

    def _L0_attn_setup():
        import jax, jax.numpy as jnp
        import numpy as np
        B, S, D, H = (2, 256, 128, 16)
        HD = D // H
        key = jax.random.key(seed)
        ks = jax.random.split(key, 5)
        scale = 1.0 / np.sqrt(D)
        x = jax.random.normal(ks[0], (B, S, D), dtype=jnp.float32)
        W_Q = jax.random.uniform(ks[1], (D, D), jnp.float32, -scale, scale)
        W_K = jax.random.uniform(ks[2], (D, D), jnp.float32, -scale, scale)
        W_V = jax.random.uniform(ks[3], (D, D), jnp.float32, -scale, scale)
        W_O = jax.random.uniform(ks[4], (D, D), jnp.float32, -scale, scale)
        return {'x': x, 'W_Q': W_Q, 'W_K': W_K, 'W_V': W_V, 'W_O': W_O}
    _L0_attn_in = _L0_attn_setup()

    def _L0_ffn_setup():
        import math
        import jax, jax.numpy as jnp
        import numpy as np
        B, T, H = (4, 256, 128)
        E, K, F = (8, 2, 256)
        CAP_FACTOR = 1.25

        def _moe_forward(x, Wg, W_in, W_out):
            b, t, h = x.shape
            xf = x.reshape(-1, h)
            S = xf.shape[0]
            C = int(math.ceil(K * S / E * CAP_FACTOR))
            logits = xf @ Wg
            probs = jax.nn.softmax(logits, axis=-1)
            top_vals, top_idx = jax.lax.top_k(probs, K)
            flat_idx = top_idx.T.reshape(-1)
            onehot = jax.nn.one_hot(flat_idx, E, dtype=jnp.int32)
            cum = jnp.cumsum(onehot, axis=0) - 1
            loc = jnp.take_along_axis(cum, flat_idx[:, None], axis=1)[:, 0]
            loc = loc.reshape(K, S).T
            keep = loc < C
            gates = top_vals * keep.astype(top_vals.dtype)
            denom = jnp.maximum(gates.sum(-1, keepdims=True), 1e-09)
            gates = gates / denom
            loc_c = jnp.where(keep, loc, C)
            e_flat = top_idx.reshape(-1)
            l_flat = loc_c.reshape(-1)
            xk = jnp.broadcast_to(xf[:, None, :], (S, K, h)).reshape(-1, h)
            xk = jnp.where(keep.reshape(-1, 1), xk, 0.0)
            buf = jnp.zeros((E, C + 1, h), x.dtype).at[e_flat, l_flat].set(xk)
            inp = buf[:, :C]
            hid = jnp.einsum('ech,ehf->ecf', inp, W_in)
            a, g = jnp.split(hid, 2, axis=-1)
            hid = jax.nn.gelu(a, approximate=False) * g
            out_e = jnp.einsum('ecf,efh->ech', hid, W_out)
            out_pad = jnp.concatenate([out_e, jnp.zeros((E, 1, h), out_e.dtype)], axis=1)
            gathered = out_pad[e_flat, l_flat].reshape(S, K, h)
            y = (gathered * gates[..., None]).sum(axis=1)
            return y.reshape(b, t, h)
        key = jax.random.key(seed)
        k1, k2, k3, k4 = jax.random.split(key, 4)
        x = jax.random.normal(k1, (B, T, H), dtype=jnp.float32)
        Wg = jax.random.normal(k2, (H, E), dtype=jnp.float32) * 0.02
        W_in = jax.random.normal(k3, (E, H, 2 * F), dtype=jnp.float32) * (1.0 / math.sqrt(H))
        W_out = jax.random.normal(k4, (E, F, H), dtype=jnp.float32) * (1.0 / math.sqrt(F))
        return {'x': x, 'Wg': Wg, 'W_in': W_in, 'W_out': W_out}
    _L0_ffn_in = _L0_ffn_setup()

    def _L1_attn_setup():
        import jax, jax.numpy as jnp
        import numpy as np
        from jax import lax
        B, L, D, K = (4, 512, 128, 3)
        H = 256

        def _layernorm(h, g, b):
            m = jnp.mean(h, axis=-1, keepdims=True)
            v = jnp.mean((h - m) ** 2, axis=-1, keepdims=True)
            return (h - m) / jnp.sqrt(v + 1e-05) * g + b
        key = jax.random.key(seed)
        ks = jax.random.split(key, 16)
        s = 0.02
        return {'x': jax.random.normal(ks[0], (B, L, D), jnp.float32), 'ln1_g': jnp.ones((D,), jnp.float32), 'ln1_b': jnp.zeros((D,), jnp.float32), 'in_W': jax.random.normal(ks[1], (D, 2 * D), jnp.float32) * s, 'in_b': jnp.zeros((2 * D,), jnp.float32), 'dw_W': jax.random.normal(ks[2], (D, 1, K), jnp.float32) * s, 'dw_b': jnp.zeros((D,), jnp.float32), 'dt_W': jax.random.normal(ks[3], (D, D), jnp.float32) * s, 'dt_b': jnp.zeros((D,), jnp.float32), 'b_W': jax.random.normal(ks[4], (D, D), jnp.float32) * s, 'b_b': jnp.zeros((D,), jnp.float32), 'c_W': jax.random.normal(ks[5], (D, D), jnp.float32) * s, 'c_b': jnp.zeros((D,), jnp.float32), 'a_log': jnp.zeros((D,), jnp.float32), 'd_skip': jnp.ones((D,), jnp.float32), 'out_W': jax.random.normal(ks[6], (D, D), jnp.float32) * s, 'out_b': jnp.zeros((D,), jnp.float32), 'ln2_g': jnp.ones((D,), jnp.float32), 'ln2_b': jnp.zeros((D,), jnp.float32), 'f1_W': jax.random.normal(ks[7], (D, H), jnp.float32) * s, 'f1_b': jnp.zeros((H,), jnp.float32), 'f2_W': jax.random.normal(ks[8], (H, D), jnp.float32) * s, 'f2_b': jnp.zeros((D,), jnp.float32)}
    _L1_attn_in = _L1_attn_setup()

    def _L1_ffn_setup():
        import jax, jax.numpy as jnp
        import numpy as np
        B, T, C = (2, 256, 128)
        H, D = (16, 64)
        CR = 8
        R = C // CR
        ROPE = D // 2
        NOPE = D - ROPE
        E, K, I, S = (8, 2, 64, 1)
        THETA = 100000.0
        EPS = 1e-05

        def _rmsnorm(x, w):
            rms = jnp.sqrt(jnp.mean(x * x, axis=-1, keepdims=True) + EPS)
            return w * (x / rms)

        def _rope(xh):
            d = xh.shape[-1]
            t = jnp.arange(xh.shape[2], dtype=jnp.float32)
            freqs = 1.0 / THETA ** (jnp.arange(0, d, 2, dtype=jnp.float32) / d)
            ang = jnp.outer(t, freqs)
            cos, sin = (jnp.cos(ang), jnp.sin(ang))
            xr = xh.reshape(xh.shape[:-1] + (d // 2, 2))
            x0, x1 = (xr[..., 0], xr[..., 1])
            rot = jnp.stack([x0 * cos - x1 * sin, x0 * sin + x1 * cos], axis=-1)
            return rot.reshape(xh.shape)

        def _attention(x, Wq, Wkva, Wkvb, Wo):
            b, t, _ = x.shape
            q = (x @ Wq).reshape(b, t, H, D).transpose(0, 2, 1, 3)
            ckv = x @ Wkva
            kv_latent, k_rope = (ckv[:, :, :R], ckv[:, :, R:])
            kv = (kv_latent @ Wkvb).reshape(b, t, H, NOPE).transpose(0, 2, 1, 3)
            k_rope = jnp.broadcast_to(k_rope[:, None, :, :], (b, H, t, ROPE))
            q_nope, q_rope = (q[..., :NOPE], q[..., NOPE:])
            q = jnp.concatenate([q_nope, _rope(q_rope)], axis=-1)
            k = jnp.concatenate([kv, _rope(k_rope)], axis=-1)
            v = jnp.concatenate([kv, jnp.zeros_like(k_rope)], axis=-1)
            att = jnp.einsum('bhqd,bhkd->bhqk', q, k) / jnp.sqrt(jnp.float32(D))
            mask = jnp.tril(jnp.ones((t, t), dtype=bool))
            att = jnp.where(mask, att, jnp.float32(-jnp.inf))
            att = jax.nn.softmax(att, axis=-1)
            y = jnp.einsum('bhqk,bhkd->bhqd', att, v)
            y = y.transpose(0, 2, 1, 3).reshape(b, t, H * D)
            return y @ Wo

        def _experts(x_flat, Wg, Wu, Wd):
            g = jax.nn.silu(jnp.einsum('nc,eci->nei', x_flat, Wg))
            u = jnp.einsum('nc,eci->nei', x_flat, Wu)
            return jnp.einsum('nei,eic->nec', g * u, Wd)

        def _moe(x, Wgate, expert_bias, Wg, Wu, Wd, sWg, sWu, sWd):
            b, t, c = x.shape
            xf = x.reshape(-1, c)
            shared = jnp.mean(_experts(xf, sWg, sWu, sWd), axis=1)
            logits = xf @ Wgate + expert_bias
            probs = jax.nn.softmax(logits, axis=-1)
            topk_p, topk_i = jax.lax.top_k(probs, K)
            topk_p = topk_p / jnp.sum(topk_p, axis=-1, keepdims=True)
            comb = jnp.sum(jax.nn.one_hot(topk_i, E, dtype=xf.dtype) * topk_p[..., None], axis=1)
            routed = jnp.einsum('ne,nec->nc', comb, _experts(xf, Wg, Wu, Wd))
            return (shared + routed).reshape(b, t, c)
        key = jax.random.key(seed)
        ks = jax.random.split(key, 16)
        w = lambda k, shp: jax.random.normal(k, shp, dtype=jnp.float32) * 0.02
        return {'x': jax.random.normal(ks[0], (B, T, C), dtype=jnp.float32), 'w_ln1': jnp.ones((C,), jnp.float32), 'Wq': w(ks[1], (C, H * D)), 'Wkva': w(ks[2], (C, R + ROPE)), 'Wkvb': w(ks[3], (R, H * NOPE)), 'Wo': w(ks[4], (H * D, C)), 'w_ln2': jnp.ones((C,), jnp.float32), 'Wgate': w(ks[5], (C, E)), 'expert_bias': jnp.zeros((E,), jnp.float32), 'Wg': w(ks[6], (E, C, I)), 'Wu': w(ks[7], (E, C, I)), 'Wd': w(ks[8], (E, I, C)), 'sWg': w(ks[9], (S, C, I)), 'sWu': w(ks[10], (S, C, I)), 'sWd': w(ks[11], (S, I, C))}
    _L1_ffn_in = _L1_ffn_setup()
    _d = {'L0_attn_x': _L0_attn_in['x'], 'L0_attn_W_Q': _L0_attn_in['W_Q'], 'L0_attn_W_K': _L0_attn_in['W_K'], 'L0_attn_W_V': _L0_attn_in['W_V'], 'L0_attn_W_O': _L0_attn_in['W_O'], 'L0_ffn_Wg': _L0_ffn_in['Wg'], 'L0_ffn_W_in': _L0_ffn_in['W_in'], 'L0_ffn_W_out': _L0_ffn_in['W_out'], 'L1_attn_ln1_g': _L1_attn_in['ln1_g'], 'L1_attn_ln1_b': _L1_attn_in['ln1_b'], 'L1_attn_in_W': _L1_attn_in['in_W'], 'L1_attn_in_b': _L1_attn_in['in_b'], 'L1_attn_dw_W': _L1_attn_in['dw_W'], 'L1_attn_dw_b': _L1_attn_in['dw_b'], 'L1_attn_dt_W': _L1_attn_in['dt_W'], 'L1_attn_dt_b': _L1_attn_in['dt_b'], 'L1_attn_b_W': _L1_attn_in['b_W'], 'L1_attn_b_b': _L1_attn_in['b_b'], 'L1_attn_c_W': _L1_attn_in['c_W'], 'L1_attn_c_b': _L1_attn_in['c_b'], 'L1_attn_a_log': _L1_attn_in['a_log'], 'L1_attn_d_skip': _L1_attn_in['d_skip'], 'L1_attn_out_W': _L1_attn_in['out_W'], 'L1_attn_out_b': _L1_attn_in['out_b'], 'L1_attn_ln2_g': _L1_attn_in['ln2_g'], 'L1_attn_ln2_b': _L1_attn_in['ln2_b'], 'L1_attn_f1_W': _L1_attn_in['f1_W'], 'L1_attn_f1_b': _L1_attn_in['f1_b'], 'L1_attn_f2_W': _L1_attn_in['f2_W'], 'L1_attn_f2_b': _L1_attn_in['f2_b'], 'L1_ffn_w_ln1': _L1_ffn_in['w_ln1'], 'L1_ffn_Wq': _L1_ffn_in['Wq'], 'L1_ffn_Wkva': _L1_ffn_in['Wkva'], 'L1_ffn_Wkvb': _L1_ffn_in['Wkvb'], 'L1_ffn_Wo': _L1_ffn_in['Wo'], 'L1_ffn_w_ln2': _L1_ffn_in['w_ln2'], 'L1_ffn_Wgate': _L1_ffn_in['Wgate'], 'L1_ffn_expert_bias': _L1_ffn_in['expert_bias'], 'L1_ffn_Wg': _L1_ffn_in['Wg'], 'L1_ffn_Wu': _L1_ffn_in['Wu'], 'L1_ffn_Wd': _L1_ffn_in['Wd'], 'L1_ffn_sWg': _L1_ffn_in['sWg'], 'L1_ffn_sWu': _L1_ffn_in['sWu'], 'L1_ffn_sWd': _L1_ffn_in['sWd']}
    _x0 = _d['L0_attn_x']
    _d['L0_attn_x'] = jax.random.normal(jax.random.fold_in(jax.random.key(seed), 1), (2, 1024, 128), dtype=_x0.dtype)
    del _x0
    return _d

def reference(L0_attn_x, L0_attn_W_Q, L0_attn_W_K, L0_attn_W_V, L0_attn_W_O, L0_ffn_Wg, L0_ffn_W_in, L0_ffn_W_out, L1_attn_ln1_g, L1_attn_ln1_b, L1_attn_in_W, L1_attn_in_b, L1_attn_dw_W, L1_attn_dw_b, L1_attn_dt_W, L1_attn_dt_b, L1_attn_b_W, L1_attn_b_b, L1_attn_c_W, L1_attn_c_b, L1_attn_a_log, L1_attn_d_skip, L1_attn_out_W, L1_attn_out_b, L1_attn_ln2_g, L1_attn_ln2_b, L1_attn_f1_W, L1_attn_f1_b, L1_attn_f2_W, L1_attn_f2_b, L1_ffn_w_ln1, L1_ffn_Wq, L1_ffn_Wkva, L1_ffn_Wkvb, L1_ffn_Wo, L1_ffn_w_ln2, L1_ffn_Wgate, L1_ffn_expert_bias, L1_ffn_Wg, L1_ffn_Wu, L1_ffn_Wd, L1_ffn_sWg, L1_ffn_sWu, L1_ffn_sWd):

    def _L0_attn_ref(x, W_Q, W_K, W_V, W_O):
        import jax, jax.numpy as jnp
        import numpy as np
        B, S, D, H = (2, 256, 128, 16)
        HD = D // H
        b, s, d = x.shape
        Q = (x @ W_Q.T).reshape(b, s, H, HD).transpose(0, 2, 1, 3)
        K = (x @ W_K.T).reshape(b, s, H, HD).transpose(0, 2, 1, 3)
        V = (x @ W_V.T).reshape(b, s, H, HD).transpose(0, 2, 1, 3)
        attn = jnp.einsum('bhqd,bhkd->bhqk', Q, K) / jnp.sqrt(jnp.float32(HD))
        slopes = 1.0 / (2.0 ** 8) ** ((jnp.arange(H, dtype=jnp.float32) + 1) / H)
        pos = jnp.arange(s)
        rel = jnp.minimum(pos[None, :] - pos[:, None], 0).astype(jnp.float32)
        bias = slopes[:, None, None] * rel[None, :, :]
        causal = pos[None, :] <= pos[:, None]
        attn = jnp.where(causal[None, None], attn + bias[None], -jnp.inf)
        attn = jax.nn.softmax(attn, axis=-1)
        out = jnp.einsum('bhqk,bhkd->bhqd', attn, V)
        out = out.transpose(0, 2, 1, 3).reshape(b, s, d)
        return out @ W_O.T

    def _L0_ffn_ref(x, Wg, W_in, W_out):
        import math
        import jax, jax.numpy as jnp
        import numpy as np
        B, T, H = (4, 256, 128)
        E, K, F = (8, 2, 256)
        CAP_FACTOR = 1.25

        def _moe_forward(x, Wg, W_in, W_out):
            b, t, h = x.shape
            xf = x.reshape(-1, h)
            S = xf.shape[0]
            C = int(math.ceil(K * S / E * CAP_FACTOR))
            logits = xf @ Wg
            probs = jax.nn.softmax(logits, axis=-1)
            top_vals, top_idx = jax.lax.top_k(probs, K)
            flat_idx = top_idx.T.reshape(-1)
            onehot = jax.nn.one_hot(flat_idx, E, dtype=jnp.int32)
            cum = jnp.cumsum(onehot, axis=0) - 1
            loc = jnp.take_along_axis(cum, flat_idx[:, None], axis=1)[:, 0]
            loc = loc.reshape(K, S).T
            keep = loc < C
            gates = top_vals * keep.astype(top_vals.dtype)
            denom = jnp.maximum(gates.sum(-1, keepdims=True), 1e-09)
            gates = gates / denom
            loc_c = jnp.where(keep, loc, C)
            e_flat = top_idx.reshape(-1)
            l_flat = loc_c.reshape(-1)
            xk = jnp.broadcast_to(xf[:, None, :], (S, K, h)).reshape(-1, h)
            xk = jnp.where(keep.reshape(-1, 1), xk, 0.0)
            buf = jnp.zeros((E, C + 1, h), x.dtype).at[e_flat, l_flat].set(xk)
            inp = buf[:, :C]
            hid = jnp.einsum('ech,ehf->ecf', inp, W_in)
            a, g = jnp.split(hid, 2, axis=-1)
            hid = jax.nn.gelu(a, approximate=False) * g
            out_e = jnp.einsum('ecf,efh->ech', hid, W_out)
            out_pad = jnp.concatenate([out_e, jnp.zeros((E, 1, h), out_e.dtype)], axis=1)
            gathered = out_pad[e_flat, l_flat].reshape(S, K, h)
            y = (gathered * gates[..., None]).sum(axis=1)
            return y.reshape(b, t, h)
        return _moe_forward(x, Wg, W_in, W_out)

    def _L1_attn_ref(x, ln1_g, ln1_b, in_W, in_b, dw_W, dw_b, dt_W, dt_b, b_W, b_b, c_W, c_b, a_log, d_skip, out_W, out_b, ln2_g, ln2_b, f1_W, f1_b, f2_W, f2_b):
        import jax, jax.numpy as jnp
        import numpy as np
        from jax import lax
        B, L, D, K = (4, 512, 128, 3)
        H = 256

        def _layernorm(h, g, b):
            m = jnp.mean(h, axis=-1, keepdims=True)
            v = jnp.mean((h - m) ** 2, axis=-1, keepdims=True)
            return (h - m) / jnp.sqrt(v + 1e-05) * g + b
        nx = _layernorm(x, ln1_g, ln1_b)
        proj = nx @ in_W + in_b
        x_proj, gate = jnp.split(proj, 2, axis=-1)
        xt = jnp.transpose(x_proj, (0, 2, 1))
        mixed = lax.conv_general_dilated(xt, dw_W, window_strides=(1,), padding=[(K // 2, K // 2)], dimension_numbers=('NCH', 'OIH', 'NCH'), feature_group_count=D)
        mixed = jnp.transpose(mixed + dw_b[None, :, None], (0, 2, 1))
        dt = jax.nn.softplus(mixed @ dt_W + dt_b)
        bt = jnp.tanh(mixed @ b_W + b_b)
        ct = jnp.tanh(mixed @ c_W + c_b)
        a = -jnp.exp(a_log)

        def step(state, inp):
            dt_t, b_t, c_t, m_t, g_t = inp
            decay = jnp.exp(dt_t * a)
            state = decay * state + dt_t * b_t * m_t
            y_t = c_t * state + d_skip * m_t
            return (state, y_t * jax.nn.sigmoid(g_t))
        seqs = tuple((jnp.transpose(t, (1, 0, 2)) for t in (dt, bt, ct, mixed, gate)))
        state0 = jnp.zeros((x.shape[0], x.shape[2]), x.dtype)
        _, ys = lax.scan(step, state0, seqs)
        y = jnp.transpose(ys, (1, 0, 2))
        x2 = x + y @ out_W + out_b
        h = _layernorm(x2, ln2_g, ln2_b)
        ffn = jax.nn.gelu(h @ f1_W + f1_b, approximate=False) @ f2_W + f2_b
        return x2 + ffn

    def _L1_ffn_ref(x, w_ln1, Wq, Wkva, Wkvb, Wo, w_ln2, Wgate, expert_bias, Wg, Wu, Wd, sWg, sWu, sWd):
        import jax, jax.numpy as jnp
        import numpy as np
        B, T, C = (2, 256, 128)
        H, D = (16, 64)
        CR = 8
        R = C // CR
        ROPE = D // 2
        NOPE = D - ROPE
        E, K, I, S = (8, 2, 64, 1)
        THETA = 100000.0
        EPS = 1e-05

        def _rmsnorm(x, w):
            rms = jnp.sqrt(jnp.mean(x * x, axis=-1, keepdims=True) + EPS)
            return w * (x / rms)

        def _rope(xh):
            d = xh.shape[-1]
            t = jnp.arange(xh.shape[2], dtype=jnp.float32)
            freqs = 1.0 / THETA ** (jnp.arange(0, d, 2, dtype=jnp.float32) / d)
            ang = jnp.outer(t, freqs)
            cos, sin = (jnp.cos(ang), jnp.sin(ang))
            xr = xh.reshape(xh.shape[:-1] + (d // 2, 2))
            x0, x1 = (xr[..., 0], xr[..., 1])
            rot = jnp.stack([x0 * cos - x1 * sin, x0 * sin + x1 * cos], axis=-1)
            return rot.reshape(xh.shape)

        def _attention(x, Wq, Wkva, Wkvb, Wo):
            b, t, _ = x.shape
            q = (x @ Wq).reshape(b, t, H, D).transpose(0, 2, 1, 3)
            ckv = x @ Wkva
            kv_latent, k_rope = (ckv[:, :, :R], ckv[:, :, R:])
            kv = (kv_latent @ Wkvb).reshape(b, t, H, NOPE).transpose(0, 2, 1, 3)
            k_rope = jnp.broadcast_to(k_rope[:, None, :, :], (b, H, t, ROPE))
            q_nope, q_rope = (q[..., :NOPE], q[..., NOPE:])
            q = jnp.concatenate([q_nope, _rope(q_rope)], axis=-1)
            k = jnp.concatenate([kv, _rope(k_rope)], axis=-1)
            v = jnp.concatenate([kv, jnp.zeros_like(k_rope)], axis=-1)
            att = jnp.einsum('bhqd,bhkd->bhqk', q, k) / jnp.sqrt(jnp.float32(D))
            mask = jnp.tril(jnp.ones((t, t), dtype=bool))
            att = jnp.where(mask, att, jnp.float32(-jnp.inf))
            att = jax.nn.softmax(att, axis=-1)
            y = jnp.einsum('bhqk,bhkd->bhqd', att, v)
            y = y.transpose(0, 2, 1, 3).reshape(b, t, H * D)
            return y @ Wo

        def _experts(x_flat, Wg, Wu, Wd):
            g = jax.nn.silu(jnp.einsum('nc,eci->nei', x_flat, Wg))
            u = jnp.einsum('nc,eci->nei', x_flat, Wu)
            return jnp.einsum('nei,eic->nec', g * u, Wd)

        def _moe(x, Wgate, expert_bias, Wg, Wu, Wd, sWg, sWu, sWd):
            b, t, c = x.shape
            xf = x.reshape(-1, c)
            shared = jnp.mean(_experts(xf, sWg, sWu, sWd), axis=1)
            logits = xf @ Wgate + expert_bias
            probs = jax.nn.softmax(logits, axis=-1)
            topk_p, topk_i = jax.lax.top_k(probs, K)
            topk_p = topk_p / jnp.sum(topk_p, axis=-1, keepdims=True)
            comb = jnp.sum(jax.nn.one_hot(topk_i, E, dtype=xf.dtype) * topk_p[..., None], axis=1)
            routed = jnp.einsum('ne,nec->nc', comb, _experts(xf, Wg, Wu, Wd))
            return (shared + routed).reshape(b, t, c)
        x = x + _attention(_rmsnorm(x, w_ln1), Wq, Wkva, Wkvb, Wo)
        residual = x
        xn = _rmsnorm(x, w_ln2)
        x_out = _moe(xn, Wgate, expert_bias, Wg, Wu, Wd, sWg, sWu, sWd)
        return residual + x_out
    x = L0_attn_x
    x = x + 0.5 * _L0_ffn_ref(_layernorm(x, axis=-1), L0_ffn_Wg, L0_ffn_W_in, L0_ffn_W_out)
    x = x + _L0_attn_ref(_layernorm(x, axis=-1), L0_attn_W_Q, L0_attn_W_K, L0_attn_W_V, L0_attn_W_O)
    x = x + 0.5 * _L0_ffn_ref(_layernorm(x, axis=-1), L0_ffn_Wg, L0_ffn_W_in, L0_ffn_W_out)
    x = x + 0.5 * _L1_ffn_ref(_layernorm(x, axis=-1), L1_ffn_w_ln1, L1_ffn_Wq, L1_ffn_Wkva, L1_ffn_Wkvb, L1_ffn_Wo, L1_ffn_w_ln2, L1_ffn_Wgate, L1_ffn_expert_bias, L1_ffn_Wg, L1_ffn_Wu, L1_ffn_Wd, L1_ffn_sWg, L1_ffn_sWu, L1_ffn_sWd)
    x = x + _L1_attn_ref(_layernorm(x, axis=-1), L1_attn_ln1_g, L1_attn_ln1_b, L1_attn_in_W, L1_attn_in_b, L1_attn_dw_W, L1_attn_dw_b, L1_attn_dt_W, L1_attn_dt_b, L1_attn_b_W, L1_attn_b_b, L1_attn_c_W, L1_attn_c_b, L1_attn_a_log, L1_attn_d_skip, L1_attn_out_W, L1_attn_out_b, L1_attn_ln2_g, L1_attn_ln2_b, L1_attn_f1_W, L1_attn_f1_b, L1_attn_f2_W, L1_attn_f2_b)
    x = x + 0.5 * _L1_ffn_ref(_layernorm(x, axis=-1), L1_ffn_w_ln1, L1_ffn_Wq, L1_ffn_Wkva, L1_ffn_Wkvb, L1_ffn_Wo, L1_ffn_w_ln2, L1_ffn_Wgate, L1_ffn_expert_bias, L1_ffn_Wg, L1_ffn_Wu, L1_ffn_Wd, L1_ffn_sWg, L1_ffn_sWu, L1_ffn_sWd)
    return x

_drawn_inputs = setup_inputs


def setup_inputs(seed=0):
    import zlib

    import numpy as np

    out = dict(_drawn_inputs(seed))
    spreads = {'L1_attn_ln1_g': (1.0, 0.6),
     'L1_attn_ln1_b': (0.0, 0.8),
     'L1_attn_in_b': (0.0, 0.8),
     'L1_attn_dw_b': (0.0, 0.8),
     'L1_attn_dt_b': (0.0, 0.8),
     'L1_attn_b_b': (0.0, 0.8),
     'L1_attn_c_b': (0.0, 0.8),
     'L1_attn_a_log': (0.0, 0.8),
     'L1_attn_d_skip': (1.0, 0.6),
     'L1_attn_out_b': (0.0, 0.1),
     'L1_attn_ln2_g': (1.0, 0.6),
     'L1_attn_ln2_b': (0.0, 0.8),
     'L1_attn_f1_b': (0.0, 0.8),
     'L1_attn_f2_b': (0.0, 0.277),
     'L1_ffn_w_ln1': (1.0, 0.6),
     'L1_ffn_w_ln2': (1.0, 0.6),
     'L1_ffn_expert_bias': (0.0, 0.8)}
    factors = {'L1_attn_in_W': 8.0,
     'L1_attn_dw_W': 8.0,
     'L1_attn_dt_W': 8.0,
     'L1_attn_b_W': 8.0,
     'L1_attn_c_W': 8.0,
     'L1_attn_out_W': 8.0,
     'L1_attn_f1_W': 3.769,
     'L1_attn_f2_W': 3.308,
     'L1_ffn_Wq': 8.0,
     'L1_ffn_Wkva': 8.0,
     'L1_ffn_Wkvb': 8.0,
     'L1_ffn_Wo': 8.0,
     'L1_ffn_Wgate': 8.0,
     'L1_ffn_Wg': 8.0,
     'L1_ffn_Wu': 8.0,
     'L1_ffn_Wd': 8.0,
     'L1_ffn_sWg': 8.0,
     'L1_ffn_sWu': 8.0,
     'L1_ffn_sWd': 8.0}
    for name, (base, spread) in spreads.items():
        noise = np.random.default_rng([zlib.crc32(name.encode()), seed]).standard_normal(out[name].shape)
        drawn = base * np.exp(spread * noise) if base else spread * noise
        out[name] = jnp.asarray(drawn.astype(out[name].dtype))
    for name, factor in factors.items():
        out[name] = (out[name] * factor).astype(out[name].dtype)
    return out
```

```python
from contextlib import ExitStack

import numpy as np

import concourse.bass as bass
from concourse import mybir

F32 = mybir.dt.float32
F16 = mybir.dt.float16
BF16 = mybir.dt.bfloat16
ALU = mybir.AluOpType
ACT = mybir.ActivationFunctionType
AX = mybir.AxisListType

P = 128
B, S, D = 2, 1024, 128
T = B * S
TT = 512
NT = T // TT
NTT = T // P
H = 16
QUAD = 4
NQ = H // QUAD
NN = B * NQ
KT = S // P
HD0 = D // H
E = 8
F0 = 256
CAP = -(-2 * T * 5 // (E * 4))
ROPE, NOPE, LAT = 32, 32, 16
I1 = 64
EPS = 1e-5
BIG = 1e30
CROW = 96
STEPS = KT * QUAD
SLOPE_PIECES = 3

UNITS = []
for _qt in range(KT):
    _n = (_qt + 1) * P
    for _c0 in range(0, _n, TT):
        _w = min(TT, _n - _c0)
        _per = max(1, min(QUAD, TT // _w))
        _per = {3: 2}.get(_per, _per)
        for _j in range(0, QUAD, _per):
            UNITS.append((_qt, _c0, _w, tuple(range(_j, _j + _per))))


def ring_plan(tail, ahead, build):
    plan = []
    if tail:
        plan += [(1, "den", 0)] + [(3, "spread", h) for h in range(2)] + [(6, "proj", h) for h in range(2)]
    if build:
        plan += [(4 + 3 * i, kind, h) for i, (h, kind) in
                 enumerate((h, k) for h in range(2) for k in ("rope", "swap"))]
        plan += [(6 + 6 * h, "lat", h) for h in range(2)]
    if ahead:
        first, last = 5, 26
        plan += [(first + i * (last - first) // len(UNITS), "unit", u) for i, u in enumerate(UNITS)]
        plan.append((28, "turn", 0))
    return [p for _, p in sorted(enumerate(plan), key=lambda e: (e[1][0], e[0]))]


def build_program(nc, a, out):
    with ExitStack() as ctx:
        def sb(name, shape, dt=F32):
            return ctx.enter_context(nc.sbuf_tensor(name, shape, dt))

        def sem(name):
            return ctx.enter_context(nc.semaphore(name))

        XT = sb("XT", [P, T])
        XN = sb("XN", [P, T])
        YA = sb("YA", [P, T])
        QS = sb("QS", [P, H, S], F16)
        KS = sb("KS", [P, H, S], F16)
        PR = sb("PR", [P, 2, QUAD, S])
        VS = sb("VS", [P, KT, QUAD, 32])
        OS = sb("OS", [P, S])
        ON = sb("ON", [P, S])
        RD = sb("RD", [P, KT * QUAD])
        RX = sb("RX", [P, S])
        HL = sb("HL", [P, 4, T], F16)
        WM = sb("WM", [P, 6144])
        QSf = QS[:, :, :].rearrange("p h s -> p (h s)").bitcast(F32)
        KSf = KS[:, :, :].rearrange("p h s -> p (h s)").bitcast(F32)
        PRf = PR[:, :, :, :].rearrange("p a j s -> p (a j s)")

        w_in = WM[:, 0:4096].rearrange("p (e f) -> p e f", e=E)
        w_out = WM[:, 4096:6144].rearrange("p (e c o) -> p e c o", e=E, c=2)
        at = [0]

        def wm(n):
            at[0] += n
            assert at[0] <= 6144
            return WM[:, at[0] - n:at[0]]

        cosT, sinT = wm(S), wm(S)
        w_rope = wm(512).rearrange("p (g m) -> p g m", g=NQ)
        w_swap = wm(512).rearrange("p (g m) -> p g m", g=NQ)
        w_lat = wm(512).rearrange("p (g m) -> p g m", g=NQ)
        w_kva = wm(96)
        w_gate1 = wm(9 * I1)
        w_up1 = wm(9 * I1)
        w_down1 = wm(5 * P).rearrange("p (g o) -> p g o", g=5)
        w_rt1 = wm(E)
        wo0 = sb("wo0", [P, NQ, P])
        wo1 = sb("wo1", [P, NQ, P])
        wq0 = sb("wq0", [P, 3, P])
        w_rt0 = sb("w_rt0", [P, E])
        brow = sb("brow", [1, E])
        ones1 = sb("ones1", [1, P])
        colp = sb("colp", [P, 20])
        stage = sb("stage", [P, 4, P])
        wnt = HL[0:32, 0:4, :].rearrange("p a t -> p (a t)").bitcast(F32)
        wqn = wnt[:, 0:2048].rearrange("p (h m) -> p h m", h=H)
        won = QSf[0:32, 0:2048].rearrange("p (h m) -> p h m", h=H)
        wkb = wnt[:, 2048:2560].rearrange("p (h m) -> p h m", h=H)

        mean_w = sb("mean_w", [P, P])
        identf = sb("identf", [P, P])
        identb = sb("identb", [P, P], BF16)
        maskqk = sb("maskqk", [P, P], BF16)
        maskkq = sb("maskkq", [P, P], BF16)
        lower = sb("lower", [P, P], BF16)
        onesb = sb("onesb", [P, P], BF16)
        sel0 = sb("sel0", [P, P])
        sel1 = sb("sel1", [P, P])
        desc = sb("desc", [P, E])
        epsc = sb("epsc", [P, 4])
        BM = sb("BM", [P, 2, QUAD, KT])
        M4 = sb("M4", [P, QUAD * KT])
        CT = sb("CT", [QUAD * KT, P], F16)
        rt = PRf[:, 5120:7680].rearrange("p (n c) -> p n c", n=10)
        ohb = sb("ohb", [P, 256], BF16)
        gT = sb("gT", [P, P])

        def pr_part(o, n):
            return PRf[:, o:o + n]

        NSQ = pr_part(0, 1024).rearrange("p (a t) -> p a t", a=2)
        NLN = pr_part(1024, 2048).rearrange("p (a b t) -> p a b t", a=2, b=2)
        NRS = pr_part(3072, 2048).rearrange("p (a b t) -> p a b t", a=2, b=2)
        GB = KSf[:, 0:8192].rearrange("p (a e t) -> p a e t", a=2, e=E)
        XS = QSf[:, 0:1024].rearrange("p (a t) -> p a t", a=2)
        GE = QSf[:, 1024:2048].rearrange("p (a t) -> p a t", a=2)
        HID = QSf[:, 2048:3584].rearrange("p (a t) -> p a t", a=3)
        HGL = QSf[:, 3584:5120].rearrange("p (a t) -> p a t", a=3)
        V0 = YA[:, :].rearrange("p (i c) -> p i c", i=NTT)
        VL = sb("VL", [P, NTT, LAT])
        BT = sb("BT", [P, 4, TT])
        XP = QSf[:, 0:2 * (S + 2)].rearrange("p (b s) -> p b s", b=B)
        MX = QSf[:, 2560:2560 + T]
        SG = QSf[:, 5120:5120 + T]
        DTm = KSf[:, 0:T]
        BTm = KSf[:, T:2 * T]
        CTm = KSf[:, 2 * T:3 * T]
        DEC = KSf[:, 3 * T:4 * T]
        ST_ = pr_part(5120, T)
        TMP = BT[:, :, :]
        F1 = OS[:, :].rearrange("p (a t) -> p a t", a=2)
        w_inp = sb("w_inp", [P, 2, P])
        w_dbc = sb("w_dbc", [P, 3, P])
        w_outp = sb("w_outp", [P, P])
        w_f1 = sb("w_f1", [P, 2, P])
        w_f2 = sb("w_f2", [P, 2, P])

        ps = [ctx.enter_context(nc.psum_tensor(f"ps{i}", [P, 2, TT], F32)) for i in range(4)]

        def bank(i):
            return ps[i // 2][:, i % 2, :]

        RING = (4, 5)
        OUTP = ps[3]

        gate_d = [nc.dram_tensor(f"gates{k}", (E, T), F32, kind="Internal").ap() for k in range(4)]

        s_x0 = sem("s_x0")
        s_w = sem("s_w")
        s_wm = sem("s_wm")
        s_wl = sem("s_wl")
        s_const = sem("s_const")
        s_ld = sem("s_ld")
        s_comp = sem("s_comp")
        s_compd = sem("s_compd")
        s_xup = sem("s_xup")
        s_mean, s_xc, s_sq, s_var = sem("s_mean"), sem("s_xc"), sem("s_sq"), sem("s_var")
        s_rs, s_xn, s_lg, s_va = sem("s_rs"), sem("s_xn"), sem("s_lg"), sem("s_va")
        s_rpe, s_rdv, s_rac = sem("s_rpe"), sem("s_rdv"), sem("s_rac")
        s_gw, s_gb, s_xs = sem("s_gw"), sem("s_gb"), sem("s_xs")
        s_ag, s_ge, s_hid, s_out = sem("s_ag"), sem("s_ge"), sem("s_hid"), sem("s_out")
        s_hg = sem("s_hg")
        s_zero = sem("s_zero")
        s_cdma = sem("s_cdma")
        s_stk = sem("s_stk")
        s_crow = sem("s_crow")
        s_st = sem("s_st")
        s_exp = sem("s_exp")
        s_pv = sem("s_pv")
        s_rr = sem("s_rr")
        s_rd = sem("s_rd")
        s_m4 = sem("s_m4")
        s_vs = sem("s_vs")
        s_wst = sem("s_wst")
        s_den = sem("s_den")
        s_wos = sem("s_wos")
        s_os = sem("s_os")
        s_kb = sem("s_kb")
        s_hl = sem("s_hl")
        s_lat = sem("s_lat")
        s_sp, s_sa, s_sd, s_so = sem("s_sp"), sem("s_sa"), sem("s_sd"), sem("s_so")
        s_fin, s_store = sem("s_fin"), sem("s_store")
        s_dve = sem("s_dve")
        s_act = sem("s_act")
        s_pool = sem("s_pool")

        class Chain:

            def __init__(self, eng, s):
                self.eng, self.s, self.n = eng, s, 0

            def up(self, ins):
                ins.then_inc(self.s, 1)
                self.n = self.n + 1

            def wait(self):
                self.eng.wait_ge(self.s, self.n)

            def link(self, ins):
                self.up(ins)
                self.wait()

        (C_L1G, C_L1B, C_INB0, C_INB1, C_DW0, C_DW1, C_DW2, C_DWB, C_DTB, C_BB, C_CB, C_A, C_DSK,
         C_OB, C_L2G, C_L2B, C_F1B0, C_F1B1, C_F2B, C_NA) = range(20)
        colw = sb("colw_sb", [P, 4])

        def tsl(t, n=TT):
            return bass.ds(t * n, n)

        def sp_load(sp):
            sp.dma_start(PRf[:, 0:T].rearrange("p (i d) -> p i d", i=NTT),
                         a["x"].rearrange("(i p) d -> p i d", p=P)).then_inc(s_x0, 16)
            loads = [
                (w_rt0[:, :], a["Wg0"]), (wq0[:, :, :], a["Wqkv0"].rearrange("n p m -> p n m")),
                (wo0[:, :, :], a["WoPad0"].rearrange("g p m -> p g m")),
                (brow[:, :], a["expert_bias"]), (colp[:, 0:19], a["cols"]), (colw[:, 0:2], a["colw"]),
                (w_inp[:, :, :], a["in_W"].rearrange("p (c m) -> p c m", c=2)),
                (w_dbc[:, 0, :], a["dt_W"]), (w_dbc[:, 1, :], a["b_W"]), (w_dbc[:, 2, :], a["c_W"]),
                (w_outp[:, :], a["out_W"]),
                (w_f1[:, :, :], a["f1_W"].rearrange("p (c m) -> p c m", c=2)),
                (w_f2[:, :, :], a["f2_W"].rearrange("(c p) m -> p c m", p=P)),
            ]
            for dst, src in loads:
                sp.dma_start(dst, src).then_inc(s_w, 16)
            load_moe_weights(sp)

        N_WFIRST = 16 * 13

        def load_moe_weights(sp):
            sp.dma_start(w_in, a["W_in"].rearrange("e p f -> p e f")).then_inc(s_wm, 16)
            sp.dma_start(w_out, a["W_out"].rearrange("e (c p) o -> p e c o", p=P)).then_inc(s_wm, 16)

        N_CONST = 12

        def pool_const(pool):
            ch = Chain(pool, s_pool)
            for m in (identf, sel0, sel1):
                ch.up(pool.memset(m[:, :], 0.0))
            for m in (identb, maskqk, maskkq):
                ch.up(pool.memset(m[:, :], 0.0))
            ch.up(pool.memset(lower[:, :], 1.0))
            ch.wait()
            for m in (identf, identb):
                pool.affine_select(out=m[:, :], in_=m[:, :], compare_op=ALU.not_equal, fill=1.0, base=0,
                                   pattern=[[-1, P]], channel_multiplier=1).then_inc(s_const, 1)
            pool.affine_select(out=maskqk[:, :], in_=maskqk[:, :], compare_op=ALU.is_ge, fill=-BIG, base=0,
                               pattern=[[-1, P]], channel_multiplier=1).then_inc(s_const, 1)
            pool.affine_select(out=maskkq[:, :], in_=maskkq[:, :], compare_op=ALU.is_ge, fill=-BIG, base=0,
                               pattern=[[1, P]], channel_multiplier=-1).then_inc(s_const, 1)
            pool.affine_select(out=lower[:, :], in_=lower[:, :], compare_op=ALU.is_gt, fill=0.0, base=0,
                               pattern=[[1, P]], channel_multiplier=-1).then_inc(s_const, 1)
            for m, r in ((sel0, HD0), (sel1, LAT)):
                pool.affine_select(out=m[:, :].rearrange("p (j c) -> p j c", j=QUAD),
                                   in_=m[:, :].rearrange("p (j c) -> p j c", j=QUAD),
                                   compare_op=ALU.not_equal, fill=1.0, base=-r,
                                   pattern=[[-32, QUAD], [0, 32]], channel_multiplier=1).then_inc(s_const, 1)
            pool.memset(onesb[:, :], 1.0).then_inc(s_const, 1)
            pool.memset(mean_w[:, :], 1.0 / D).then_inc(s_const, 1)
            pool.memset(ones1[:, :], 1.0).then_inc(s_const, 1)
            pool.memset(BM[:, :, :, :], -3e38).then_inc(s_const, 1)
            for e in range(E):
                ins = pool.memset(desc[:, e:e + 1], float(E - e))
            pool.memset(epsc[:, 0:1], EPS)
            ins = pool.memset(epsc[:, 1:2], EPS * EPS)
            ins.then_inc(s_const, 1)

        def pe_load(pe):
            pe.wait_ge(s_const, N_CONST)
            pe.wait_ge(s_x0, 16)
            for i in range(NTT):
                ins = pe.transpose(bank(i // 4)[:, (i % 4) * P:(i % 4 + 1) * P],
                                   PRf[:, i * P:(i + 1) * P], identf[:, :])
                if i % 4 == 3:
                    ins.then_inc(s_ld, 1)

        def dve_load(dve):
            for t in range(NT):
                dve.wait_ge(s_ld, t + 1)
                dve.tensor_copy(XT[:, t * TT:(t + 1) * TT], bank(t)).then_inc(s_xup, 1)

        def norm_src(mode):
            return YA if mode in ("rms", "ln2") else XT

        def pe_norm(pe, k, mode, ready):
            src = norm_src(mode)
            pe.wait_ge(*ready)

            def mean(t):
                pe.matmul(bank(t % 2), mean_w[:, :], src[:, tsl(t)], start=True, stop=True).then_inc(s_mean, 1)

            def var(t):
                pe.wait_ge(s_sq, 4 * k + t + 1)
                if t >= 2:
                    pe.wait_ge(s_va, 4 * k + t - 1)
                pe.matmul(bank(2 + t % 2), mean_w[:, :], NSQ[:, t % 2, :], start=True, stop=True).then_inc(s_var, 1)

            mean(0)
            mean(1)
            for t in range(NT):
                var(t)
                if t + 2 < NT:
                    mean(t + 2)

        def dve_norm(dve, k, mode, w=None, b=None, ch=None, prev=None):
            src = norm_src(mode)

            def center(t):
                dve.wait_ge(s_mean, 4 * k + t + 1)
                if mode == "rms":
                    dve.tensor_copy(XN[:, tsl(t)], src[:, tsl(t)]).then_inc(s_xc, 1)
                else:
                    dve.tensor_tensor(XN[:, tsl(t)], src[:, tsl(t)], bank(t % 2), ALU.subtract).then_inc(s_xc, 1)

            def scale(t):
                dve.wait_ge(s_rs, 4 * k + t + 1)
                r1, r2 = NRS[:, t % 2, 0, :], NRS[:, t % 2, 1, :]
                if mode == "fused":
                    dve.tensor_tensor(YA[:, tsl(t)], XN[:, tsl(t)], r1, ALU.mult)
                r = r2 if mode == "fused" else r1
                if w is None:
                    dve.tensor_tensor(XN[:, tsl(t)], XN[:, tsl(t)], r, ALU.mult).then_inc(s_xn, 1)
                elif b is None:
                    dve.scalar_tensor_tensor(out=XN[:, tsl(t)], in0=XN[:, tsl(t)], scalar=w, in1=r,
                                             op0=ALU.mult, op1=ALU.mult).then_inc(s_xn, 1)
                else:
                    ch.link(dve.scalar_tensor_tensor(out=XN[:, tsl(t)], in0=XN[:, tsl(t)], scalar=w, in1=r,
                                                     op0=ALU.mult, op1=ALU.mult))
                    dve.tensor_scalar(XN[:, tsl(t)], XN[:, tsl(t)], b, None, ALU.add).then_inc(s_xn, 1)

            center(0)
            center(1)
            for t in range(NT):
                scale(t)
                if t + 2 < NT:
                    center(t + 2)

        def act_norm(act, k, mode, ch):
            n = 2 if mode == "fused" else 1

            def square(t):
                act.wait_ge(s_xc, 4 * k + t + 1)
                if t >= 2:
                    act.wait_ge(s_var, 4 * k + t - 1)
                act.activation(NSQ[:, t % 2, :], XN[:, tsl(t)], ACT.Square).then_inc(s_sq, 1)

            def rstd(t):
                act.wait_ge(s_var, 4 * k + t + 1)
                if t >= 2:
                    act.wait_ge(s_xn, 4 * k + t - 1)
                v = bank(2 + t % 2)
                ins = act.activation(NLN[:, t % 2, 0, :], v, ACT.Ln, bias=epsc[:, 0:1])
                if n == 2:
                    ch.up(ins)
                    ins = act.activation(NLN[:, t % 2, 1, :], v, ACT.Ln, bias=epsc[:, 1:2], scale=1.0 + EPS)
                ins.then_inc(s_va, 1)
                act.wait_ge(s_va, 4 * k + t + 1)
                if n == 2:
                    ch.wait()
                act.activation(NRS[:, t % 2, 0:n, :], NLN[:, t % 2, 0:n, :], ACT.Exp, scale=-0.5).then_inc(s_rs, 1)

            square(0)
            for t in range(NT):
                if t + 1 < NT:
                    square(t + 1)
                rstd(t)

        def pe_router(pe, r, kn, w, bias, cap):
            pe.wait_ge(s_xn, 4 * (kn + 1))
            for i in range(NTT):
                o = bank(0)[:, i * E:(i + 1) * E]
                ins = pe.matmul(o, XN[:, i * P:(i + 1) * P], w, start=True, stop=not bias)
                if bias:
                    ins = pe.matmul(o, ones1[0:1, :], brow[0:1, :], start=False, stop=True)
            ins.then_inc(s_rpe, 1)
            if cap:
                pe.wait_ge(s_rdv, 3 * r + 2)
                pe.matmul(bank(1)[:, 0:256], lower[:, :], ohb[:, :], start=True, stop=True)
                pe.matmul(bank(2)[:, 0:256], onesb[:, :], ohb[:, :], start=True, stop=True).then_inc(s_rpe, 1)
            pe.wait_ge(s_rdv, 3 * r + 3)
            ins = pe.transpose(bank(3)[:, 0:P], rt[:, 0, 0:P], identf[:, :])
            ins.then_inc(s_rpe, 1 if cap else 2)

        def act_router(act, r):
            act.wait_ge(s_rdv, 3 * r + 1)
            act.activation(rt[:, 1, 0:P], rt[:, 0, 0:P], ACT.Exp).then_inc(s_rac, 1)

        def dve_router(dve, r, cap, ch):
            def v3(i, o=0):
                return rt[:, i, o:o + P].rearrange("p (i e) -> p i e", e=E)

            def over_e(x):
                return x.unsqueeze(2).to_broadcast([P, NTT, E])

            m = [rt[:, 9, 16 * q:16 * q + 16] for q in range(8)]
            dve.wait_ge(s_rpe, 3 * r + 1)
            lg = bank(0)[:, 0:P].rearrange("p (i e) -> p i e", e=E)
            ch.link(dve.tensor_reduce(m[0], lg, AX.X, ALU.max))
            dve.tensor_tensor(v3(0), lg, over_e(m[0]), ALU.subtract).then_inc(s_rdv, 1)
            dve.wait_ge(s_rac, r + 1)
            ch.link(dve.tensor_reduce(m[1], v3(1), AX.X, ALU.add))
            ch.link(dve.reciprocal(m[2], m[1]))
            ch.link(dve.tensor_tensor(v3(2), v3(1), over_e(m[2]), ALU.mult))

            def best(p, w, oh):
                ch.link(dve.tensor_reduce(m[3], p, AX.X, ALU.max))
                ch.link(dve.tensor_tensor(w, p, over_e(m[3]), ALU.is_equal))
                ch.link(dve.tensor_tensor(w, w, desc[:, :].unsqueeze(1).to_broadcast([P, NTT, E]), ALU.mult))
                ch.link(dve.tensor_reduce(m[4], w, AX.X, ALU.max))
                ch.link(dve.tensor_tensor(oh, w, over_e(m[4]), ALU.is_equal))

            best(v3(2), v3(3), v3(4, 0))
            ch.link(dve.scalar_tensor_tensor(out=v3(5), in0=v3(4, 0), scalar=-2.0, in1=v3(2),
                                             op0=ALU.mult, op1=ALU.add))
            best(v3(5), v3(3), v3(4, P))
            oh = rt[:, 4, :]
            if cap:
                dve.tensor_copy(ohb[:, :], oh).then_inc(s_rdv, 1)
                dve.wait_ge(s_rpe, 3 * r + 2)
                ch.link(dve.tensor_copy(rt[:, 5, :], bank(2)[:, 0:256]))
                src = 5
                for step, dst in ((8, 6), (16, 7), (32, 6), (64, 7), (128, 6)):
                    ch.up(dve.tensor_copy(rt[:, dst, 0:step], rt[:, src, 0:step]))
                    ch.link(dve.tensor_tensor(rt[:, dst, step:256], rt[:, src, step:256],
                                              rt[:, src, 0:256 - step], ALU.add))
                    src = dst
                ch.link(dve.tensor_tensor(rt[:, 7, :], rt[:, 6, :], rt[:, 5, :], ALU.subtract))
                ch.link(dve.tensor_tensor(rt[:, 7, :], rt[:, 7, :], bank(1)[:, 0:256], ALU.add))
                ch.link(dve.scalar_tensor_tensor(out=rt[:, 8, :], in0=rt[:, 7, :], scalar=float(CAP), in1=oh,
                                                 op0=ALU.is_lt, op1=ALU.mult))
                kept = rt[:, 8, :]
            else:
                ch.up(dve.tensor_copy(rt[:, 8, 0:8], oh[:, 0:8]))
                dve.tensor_copy(ohb[:, 0:8], oh[:, 0:8]).then_inc(s_rdv, 1)
                kept = oh
            ch.wait()
            ch.link(dve.tensor_tensor(rt[:, 5, 0:P], kept[:, 0:P], kept[:, P:256], ALU.add))
            ch.link(dve.tensor_tensor(v3(5), v3(5), v3(2), ALU.mult))
            ch.link(dve.tensor_reduce(m[5], v3(5), AX.X, ALU.add))
            if cap:
                ch.link(dve.tensor_scalar(m[5], m[5], 1e-9, None, ALU.max))
            ch.link(dve.reciprocal(m[6], m[5]))
            dve.tensor_tensor(rt[:, 0, 0:P].rearrange("p (e i) -> p i e", e=E), v3(5), over_e(m[6]),
                              ALU.mult).then_inc(s_rdv, 1)
            dve.wait_ge(s_rpe, 3 * r + 3)
            dve.tensor_copy(gT[:, :], bank(3)[:, 0:P]).then_inc(s_hg, 1)

        def sp_gates(sp, r, halves):
            sp.wait_ge(s_hg, r + 1)
            sp.dma_start(gate_d[r].rearrange("e (i t) -> (e i) t", t=P), gT[:, :]).then_inc(s_gw, 16)
            sp.wait_ge(s_gw, 16 * (r + 1))
            for t in range(NT):
                if t >= 2:
                    sp.wait_ge(s_xs, 4 * r + t - 1)
                if halves:
                    for h in range(2):
                        src = gate_d[r].rearrange("(g h) t -> h g t", h=2)[h:h + 1, :, t * TT:(t + 1) * TT]
                        sp.dma_start(GB[64 * h:64 * h + 64, t % 2, 0:4, :],
                                     src.to_broadcast([64, 4, TT])).then_inc(s_gb, 16)
                else:
                    src = gate_d[r].unsqueeze(0)[:, :, t * TT:(t + 1) * TT]
                    sp.dma_start(GB[:, t % 2, :, :], src.to_broadcast([P, E, TT])).then_inc(s_gb, 32)
                sp.wait_ge(s_gb, 32 * (4 * r + t + 1))

        ST0 = 2 * E
        ST1 = 5

        def ag_base(r):
            return (0, NT * ST0, 2 * NT * ST0, 2 * NT * ST0 + NT * ST1)[r]

        def pairbank(u, g):
            return bank(2 + 2 * (u % 3) + g)

        XSB = (0, NT * E, 2 * NT * E, 2 * NT * E)

        s_xg = sem("s_xg")

        def pool_moe0(pool, r):
            for t in range(NT):
                pool.wait_ge(s_gb, 32 * (4 * r + t + 1))
                for e in range(E):
                    n = t * E + e
                    if n >= 2:
                        pool.wait_ge(s_ag, ag_base(r) + 2 * (n - 1))
                    ins = pool.tensor_tensor(XS[:, n % 2, :], XN[:, tsl(t)], GB[:, t % 2, e, :], ALU.mult)
                    ins.then_inc(s_xg, 1)
                pool.wait_ge(s_xg, XSB[r] + (t + 1) * E)
                pool.memset(epsc[:, 3:4], 0.0).then_inc(s_xs, 1)

        def pe_moe0(pe, r):
            pe.wait_ge(s_wm, 32)
            pe.wait_ge(s_hg, r + 1)
            base = ag_base(r)

            def out_mm(v):
                t, e, c = v // ST0, v % ST0 // 2, v % 2
                pe.wait_ge(s_hid, base + v + 1)
                if e == 0 and c == 0 and t >= 2:
                    pe.wait_ge(s_xup, xup_base["moe", r] + t - 1)
                pe.matmul(bank(t % 2), w_out[:, e, c, :], HID[:, v % 3, :], start=(v % ST0 == 0),
                          stop=(v % ST0 == ST0 - 1)).then_inc(s_out, 1)

            for u in range(NT * ST0):
                t, e, c = u // ST0, u % ST0 // 2, u % 2
                if u >= 3:
                    pe.wait_ge(s_hid, base + u - 2)
                pe.matmul(pairbank(u, 0), w_in[:, e, c * P:(c + 1) * P], XN[:, tsl(t)], start=True, stop=True)
                pe.wait_ge(s_xg, XSB[r] + t * E + e + 1)
                pe.matmul(pairbank(u, 1), w_in[:, e, F0 + c * P:F0 + (c + 1) * P], XS[:, (t * E + e) % 2, :],
                          start=True, stop=True).then_inc(s_ag, 1)
                if u >= 2:
                    out_mm(u - 2)
            out_mm(NT * ST0 - 2)
            out_mm(NT * ST0 - 1)

        def act_moe0(act, r):
            base = ag_base(r)
            for u in range(NT * ST0):
                act.wait_ge(s_ag, base + u + 1)
                if u >= 2:
                    act.wait_ge(s_hid, base + u - 1)
                act.activation(GE[:, u % 2, :], pairbank(u, 0), ACT.Gelu).then_inc(s_ge, 1)

        def dve_moe0(dve, r):
            base = ag_base(r)

            def update(t):
                dve.wait_ge(s_out, base + (t + 1) * ST0)
                dve.scalar_tensor_tensor(out=XT[:, tsl(t)], in0=bank(t % 2), scalar=0.5, in1=XT[:, tsl(t)],
                                         op0=ALU.mult, op1=ALU.add).then_inc(s_xup, 1)

            for u in range(NT * ST0):
                dve.wait_ge(s_ge, base + u + 1)
                if u >= 3:
                    dve.wait_ge(s_out, base + u - 2)
                dve.tensor_tensor(HID[:, u % 3, :], GE[:, u % 2, :], pairbank(u, 1), ALU.mult).then_inc(s_hid, 1)
                if u % ST0 == 3 and u > ST0:
                    update(u // ST0 - 1)
            update(NT - 1)

        def rows1(g):
            return P if g < 4 else I1

        def pe_moe1(pe, r):
            pe.wait_ge(s_hg, r + 1)
            base = ag_base(r)

            def out_mm(v):
                t, g = v // ST1, v % ST1
                pe.wait_ge(s_hid, base + v + 1)
                if g == 0 and t >= 2:
                    pe.wait_ge(s_xup, xup_base["moe", r] + t - 1)
                pe.matmul(bank(t % 2), w_down1[0:rows1(g), g, :], HID[0:rows1(g), v % 3, :], start=(g == 0),
                          stop=(g == ST1 - 1)).then_inc(s_out, 1)

            for u in range(NT * ST1):
                t, g = u // ST1, u % ST1
                if u >= 3:
                    pe.wait_ge(s_hid, base + u - 2)
                n = rows1(g)
                pe.matmul(pairbank(u, 0)[0:n, :], w_gate1[:, g * P:g * P + n], XN[:, tsl(t)], start=True, stop=True)
                pe.matmul(pairbank(u, 1)[0:n, :], w_up1[:, g * P:g * P + n], XN[:, tsl(t)], start=True,
                          stop=True).then_inc(s_ag, 1)
                if u >= 2:
                    out_mm(u - 2)
            out_mm(NT * ST1 - 2)
            out_mm(NT * ST1 - 1)

        def act_moe1(act, r):
            base = ag_base(r)
            for u in range(NT * ST1):
                n = rows1(u % ST1)
                act.wait_ge(s_ag, base + u + 1)
                if u >= 2:
                    act.wait_ge(s_hgl, hgl_base(r) + u - 1)
                act.activation(GE[0:n, u % 2, :], pairbank(u, 0)[0:n, :], ACT.Silu).then_inc(s_ge, 1)

        s_hgl = sem("s_hgl")

        def hgl_base(r):
            return (r - 2) * NT * ST1

        def dve_moe1(dve, r, ch):
            base = ag_base(r)

            def update(t):
                dve.wait_ge(s_out, base + (t + 1) * ST1)
                ch.link(dve.tensor_tensor(YA[:, tsl(t)], YA[:, tsl(t)], bank(t % 2), ALU.add))
                dve.scalar_tensor_tensor(out=XT[:, tsl(t)], in0=YA[:, tsl(t)], scalar=0.5, in1=XT[:, tsl(t)],
                                         op0=ALU.mult, op1=ALU.add).then_inc(s_xup, 1)

            for u in range(NT * ST1):
                n = rows1(u % ST1)
                dve.wait_ge(s_ge, base + u + 1)
                if u >= 3:
                    dve.wait_ge(s_hid, base + u - 2)
                dve.tensor_tensor(HGL[0:n, u % 3, :], GE[0:n, u % 2, :], pairbank(u, 1)[0:n, :],
                                  ALU.mult).then_inc(s_hgl, 1)
                if u % ST1 == 3 and u > ST1:
                    update(u // ST1 - 1)
            update(NT - 1)

        def pool_moe1(pool, r):
            base = ag_base(r)
            for u in range(NT * ST1):
                t, g = u // ST1, u % ST1
                n = rows1(g)
                if g == 0:
                    pool.wait_ge(s_gb, 32 * (4 * r + t + 1))
                pool.wait_ge(s_hgl, hgl_base(r) + u + 1)
                if u >= 3:
                    pool.wait_ge(s_out, base + u - 2)
                if g < 4:
                    pool.tensor_tensor(HID[:, u % 3, :], HGL[:, u % 3, :], GB[:, t % 2, g, :],
                                       ALU.mult).then_inc(s_hid, 1)
                else:
                    pool.tensor_copy(HID[0:n, u % 3, :], HGL[0:n, u % 3, :]).then_inc(s_hid, 1)
                if g == 4:
                    pool.wait_ge(s_hid, base + u + 1)
                    pool.memset(epsc[:, 3:4], 0.0).then_inc(s_xs, 1)

        def iterations(latent):
            if latent:
                return [(0, 1, False, True, True), (1, NN - 2, True, True, True),
                        (NN - 2, NN - 1, True, True, False), (NN - 1, NN, True, False, False)]
            return [(0, 1, False, True, False), (1, NN - 1, True, True, False), (NN - 1, NN, True, False, False)]

        PRO = {0: 2 * NT + NT, 1: NT + 1 + 12}

        TAIL = [("den", 0)] + [("spread", h) for h in range(2)] + [("proj", h) for h in range(2)]

        def ring_starts(k):
            lat = k > 0
            n = sum(ring_total(i) for i in range(k)) + PRO[int(lat)] + len(ring_plan(False, True, False))
            starts = []
            for lo, hi, tail, ahead, build in iterations(lat):
                starts.append(n)
                n += (hi - lo) * len(ring_plan(tail, ahead, build))
            return starts, n

        def ring_total(k):
            lat = k > 0
            n = PRO[int(lat)] + len(ring_plan(False, True, False)) + len(TAIL)
            for lo, hi, tail, ahead, build in iterations(lat):
                n += (hi - lo) * len(ring_plan(tail, ahead, build))
            return n

        def ring_first(k):
            return sum(ring_total(i) for i in range(k))

        def run(eng, k, body):
            starts, end = ring_starts(k)
            for (lo, hi, tail, ahead, build), r0 in zip(iterations(k > 0), starts):
                per = len(ring_plan(tail, ahead, build))
                if hi - lo == 1:
                    body(lo, r0, tail, ahead, build, lo == 0)
                else:
                    with eng.Fori(0, hi - lo) as i:
                        body(i + lo, i * per + r0, tail, ahead, build, False)
            return end

        def slot(n):
            return (n % NQ) * QUAD

        def seq(n):
            return n // NQ

        STK = (24 * 16, 16 * 16)

        def stk_base(k):
            return NN * STK[0] * min(k, 1) + NN * STK[1] * max(k - 1, 0)

        def pe_unit(pe, k, n, u, bnk):
            qt, c0, w, heads = u
            for o, j in enumerate(heads):
                dst = bnk[:, o * w:(o + 1) * w]
                q = QS[0:CROW, bass.ds(slot(n) + j, 1), qt * P:(qt + 1) * P].squeeze(1)
                if k == 0:
                    key = KS[0:CROW, bass.ds(slot(n) + j, 1), c0:c0 + w].squeeze(1)
                else:
                    key = KS[0:CROW, bass.ds(seq(n), 1), c0:c0 + w].squeeze(1)
                diag = c0 + w == (qt + 1) * P
                ins = pe.matmul(dst, q, key, start=True, stop=not diag)
                if diag:
                    ins = pe.matmul(dst[:, w - P:w], identb[:, :], maskqk[:, :], start=False, stop=True)
            return ins

        def pe_scores(pe, k, n, s):
            kt, j = divmod(s, QUAD)
            q0 = kt * P
            tile = ps[s % 2]
            pieces = [(lo, hi) for lo, hi in ((q0, TT), (max(q0, TT), S)) if lo < hi]
            for lo, hi in pieces:
                dst = tile[:, lo // TT, lo % TT:lo % TT + hi - lo]
                diag = lo == q0
                if k == 0:
                    terms = [(slot(n) + j, CROW + 1)]
                else:
                    terms = [(seq(n), CROW + 1), (seq(n) + B, CROW)]
                for i, (ks, rows) in enumerate(terms):
                    ins = pe.matmul(dst, KS[0:rows, bass.ds(ks, 1), q0:q0 + P].squeeze(1),
                                    QS[0:rows, bass.ds(slot(n) + j, 1), lo:hi].squeeze(1),
                                    start=(i == 0), stop=(i == len(terms) - 1 and not diag))
                if diag:
                    ins = pe.matmul(dst[:, 0:P], identb[:, :], maskkq[:, :], start=False, stop=True)
            ins.then_inc(s_st, 1)

        def pe_pv(pe, k, n, kt, first):
            pe.wait_ge(s_exp, 32 * NN * k + n * STEPS + 4 * (kt + 1))
            if kt == 0:
                pe.wait_ge(s_vs, NN * k + n + 1)
                if not first:
                    pe.wait_ge(s_os, 2 * NN * k + 2 * n)
            q0 = kt * P
            for lo, hi in ((q0, TT), (max(q0, TT), S)):
                if lo >= hi:
                    continue
                for j in range(QUAD):
                    ins = pe.matmul(OUTP[32 * j:32 * j + 32, lo // TT, lo % TT:lo % TT + hi - lo],
                                    VS[:, kt, j, :], PR[:, kt % 2, j, lo:hi], start=(kt == 0),
                                    stop=(kt == (3 if lo < TT else KT - 1)))
            ins.then_inc(s_pv, 1)

        def pe_ring(pe, k, n, kind, arg, r, l):
            pe.wait_ge(s_rd, r - 1 if l >= 2 else r)
            bnk = bank(RING[l % 2])
            if kind == "unit":
                ins = pe_unit(pe, k, n + 1, arg, bnk)
            elif kind == "turn":
                pe.wait_ge(s_m4, NN * k + n + 2)
                ins = pe.transpose(bnk[0:QUAD * KT, 0:P], M4[:, :], identf[:, :])
            elif kind == "den":
                pe.wait_ge(s_os, 2 * NN * k + 2 * n)
                pick = (sel1 if k else sel0)[:, :].rearrange("p (j c) -> p j c", j=QUAD)[:, :, 0]
                for c in range(KT):
                    ins = pe.matmul(bnk[:, c * QUAD:(c + 1) * QUAD], OS[:, c * P:(c + 1) * P], pick,
                                    start=True, stop=True)
            elif kind == "spread":
                pe.wait_ge(s_rd, r)
                for i in range(KT // 2):
                    c = arg * (KT // 2) + i
                    ins = pe.matmul(bnk[:, i * P:(i + 1) * P], RX[:, c * P:(c + 1) * P], identf[:, :],
                                    start=True, stop=True)
            elif kind == "proj":
                pe.wait_ge(s_wos, NN * k + n)
                ins = pe.matmul(bnk, stage[:, 3, :], ON[:, arg * TT:(arg + 1) * TT], start=True, stop=True)
            else:
                w = ("rope", "swap", "lat").index(kind)
                if w == 0 and arg == 0:
                    pe.wait_ge(s_wst, NN * (k - 1) + n + 3)
                ins = pe.matmul(bnk, stage[:, w, :], XN[:, bass.ds(seq(n + 2) * S + arg * TT, TT)],
                                start=True, stop=True)
            ins.then_inc(s_rr, 1)

        def pe_attn(pe, k, kn):
            r = ring_first(k)
            pe.wait_ge(s_xn, 4 * (kn + 1))
            l = 0

            def use(mm):
                nonlocal l
                if l >= 2:
                    pe.wait_ge(s_rd, r + l - 1)
                elif k:
                    pe.wait_ge(s_rd, r)
                mm(bank(RING[l % 2])).then_inc(s_rr, 1)
                l += 1

            if k == 0:
                pe.wait_ge(s_w, N_WFIRST)
                for w in (0, 1):
                    for t in range(NT):
                        use(lambda o: pe.matmul(o, wq0[:, w, :], XN[:, tsl(t)], start=True, stop=True))

                def values(o, t):
                    for i in range(4):
                        ins = pe.matmul(o[:, i * P:(i + 1) * P], XN[:, (4 * t + i) * P:(4 * t + i + 1) * P],
                                        wq0[:, 2, :], start=True, stop=True)
                    return ins
                for t in range(NT):
                    use(lambda o: values(o, t))
            else:
                for t in range(NT):
                    use(lambda o: pe.matmul(o[0:96, :], w_kva, XN[:, tsl(t)], start=True, stop=True))

                def values(o):
                    for i in range(NTT):
                        ins = pe.matmul(o[:, i * LAT:(i + 1) * LAT], XN[:, i * P:(i + 1) * P], w_kva[:, 0:LAT],
                                        start=True, stop=True)
                    return ins
                use(values)
                for m in range(2):
                    pe.wait_ge(s_wst, NN * (k - 1) + m + 1)
                    for h in range(2):
                        for w in range(3):
                            use(lambda o: pe.matmul(o, stage[:, w, :], XN[:, tsl(h)], start=True, stop=True))
            assert l == PRO[int(k > 0)]
            pe.wait_ge(s_stk, stk_base(k) + STK[int(k > 0)])
            pe.wait_ge(s_cdma, cdma_need[k])
            pe.wait_ge(s_zero, zero_need[k])
            for i, (_, kind, arg) in enumerate(ring_plan(False, True, False)):
                pe_ring(pe, k, -1, kind, arg, r + l, l)
                l += 1

            def body(n, r0, tail, ahead, build, first):
                plan = ring_plan(tail, ahead, build)
                at_ = 0

                def ring_until(s):
                    nonlocal at_
                    while at_ < len(plan) and plan[at_][0] <= s:
                        pe_ring(pe, k, n, plan[at_][1], plan[at_][2], r0 + at_, at_)
                        at_ += 1

                pe.wait_ge(s_crow, 16 * (NN * k + n + 1))
                for s in range(STEPS):
                    if ahead and s == 4:
                        pe.wait_ge(s_stk, stk_base(k) + STK[int(k > 0)] * (n + 2))
                    if not (first and s < 2 and k == 0):
                        pe.wait_ge(s_exp, 32 * NN * k + n * STEPS + s - 1)
                    pe_scores(pe, k, n, s)
                    ring_until(s)
                    if s % QUAD == 1 and s > QUAD:
                        pe_pv(pe, k, n, s // QUAD - 1, first)
                ring_until(STEPS)
                pe_pv(pe, k, n, KT - 1, first)

            end = run(pe, k, body)
            for i, (kind, arg) in enumerate(TAIL):
                pe_ring(pe, k, NN, kind, arg, end + i, i)

        def act_attn(act, k):
            def body(n, r0, tail, ahead, build, first):
                for s in range(STEPS):
                    kt, j = divmod(s, QUAD)
                    q0 = kt * P
                    act.wait_ge(s_st, 32 * NN * k + n * STEPS + s + 1)
                    if j == 0 and not (first and kt < 2):
                        act.wait_ge(s_pv, 8 * NN * k + n * KT + kt - 1)
                    act.activation(PR[:, kt % 2, j, q0:S], ps[s % 2][:, :, :].rearrange("p a t -> p (a t)")[:, q0:S],
                                   ACT.Exp).then_inc(s_exp, 1)
            run(act, k, body)

        dest = (XT, YA, YA)

        def dve_ring(dve, k, n, kind, arg, r, l):
            dve.wait_ge(s_rr, r + 1)
            bnk = bank(RING[l % 2])
            if kind == "unit":
                qt, c0, w, heads = arg
                dve.tensor_reduce(BM[:, c0 // TT, heads[0]:heads[0] + len(heads), qt],
                                  bnk[:, 0:w * len(heads)].rearrange("p (j w) -> p j w", w=w),
                                  AX.X, ALU.max).then_inc(s_rd, 1)
            elif kind == "turn":
                dve.tensor_copy(CT[:, :], bnk[0:QUAD * KT, 0:P]).then_inc(s_rd, 1)
            elif kind == "den":
                dve.reciprocal(RD[:, :], bnk[:, 0:KT * QUAD]).then_inc(s_den, 1)
                dve.wait_ge(s_den, NN * k + n)
                dve.tensor_copy(RX[:, :].rearrange("p (c r) -> p c r", r=32),
                                RD[:, :].unsqueeze(2).to_broadcast([P, KT * QUAD, 32])).then_inc(s_rd, 1)
            elif kind == "spread":
                hs = slice(arg * TT, (arg + 1) * TT)
                dve.tensor_tensor(ON[:, hs], OS[:, hs], bnk, ALU.mult).then_inc(s_rd, 1)
            elif kind == "proj":
                x = dest[k][:, bass.ds(seq(n - 1) * S + arg * TT, TT)]
                ins = dve.tensor_tensor(x, x, bnk, ALU.add)
                ins.then_inc(s_rd, 1)
            elif kind == "lat":
                m = n + 2
                h = arg
                if not (isinstance(m, int) and m == 0):
                    dve.wait_ge(s_stk, stk_base(k) + STK[1] * m)
                dve.tensor_copy(HL[:, 2, h * TT:(h + 1) * TT], bnk).then_inc(s_lat, 1)
                dve.wait_ge(s_lat, 2 * NN * (k - 1) + 2 * m + h + 1)
                dve.tensor_tensor(HL[:, 3, h * TT:(h + 1) * TT], bnk, HL[:, 2, h * TT:(h + 1) * TT],
                                  ALU.subtract).then_inc(s_rd, 1)
            else:
                w = ("rope", "swap").index(kind)
                m = n + 2
                if not (isinstance(m, int) and m == 0):
                    dve.wait_ge(s_kb, kb_base(k) + 6 * m)
                dve.tensor_tensor(BT[:, 2 * arg + w, :], bnk, (cosT, sinT)[w][:, arg * TT:(arg + 1) * TT],
                                  ALU.mult).then_inc(s_rd, 1)

        def kb_base(k):
            return (k - 1) * (3 * NT + 6 * NN) + 3 * NT

        def dve_plan(dve, k, n, plan, r0):
            for i, (_, kind, arg) in enumerate(plan):
                if kind == "turn":
                    dve.wait_ge(s_rd, r0 + i)
                    if not (isinstance(n, int) and k == 0 and n < 0):
                        dve.wait_ge(s_crow, 16 * (NN * k + n + 1))
                    dve.tensor_tensor(M4[:, :], BM[:, 0, :, :].rearrange("p j q -> p (j q)"),
                                      BM[:, 1, :, :].rearrange("p j q -> p (j q)"), ALU.max).then_inc(s_m4, 1)
                dve_ring(dve, k, n, kind, arg, r0 + i, i)

        def dve_copy_out(dve, k, n):
            dve.wait_ge(s_pv, 8 * NN * k + n * KT)
            for h in range(2):
                dve.tensor_copy(OS[:, h * TT:(h + 1) * TT], OUTP[:, h, :]).then_inc(s_os, 1)

        SC0 = float(np.float32(1.0) / np.sqrt(np.float32(HD0)))

        def dve_attn(dve, k, ch):
            r = ring_first(k)
            if k == 0:
                for i in range(2 * NT):
                    w, t = divmod(i, NT)
                    sc = (SC0, 1.0)[w]
                    bnk = bank(RING[i % 2])
                    dve.wait_ge(s_rr, r + i + 1)
                    ch.link(dve.tensor_scalar(HL[:, 2 * w, tsl(t)], bnk, sc, None, ALU.mult))
                    dve.scalar_tensor_tensor(out=HL[:, 2 * w + 1, tsl(t)], in0=bnk, scalar=sc,
                                             in1=HL[:, 2 * w, tsl(t)], op0=ALU.mult,
                                             op1=ALU.subtract).then_inc(s_rd, 1)
                for t in range(NT):
                    dve.wait_ge(s_rr, r + 2 * NT + t + 1)
                    dve.tensor_copy(YA[:, tsl(t)], bank(RING[t % 2])).then_inc(s_rd, 1)
            else:
                for t in range(NT):
                    bnk = bank(RING[t % 2])
                    dve.wait_ge(s_rr, r + t + 1)
                    cs = slice((t % 2) * TT, (t % 2 + 1) * TT)
                    if t:
                        dve.wait_ge(s_kb, kb_base(k) - 3 * NT + 3 * t)
                    ch.up(dve.tensor_copy(BT[0:32, 0, :], bnk[0:32, :]))
                    ch.up(dve.tensor_tensor(BT[32:64, 0, :], bnk[32:64, :], cosT[32:64, cs], ALU.mult))
                    dve.tensor_tensor(BT[32:64, 1, :], bnk[64:96, :], sinT[64:96, cs], ALU.mult).then_inc(s_rd, 1)
                dve.wait_ge(s_rr, r + NT + 1)
                dve.tensor_copy(VL[:, :, :].rearrange("p i c -> p (i c)"), bank(RING[NT % 2])[:, 0:NTT * LAT])\
                   .then_inc(s_rd, 1)
                dve.wait_ge(s_kdma, 96 * k)
                l = NT + 1
                for m in range(2):
                    for h in range(2):
                        for kind in ("rope", "swap", "lat"):
                            dve_ring(dve, k, m - 2, kind, h, r + l, l)
                            l += 1
            l = PRO[int(k > 0)]
            for i, (_, kind, arg) in enumerate(ring_plan(False, True, False)):
                if kind == "turn":
                    dve.wait_ge(s_rd, r + l + i)
                    if k:
                        dve.wait_ge(s_crow, 16 * NN * k)
                    dve.tensor_tensor(M4[:, :], BM[:, 0, :, :].rearrange("p j q -> p (j q)"),
                                      BM[:, 1, :, :].rearrange("p j q -> p (j q)"), ALU.max).then_inc(s_m4, 1)
                dve_ring(dve, k, -1, kind, arg, r + l + i, l + i)

            def body(n, r0, tail, ahead, build, first):
                if tail:
                    dve_copy_out(dve, k, n)
                dve_plan(dve, k, n, ring_plan(tail, ahead, build), r0)

            end = run(dve, k, body)
            dve_copy_out(dve, k, NN)
            for i, (kind, arg) in enumerate(TAIL):
                dve_ring(dve, k, NN, kind, arg, end + i, i)
            dve.wait_ge(s_rd, end + len(TAIL))
            s_done = s_xup if k == 0 else s_ya
            dve.memset(epsc[:, 2:3], 0.0).then_inc(s_done, 4)

        s_ya = sem("s_ya")
        s_kdma = sem("s_kdma")
        cdma_need = (16 * 2, 16 * 2, 16 * 2)
        zero_need = (1, 2, 3)

        def pool_attn_setup(pool, k, ch):
            if k == 0:
                pool.wait_ge(s_xup, xup_base["moe", 0] + 4)
            else:
                pool.wait_ge(s_xup, setup_after[k])
            for h in range(H):
                ch.up(pool.memset(QS[:, h, :].bitcast(F32), 0.0))
                ch.up(pool.memset(KS[:, h, :].bitcast(F32), 0.0))
            ch.wait()
            ch.link(pool.memset(KS[CROW:CROW + 1, :, :].rearrange("p h s -> p (h s)"), -1.0))
            ch.up(pool.memset(VS[:, :, :, :].rearrange("p a j c -> p (a j c)"), 0.0))
            ch.wait()
            c = LAT if k else HD0
            pool.memset(VS[:, :, :, c:c + 1].rearrange("p a j c -> p (a j) c"), 1.0).then_inc(s_zero, 1)

        def pool_attn(pool, k, ch):
            w_o = wo1 if k else wo0

            def stage_q(m, first):
                if not first:
                    pool.wait_ge(s_lat, 2 * NN * (k - 1) + 2 * m)
                pool.wait_ge(s_const, 1)
                qd = m % NQ
                for i, w in enumerate((w_rope, w_swap, w_lat)):
                    src = w[:, bass.ds(qd, 1), :].squeeze(1)
                    ins = pool.tensor_copy(stage[:, i, :], src)
                    if i < 2:
                        ch.up(ins)
                ins.then_inc(s_wst, 1)
                ch.wait()
                pool.wait_ge(s_wst, NN * (k - 1) + m + 1)

            def parts(m, h, rings):
                n0 = kb_base(k) + 6 * m + 3 * h
                hs = slice(h * TT, (h + 1) * TT)
                if not (isinstance(m, int) and m == 0):
                    pool.wait_ge(s_stk, stk_base(k) + STK[1] * m)
                pool.wait_ge(s_rd, rings)
                pool.tensor_tensor(HL[:, 0, hs], BT[:, 2 * h, :], BT[:, 2 * h + 1, :], ALU.add).then_inc(s_kb, 1)
                pool.tensor_tensor(BT[:, 2 * h, :], BT[:, 2 * h, :], BT[:, 2 * h + 1, :], ALU.add).then_inc(s_kb, 1)
                pool.wait_ge(s_kb, n0 + 2)
                pool.tensor_tensor(HL[:, 1, hs], BT[:, 2 * h, :], HL[:, 0, hs], ALU.subtract).then_inc(s_kb, 1)

            r = ring_first(k)
            if k:
                stage_q(0, True)
                for t in range(NT):
                    n0 = kb_base(k) - 3 * NT + 3 * t
                    pool.wait_ge(s_rd, r + t + 1)
                    ch.link(pool.tensor_tensor(BT[32:64, 0, :], BT[32:64, 0, :], BT[32:64, 1, :], ALU.add))
                    pool.tensor_scalar(BT[0:64, 2, :], BT[0:64, 0, :], 0.125, None, ALU.mult).then_inc(s_kb, 1)
                    pool.wait_ge(s_kb, n0 + 1)
                    pool.tensor_copy(HL[0:64, 0, tsl(t)], BT[0:64, 2, :]).then_inc(s_kb, 1)
                    pool.wait_ge(s_kb, n0 + 2)
                    pool.tensor_tensor(HL[0:64, 1, tsl(t)], BT[0:64, 2, :], HL[0:64, 0, tsl(t)],
                                       ALU.subtract).then_inc(s_kb, 1)
                pool.wait_ge(s_kdma, 96 * k)
                for m in range(2):
                    for h in range(2):
                        parts(m, h, r + NT + 1 + 6 * m + 3 * h + 2)
                    if m == 0:
                        stage_q(1, False)

            def stage_v(n, first):
                if first:
                    pool.wait_ge(s_rd, r + (NT + 1 if k else 3 * NT))
                else:
                    pool.wait_ge(s_pv, 8 * NN * k + n * KT)
                pool.wait_ge(s_const, 1)
                if k == 0:
                    src = V0[:, bass.ds(seq(n) * KT, KT), bass.ds((n % NQ) * 32, 32)]
                    pool.tensor_copy(VS[:, :, :, 0:HD0], src.rearrange("p i (j d) -> p i j d", j=QUAD))\
                        .then_inc(s_vs, 1)
                else:
                    src = VL[:, bass.ds(seq(n) * KT, KT), :]
                    for j in range(QUAD):
                        ins = pool.tensor_copy(VS[:, :, j, 0:LAT], src)
                        if j < QUAD - 1:
                            ch.up(ins)
                    ch.wait()
                    ins.then_inc(s_vs, 1)

            def finish(n):
                pool.wait_ge(s_pv, 8 * NN * k + n * KT)
                pool.wait_ge(s_const, 1)
                src = w_o[:, bass.ds((n - 1) % NQ, 1), :].squeeze(1)
                pool.tensor_copy(stage[:, 3, :], src).then_inc(s_wos, 1)

            def body(n, r0, tail, ahead, build, first):
                n_ch = ch.n
                stage_v(n, first)
                if tail:
                    finish(n)
                if build:
                    plan = ring_plan(tail, ahead, build)
                    stage_q(n + 2, False)
                    for h in range(2):
                        at_ = max(i for i, (_, kd, ar) in enumerate(plan) if kd in ("rope", "swap") and ar == h)
                        parts(n + 2, h, r0 + at_ + 1)

            base = ch.n
            starts, end = ring_starts(k)
            for (lo, hi, tail, ahead, build), r0 in zip(iterations(k > 0), starts):
                per = len(ring_plan(tail, ahead, build))
                own = (3 if k else 0) + (2 if build else 0)
                c0 = ch.n
                if hi - lo == 1:
                    body(lo, r0, tail, ahead, build, lo == 0)
                else:
                    with pool.Fori(0, hi - lo) as i:
                        ch.n = i * own + c0
                        body(i + lo, i * per + r0, tail, ahead, build, False)
                ch.n = c0 + own * (hi - lo)
            finish(NN)

        def sp_attn(sp, k):
            if k == 0:
                sp.wait_ge(s_zero, 1)
                sp.dma_start(QS[24:24 + SLOPE_PIECES, :, :], a["slopes"]).then_inc(s_cdma, 16)
                sp.dma_start(KS[24:24 + SLOPE_PIECES, :, :], a["kpos"]).then_inc(s_cdma, 16)
                sp.wait_ge(s_rd, 2 * NT)
            r = ring_first(k)

            def stacks(m):
                b_, sl = seq(m), slot(m)
                if k == 0:
                    for j in range(QUAD):
                        for rows, part in ((0, 0), (8, 1), (16, 0)):
                            yield QS[rows:rows + 8, bass.ds(sl + j, 1), :].squeeze(1), part, j, b_
                        for rows, part in ((0, 2), (8, 2), (16, 3)):
                            yield KS[rows:rows + 8, bass.ds(sl + j, 1), :].squeeze(1), part, j, b_

            def put0(m):
                for dst, part, j, b_ in stacks(m):
                    h0 = ((m % NQ) * QUAD + j) * HD0
                    sp.dma_start(dst, HL[h0:h0 + HD0, part, b_ * S:(b_ + 1) * S]).then_inc(s_stk, 16)

            def put1(m):
                for j in range(QUAD):
                    for part, row, n_ in ((0, 0, 32), (2, 32, 16), (1, 48, 32), (3, 80, 16)):
                        sp.dma_start(QS[row:row + n_, bass.ds(slot(m) + j, 1), :].squeeze(1),
                                     HL[32 * j:32 * j + n_, part, 0:S]).then_inc(s_stk, 16)

            def crow(m, turned, landed=None):
                sp.wait_ge(s_rd, turned)
                if landed is not None:
                    sp.wait_ge(s_stk, landed)
                sp.dma_start(QS[CROW:CROW + 1, bass.ds(slot(m), QUAD), :], CT[:, :]).then_inc(s_crow, 16)

            per0 = PRO[int(k > 0)] + len(ring_plan(False, True, False))
            if k == 0:
                for m in range(2):
                    put0(m)
                    sp.wait_ge(s_stk, STK[0] * (m + 1))
                crow(0, r + per0)
                starts, _ = ring_starts(k)
                rr = starts[0]
                for n in range(NN - 1):
                    if n + 2 < NN:
                        if n + 2 >= NQ:
                            sp.wait_ge(s_st, STEPS * (n + 2 - NQ + 1))
                        put0(n + 2)
                        sp.wait_ge(s_stk, STK[0] * (n + 3))
                    rr += len(ring_plan(n > 0, True, False))
                    crow(n + 1, rr)
            else:
                sp.wait_ge(s_zero, k + 1)
                sp.wait_ge(s_kb, kb_base(k))
                for dst, src in ((KS[0:32, 0:B, :], HL[32:64, 0, :]), (KS[48:80, 0:B, :], HL[32:64, 0, :]),
                                 (KS[32:48, 0:B, :], HL[0:16, 0, :]), (KS[80:96, 0:B, :], HL[0:16, 0, :]),
                                 (KS[0:32, B:2 * B, :], HL[32:64, 1, :]), (KS[32:48, B:2 * B, :], HL[0:16, 1, :])):
                    sp.dma_start(dst, src.rearrange("p (b s) -> p b s", b=B)).then_inc(s_kdma, 16)
                sp.wait_ge(s_kdma, 96 * k)
                for m in range(2):
                    sp.wait_ge(s_kb, kb_base(k) + 6 * (m + 1))
                    sp.wait_ge(s_rd, r + NT + 1 + 6 * (m + 1))
                    put1(m)
                    sp.wait_ge(s_stk, stk_base(k) + STK[1] * (m + 1))
                crow(0, r + per0)
                starts, _ = ring_starts(k)
                for (lo, hi, tail, ahead, build), r0 in zip(iterations(True), starts):
                    plan = ring_plan(tail, ahead, build)

                    def it(n, r0):
                        if build:
                            lat_at = max(i for i, (_, kd, _) in enumerate(plan) if kd == "lat")
                            sp.wait_ge(s_rd, r0 + lat_at + 1)
                            sp.wait_ge(s_kb, kb_base(k) + 6 * (n + 3))
                            sp.wait_ge(s_const, 1)
                            put1(n + 2)
                        if ahead:
                            crow(n + 1, r0 + len(plan), stk_base(k) + STK[1] * (n + 3) if build else None)
                    if hi - lo == 1:
                        it(lo, r0)
                    else:
                        with sp.Fori(0, hi - lo) as i:
                            it(i + lo, i * len(plan) + r0)

        def sp_last_weights(sp):
            sp.wait_ge(s_xup, xup_base["moe", 1] + 4)
            loads = [(cosT, a["cosT"]), (sinT, a["sinT"]), (w_rope, a["w_rope"].rearrange("p (g m) -> p g m", g=NQ)),
                     (w_swap, a["w_swap"].rearrange("p (g m) -> p g m", g=NQ)), (w_kva, a["w_kva"]),
                     (w_gate1, a["w_gate1"]), (w_up1, a["w_up1"]), (w_down1[:, 0:4, :], a["Wd"].rearrange("(g e) i o -> (e i) g o", e=2)),
                     (w_down1[0:I1, 4, :], a["sWd"]), (w_rt1, a["Wgate"]),
                     (wqn, a["wqn"]), (wkb, a["wkb"]), (won, a["won"])]
            for dst, src in loads:
                sp.dma_start(dst, src).then_inc(s_wl, 16)

        N_WL = 16 * 13

        def pe_comp(pe):
            pe.wait_ge(s_wl, N_WL)
            for h in range(H):
                ins = pe.matmul(bank(6)[:, h * 32:(h + 1) * 32], wqn[:, h, :], wkb[:, h, :], start=True, stop=True)
            ins.then_inc(s_comp, 1)
            for h in range(H):
                g, j = divmod(h, QUAD)
                ins = pe.matmul(bank(7)[32 * j:32 * j + 32, g * P:(g + 1) * P], wkb[:, h, :], won[:, h, :],
                                start=True, stop=True)
            ins.then_inc(s_comp, 1)

        def dve_comp(dve):
            dve.wait_ge(s_comp, 1)
            dve.tensor_copy(w_lat.rearrange("p g m -> p (g m)"), bank(6)).then_inc(s_compd, 1)
            dve.wait_ge(s_comp, 2)
            dve.tensor_copy(wo1[:, :, :].rearrange("p g m -> p (g m)"), bank(7)).then_inc(s_compd, 1)

        def pe_scan(pe, kn):
            for t in range(NT):
                if t == 0:
                    pe.wait_ge(s_xn, 4 * (kn + 1))
                else:
                    pe.wait_ge(s_sa, 2 * t)
                pe.matmul(bank(0), w_inp[:, 0, :], XN[:, tsl(t)], start=True, stop=True)
                pe.matmul(bank(1), w_inp[:, 1, :], XN[:, tsl(t)], start=True, stop=True).then_inc(s_sp, 1)
            for t in range(NT):
                pe.wait_ge(s_sd, 1 + t // 2)
                if t:
                    pe.wait_ge(s_so, t)
                for w in range(3):
                    ins = pe.matmul(bank(2 + w), w_dbc[:, w, :], MX[:, tsl(t)], start=True, stop=True)
                ins.then_inc(s_sp, 1)
            for t in range(NT):
                pe.wait_ge(s_sd, 3 + t // 2)
                if t >= 2:
                    pe.wait_ge(s_ya, 4 + t - 1)
                pe.matmul(bank(5 + t % 2), w_outp[:, :], DTm[:, tsl(t)], start=True, stop=True).then_inc(s_sp, 1)

        def act_scan(act, ch):
            for t in range(NT):
                b_, o = divmod(t * TT, S)
                act.wait_ge(s_sp, t + 1)
                act.activation(XP[:, b_, 1 + o:1 + o + TT], bank(0), ACT.Identity,
                               bias=colp[:, C_INB0:C_INB0 + 1]).then_inc(s_sa, 1)
                act.activation(SG[:, tsl(t)], bank(1), ACT.Sigmoid, bias=colp[:, C_INB1:C_INB1 + 1]).then_inc(s_sa, 1)
            ch.link(act.activation(colw[:, 2:3], colp[:, C_A:C_A + 1], ACT.Exp))
            ch.link(act.mul(colw[:, 3:4], colw[:, 2:3], -1.0))
            for t in range(NT):
                act.wait_ge(s_sp, NT + t + 1)
                ch.up(act.activation(BTm[:, tsl(t)], bank(3), ACT.Tanh, bias=colp[:, C_BB:C_BB + 1]))
                ch.up(act.activation(CTm[:, tsl(t)], bank(4), ACT.Tanh, bias=colp[:, C_CB:C_CB + 1]))
                ch.link(act.activation(DEC[:, tsl(t)], bank(2), ACT.Abs, bias=colp[:, C_DTB:C_DTB + 1]))
                ch.link(act.activation(DEC[:, tsl(t)], DEC[:, tsl(t)], ACT.Exp, scale=-1.0))
                act.activation(DEC[:, tsl(t)], DEC[:, tsl(t)], ACT.Ln, bias=1.0).then_inc(s_sa, 1)
            for t in range(NT):
                act.wait_ge(s_so, t + 1)
                act.activation(DEC[:, tsl(t)], DTm[:, tsl(t)], ACT.Exp, scale=colw[:, 3:4]).then_inc(s_sa, 1)

        def dve_scan(dve, kn, ch):
            def col(c):
                return colp[:, c:c + 1]

            dve.wait_ge(s_xn, 4 * (kn + 1))
            for b_ in range(B):
                ch.up(dve.memset(XP[:, b_, 0:1], 0.0))
                ch.up(dve.memset(XP[:, b_, S + 1:S + 2], 0.0))
            for b_ in range(B):
                dve.wait_ge(s_sa, 4 * (b_ + 1))
                ch.wait()
                m = MX[:, b_ * S:(b_ + 1) * S]
                ch.link(dve.tensor_scalar(m, XP[:, b_, 1:S + 1], col(C_DW1), col(C_DWB), ALU.mult, ALU.add))
                ch.link(dve.scalar_tensor_tensor(out=m, in0=XP[:, b_, 0:S], scalar=col(C_DW0), in1=m,
                                                 op0=ALU.mult, op1=ALU.add))
                dve.scalar_tensor_tensor(out=m, in0=XP[:, b_, 2:S + 2], scalar=col(C_DW2), in1=m,
                                         op0=ALU.mult, op1=ALU.add).then_inc(s_sd, 1)
            for t in range(NT):
                dve.wait_ge(s_sa, 2 * NT + t + 1)
                ch.link(dve.tensor_scalar(DTm[:, tsl(t)], bank(2), col(C_DTB), 0.0, ALU.add, ALU.max))
                dve.tensor_tensor(DTm[:, tsl(t)], DTm[:, tsl(t)], DEC[:, tsl(t)], ALU.add).then_inc(s_so, 1)
            for b_ in range(B):
                c = slice(b_ * S, (b_ + 1) * S)
                dve.wait_ge(s_sa, 3 * NT + 2 * (b_ + 1))
                dve.wait_ge(s_so, NT)
                ch.link(dve.tensor_tensor(BTm[:, c], BTm[:, c], DTm[:, c], ALU.mult))
                ch.link(dve.tensor_tensor(BTm[:, c], BTm[:, c], MX[:, c], ALU.mult))
                ch.link(dve.tensor_tensor_scan(ST_[:, c], DEC[:, c], BTm[:, c], 0.0, ALU.mult, ALU.add))
                ch.link(dve.tensor_tensor(ST_[:, c], ST_[:, c], CTm[:, c], ALU.mult))
                ch.link(dve.scalar_tensor_tensor(out=ST_[:, c], in0=MX[:, c], scalar=col(C_DSK), in1=ST_[:, c],
                                                 op0=ALU.mult, op1=ALU.add))
                dve.tensor_tensor(DTm[:, c], ST_[:, c], SG[:, c], ALU.mult).then_inc(s_sd, 1)
            for t in range(NT):
                dve.wait_ge(s_sp, 2 * NT + t + 1)
                dve.scalar_tensor_tensor(out=YA[:, tsl(t)], in0=bank(5 + t % 2), scalar=col(C_OB),
                                         in1=YA[:, tsl(t)], op0=ALU.add, op1=ALU.add).then_inc(s_ya, 1)

        def pe_ffn(pe, kn):
            pe.wait_ge(s_xn, 4 * (kn + 1))
            for t in range(NT):
                if t:
                    pe.wait_ge(s_sa, 4 * NT + 2 * t)
                pe.matmul(bank(0), w_f1[:, 0, :], XN[:, tsl(t)], start=True, stop=True)
                pe.matmul(bank(1), w_f1[:, 1, :], XN[:, tsl(t)], start=True, stop=True).then_inc(s_sp, 1)
                pe.wait_ge(s_sa, 4 * NT + 2 * (t + 1))
                if t >= 2:
                    pe.wait_ge(s_xup, xup_base["scan", 0] + t - 1)
                pe.matmul(bank(2 + t % 2), w_f2[:, 0, :], F1[:, 0, :], start=True, stop=False)
                pe.matmul(bank(2 + t % 2), w_f2[:, 1, :], F1[:, 1, :], start=False, stop=True).then_inc(s_sp, 1)

        def act_ffn(act):
            for t in range(NT):
                act.wait_ge(s_sp, 3 * NT + 2 * t + 1)
                for c in range(2):
                    act.activation(F1[:, c, :], bank(c), ACT.Gelu,
                                   bias=colp[:, C_F1B0 + c:C_F1B0 + c + 1]).then_inc(s_sa, 1)

        def dve_ffn(dve, ch):
            for t in range(NT):
                dve.wait_ge(s_sp, 3 * NT + 2 * (t + 1))
                ch.link(dve.scalar_tensor_tensor(out=YA[:, tsl(t)], in0=bank(2 + t % 2),
                                                 scalar=colp[:, C_F2B:C_F2B + 1], in1=YA[:, tsl(t)],
                                                 op0=ALU.add, op1=ALU.add))
                dve.tensor_tensor(XT[:, tsl(t)], XT[:, tsl(t)], YA[:, tsl(t)], ALU.add).then_inc(s_xup, 1)

        def pe_store(pe):
            pe.wait_ge(s_xup, xup_base["end", 0])
            for i in range(NTT):
                ins = pe.transpose(bank(i // 4)[:, (i % 4) * P:(i % 4 + 1) * P], XT[:, i * P:(i + 1) * P], identf[:, :])
                if i % 4 == 3:
                    ins.then_inc(s_ld, 1)

        def dve_store(dve):
            for t in range(NT):
                dve.wait_ge(s_ld, NT + t + 1)
                dve.tensor_copy(XN[:, tsl(t)], bank(t)).then_inc(s_fin, 1)

        def sp_store(sp):
            for t in range(NT):
                sp.wait_ge(s_fin, t + 1)
                sp.dma_start(out.rearrange("(i p) d -> p i d", p=P)[:, 4 * t:4 * t + 4, :],
                             XN[:, tsl(t)].rearrange("p (i d) -> p i d", i=4)).then_inc(s_store, 16)
            sp.wait_ge(s_store, 16 * NT)

        xup_base = {("moe", 0): 4, ("attn", 0): 8, ("moe", 1): 12, ("moe", 2): 16, ("scan", 0): 20,
                    ("moe", 3): 24, ("end", 0): 28}
        setup_after = {1: 16, 2: 24}

        block = ctx.enter_context(nc.Block())

        @block.sync
        def _(sp):
            sp_load(sp)
            sp_gates(sp, 0, False)
            sp_attn(sp, 0)
            sp.wait_ge(s_xup, 12)
            sp_gates(sp, 1, False)
            sp_last_weights(sp)
            sp_attn(sp, 1)
            sp_gates(sp, 2, True)
            sp_attn(sp, 2)
            sp_gates(sp, 3, True)
            sp_store(sp)

        @block.gpsimd
        def _(pool):
            pool_const(pool)
            ch = Chain(pool, s_pool)
            ch.n = 7
            pool_moe0(pool, 0)
            pool_attn_setup(pool, 0, ch)
            pool_attn(pool, 0, ch)
            pool_moe0(pool, 1)
            pool.wait_ge(s_compd, 2)
            pool_attn_setup(pool, 1, ch)
            pool_attn(pool, 1, ch)
            pool_moe1(pool, 2)
            pool_attn_setup(pool, 2, ch)
            pool_attn(pool, 2, ch)
            pool_moe1(pool, 3)

        @block.scalar
        def _(act):
            ch = Chain(act, s_act)
            act.wait_ge(s_const, N_CONST)
            act_norm(act, 0, "plain", ch)
            act_router(act, 0)
            act_moe0(act, 0)
            act_norm(act, 1, "plain", ch)
            act_attn(act, 0)
            act_norm(act, 2, "plain", ch)
            act_router(act, 1)
            act_moe0(act, 1)
            act_norm(act, 3, "fused", ch)
            act_attn(act, 1)
            act_norm(act, 4, "rms", ch)
            act_router(act, 2)
            act_moe1(act, 2)
            act_norm(act, 5, "fused", ch)
            act_scan(act, ch)
            act_norm(act, 6, "ln2", ch)
            act_ffn(act)
            act_norm(act, 7, "fused", ch)
            act_attn(act, 2)
            act_norm(act, 8, "rms", ch)
            act_router(act, 3)
            act_moe1(act, 3)

        @block.tensor
        def _(pe):
            pe_load(pe)
            pe_norm(pe, 0, "plain", (s_xup, 4))
            pe.wait_ge(s_w, N_WFIRST)
            pe_router(pe, 0, 0, w_rt0[:, :], False, True)
            pe_moe0(pe, 0)
            pe_norm(pe, 1, "plain", (s_xup, 8))
            pe_attn(pe, 0, 1)
            pe_norm(pe, 2, "plain", (s_xup, 12))
            pe_router(pe, 1, 2, w_rt0[:, :], False, True)
            pe_moe0(pe, 1)
            pe.wait_ge(s_xup, 16)
            pe_comp(pe)
            pe_norm(pe, 3, "fused", (s_xup, 16))
            pe_attn(pe, 1, 3)
            pe_norm(pe, 4, "rms", (s_ya, 4))
            pe_router(pe, 2, 4, w_rt1, True, False)
            pe_moe1(pe, 2)
            pe_norm(pe, 5, "fused", (s_xup, 20))
            pe_scan(pe, 5)
            pe_norm(pe, 6, "ln2", (s_ya, 8))
            pe_ffn(pe, 6)
            pe_norm(pe, 7, "fused", (s_xup, 24))
            pe_attn(pe, 2, 7)
            pe_norm(pe, 8, "rms", (s_ya, 12))
            pe_router(pe, 3, 8, w_rt1, True, False)
            pe_moe1(pe, 3)
            pe_store(pe)

        @block.vector
        def _(dve):
            ch = Chain(dve, s_dve)
            dve_load(dve)
            dve.wait_ge(s_const, N_CONST)
            dve.wait_ge(s_w, N_WFIRST)
            dve_norm(dve, 0, "plain")
            dve_router(dve, 0, True, ch)
            dve_moe0(dve, 0)
            dve_norm(dve, 1, "plain")
            dve_attn(dve, 0, ch)
            dve_norm(dve, 2, "plain")
            dve_router(dve, 1, True, ch)
            dve_moe0(dve, 1)
            dve_comp(dve)
            dve_norm(dve, 3, "fused", w=colw[:, 0:1])
            dve_attn(dve, 1, ch)
            dve_norm(dve, 4, "rms", w=colw[:, 1:2])
            dve_router(dve, 2, False, ch)
            dve_moe1(dve, 2, ch)
            dve_norm(dve, 5, "fused", w=colp[:, C_L1G:C_L1G + 1], b=colp[:, C_L1B:C_L1B + 1], ch=ch)
            dve_scan(dve, 5, ch)
            dve_norm(dve, 6, "ln2", w=colp[:, C_L2G:C_L2G + 1], b=colp[:, C_L2B:C_L2B + 1], ch=ch)
            dve_ffn(dve, ch)
            dve_norm(dve, 7, "fused", w=colw[:, 0:1])
            dve_attn(dve, 2, ch)
            dve_norm(dve, 8, "rms", w=colw[:, 1:2])
            dve_router(dve, 3, False, ch)
            dve_moe1(dve, 3, ch)
            dve_store(dve)


def shape_constants():
    f = np.float32
    slopes = f(1.0) / np.power(f(2.0 ** 8), (np.arange(H, dtype=f) + f(1)) / f(H), dtype=f)
    pieces, rest = [], slopes.copy()
    for _ in range(SLOPE_PIECES):
        piece = rest.astype(np.float16)
        pieces.append(piece)
        rest = rest - piece.astype(f)
    slope_rows = np.stack([np.repeat(p[:, None], S, 1) for p in pieces])
    kpos = np.broadcast_to((np.arange(S) - S // 2).astype(np.float16), (SLOPE_PIECES, H, S)).copy()
    freqs = f(1.0) / np.power(100000.0, np.arange(0, ROPE, 2) / ROPE).astype(f)
    ang = np.outer(np.arange(S, dtype=f), freqs).astype(f)
    cos, sin = np.cos(ang).astype(f), np.sin(ang).astype(f)
    c32 = np.repeat(cos.T, 2, 0)
    s32 = np.repeat(sin.T, 2, 0)
    s32[0::2] = -s32[0::2]
    return {"slopes": slope_rows, "kpos": kpos, "cosT": np.tile(c32, (4, 1)), "sinT": np.tile(s32, (4, 1))}


def layouts(i):
    g = {k: np.asarray(v) for k, v in i.items()}
    f = np.float32
    d = {"x": g["L0_attn_x"].reshape(T, D)}
    d["Wg0"], d["W_in"], d["W_out"] = g["L0_ffn_Wg"], g["L0_ffn_W_in"], g["L0_ffn_W_out"]
    d["Wqkv0"] = np.stack([g["L0_attn_W_Q"].T, g["L0_attn_W_K"].T, g["L0_attn_W_V"].T])
    wo = np.zeros((NQ, QUAD, 32, D), f)
    wo[:, :, 0:HD0, :] = g["L0_attn_W_O"].T.reshape(NQ, QUAD, HD0, D)
    d["WoPad0"] = wo.reshape(NQ, P, D)
    d["expert_bias"] = g["L1_ffn_expert_bias"].reshape(1, E)
    n = "L1_attn_"
    dw = g[n + "dw_W"].reshape(D, 3)
    d["cols"] = np.stack([g[n + "ln1_g"], g[n + "ln1_b"], g[n + "in_b"][:D], g[n + "in_b"][D:], dw[:, 0], dw[:, 1],
                          dw[:, 2], g[n + "dw_b"], g[n + "dt_b"], g[n + "b_b"], g[n + "c_b"], g[n + "a_log"],
                          g[n + "d_skip"], g[n + "out_b"], g[n + "ln2_g"], g[n + "ln2_b"], g[n + "f1_b"][:D],
                          g[n + "f1_b"][D:], g[n + "f2_b"]], axis=1)
    d["colw"] = np.stack([g["L1_ffn_w_ln1"], g["L1_ffn_w_ln2"]], axis=1)
    for k in ("in_W", "dt_W", "b_W", "c_W", "out_W", "f1_W", "f2_W"):
        d[k] = g[n + k]
    wq = g["L1_ffn_Wq"].reshape(D, H, 64)
    d["w_rope"] = wq[:, :, NOPE:].reshape(D, H * ROPE)
    d["w_swap"] = wq[:, :, NOPE:].reshape(D, H, ROPE // 2, 2)[..., ::-1].reshape(D, H * ROPE)
    kva = g["L1_ffn_Wkva"]
    pad = np.zeros((D, 16), f)
    d["w_kva"] = np.concatenate([kva[:, :LAT], pad, kva[:, LAT:],
                                 kva[:, LAT:].reshape(D, ROPE // 2, 2)[..., ::-1].reshape(D, ROPE)], axis=1)
    d["wqn"] = wq[:, :, :NOPE].transpose(2, 1, 0)
    kb = np.zeros((NOPE, H, 32), f)
    kb[:, :, :LAT] = g["L1_ffn_Wkvb"].reshape(LAT, H, NOPE).transpose(2, 1, 0)
    d["wkb"] = kb
    d["won"] = g["L1_ffn_Wo"].reshape(H, 64, D)[:, :NOPE].transpose(1, 0, 2)
    for k, w, s in (("w_gate1", "Wg", "sWg"), ("w_up1", "Wu", "sWu")):
        d[k] = np.concatenate([g["L1_ffn_" + w].transpose(1, 0, 2).reshape(D, E * I1), g["L1_ffn_" + s][0]], axis=1)
    d["Wd"], d["sWd"], d["Wgate"] = g["L1_ffn_Wd"], g["L1_ffn_sWd"][0], g["L1_ffn_Wgate"]
    d.update(shape_constants())
    return {k: np.ascontiguousarray(v) for k, v in d.items()}


def kernel(**inputs):
    import concourse.bacc as bacc
    from concourse.bass_utils import run_bass_kernel_spmd

    arrays = layouts(inputs)
    nc = bacc.Bacc("TRN2", target_bir_lowering=False, num_devices=1)
    aps = {k: nc.dram_tensor(k, v.shape, mybir.dt.from_np(v.dtype), kind="ExternalInput").ap()
           for k, v in arrays.items()}
    out = nc.dram_tensor("out", (T, D), F32, kind="ExternalOutput").ap()
    build_program(nc, aps, out)
    r = run_bass_kernel_spmd(nc, [arrays], core_ids=[0])
    return r.results[0]["out"].reshape(B, S, D)
```

```python
from contextlib import ExitStack

import numpy as np

import concourse.bass as bass
from concourse import mybir

F32 = mybir.dt.float32
F16 = mybir.dt.float16
BF16 = mybir.dt.bfloat16
ALU = mybir.AluOpType
ACT = mybir.ActivationFunctionType
AX = mybir.AxisListType

P = 128
B, S, D = 2, 1024, 128
T = B * S
TT = 512
NT = T // TT
NTT = T // P
H = 16
QUAD = 4
NQ = H // QUAD
NN = B * NQ
KT = S // P
HD0 = D // H
E = 8
F0 = 256
CAP = -(-2 * T * 5 // (E * 4))
ROPE, NOPE, LAT = 32, 32, 16
I1 = 64
EPS = 1e-5
BIG = 1e30
CROW = 96
STEP = [(kt, heads) for kt in range(KT)
        for heads in ([(j,) for j in range(QUAD)] if kt * P < TT else [(0, 1), (2, 3)])]
STEPS = len(STEP)


def steps_to(kt):
    return sum(1 for t, _ in STEP if t <= kt)


SLOPE_PIECES = 3

UNITS = []
for _qt in range(KT):
    _n = (_qt + 1) * P
    for _c0 in range(0, _n, TT):
        _w = min(TT, _n - _c0)
        _per = max(1, min(QUAD, TT // _w))
        _per = {3: 2}.get(_per, _per)
        for _j in range(0, QUAD, _per):
            UNITS.append((_qt, _c0, _w, tuple(range(_j, _j + _per))))


def halves_of(kt):
    q0 = kt * P
    return [(lo, hi) for lo, hi in ((q0, TT), (max(q0, TT), S)) if lo < hi]


WORK = []
for _s in range(STEPS):
    WORK.append(("scores", _s, None))
    _kt = STEP[_s][0]
    if _kt and _s == steps_to(_kt - 1) + 1:
        WORK += [("pv", _kt - 1, piece) for piece in halves_of(_kt - 1)]
WORK += [("pv", KT - 1, piece) for piece in halves_of(KT - 1)]


def ring_plan(tail, ahead, build, terms=2):
    pe_cost = {"den": 0.9, "spread": 0.9, "proj": 0.9, "rope": 0.9, "swap": 0.9, "lat": 0.9, "unit": 0.3, "turn": 0.1}
    dve_cost = {"den": 1.0, "spread": 0.65, "proj": 0.65, "rope": 0.65, "swap": 0.65, "lat": 1.3, "unit": 0.66,
                "turn": 0.3}
    own = []
    if tail:
        own += [(2.0, "den", 0)] + [(0, "spread", h) for h in range(2)] + [(0, "proj", h) for h in range(2)]
    if build:
        own += [(8.0, kind, h) for h in range(2) for kind in ("rope", "swap", "lat")]
    units = [("unit", u) for u in UNITS] if ahead else []
    plan, t, exp_end, dve, bank_free = [], 0.0, [0.0, 0.0], 1.5 if tail else 0.0, [0.0, 0.0]
    since = 0
    for place, (what, s, piece) in enumerate(WORK):
        if what == "scores":
            cols = (S - STEP[s][0] * P) * len(STEP[s][1])
            t = max(t, exp_end[-2] + 0.1) + 0.1 + terms * cols * 0.00042
            exp_end.append(max(exp_end[-1], t + 0.2) + 0.2 + cols * 0.0007)
        else:
            t += QUAD * (piece[1] - piece[0]) * 0.00085
        while (own or units) and bank_free[len(plan) % 2] <= t:
            if own and own[0][0] <= t and (not units or since >= 1 or own[0][1] in ("den", "spread", "proj")):
                _, kind, arg = own.pop(0)
                since = 0
            elif units:
                kind, arg = units.pop(0)
                since += 1
            else:
                break
            l = len(plan)
            plan.append((place, kind, arg))
            t += pe_cost[kind]
            dve = max(dve, t + 0.15) + dve_cost[kind]
            bank_free[l % 2] = dve + 0.1
    last = len(WORK) - 1
    plan += [(last, kind, arg) for _, kind, arg in own] + [(last, kind, arg) for kind, arg in units]
    if ahead:
        plan.append((max(TURN, plan[-1][0]), "turn", 0))
    return plan


TURN = WORK.index(("scores", STEPS - 4, None))


def build_program(nc, a, out):
    with ExitStack() as ctx:
        def sb(name, shape, dt=F32):
            return ctx.enter_context(nc.sbuf_tensor(name, shape, dt))

        def sem(name):
            return ctx.enter_context(nc.semaphore(name))

        XT = sb("XT", [P, T])
        XN = sb("XN", [P, T])
        YA = sb("YA", [P, T])
        QS = sb("QS", [P, H, S], F16)
        KS = sb("KS", [P, H, S], F16)
        PR = sb("PR", [P, 2, QUAD, S])
        VS = sb("VS", [P, KT, QUAD, 32])
        OS = sb("OS", [P, S])
        ON = sb("ON", [P, S])
        RD = sb("RD", [P, KT * QUAD])
        RX = sb("RX", [P, S])
        HL = sb("HL", [P, 4, T], F16)
        WM = sb("WM", [P, 6144])
        QSf = QS[:, :, :].rearrange("p h s -> p (h s)").bitcast(F32)
        KSf = KS[:, :, :].rearrange("p h s -> p (h s)").bitcast(F32)
        PRf = PR[:, :, :, :].rearrange("p a j s -> p (a j s)")

        HLw = HL[:, :, :].rearrange("p a t -> p (a t)").bitcast(F32)
        w_in = WM[:, 0:4096].rearrange("p (e f) -> p e f", e=E)
        w_out = WM[:, 4096:6144].rearrange("p (e c o) -> p e c o", e=E, c=2)
        at = [0]

        def wm(n):
            at[0] += n
            assert at[0] <= 6144
            return WM[:, at[0] - n:at[0]]

        cosT, sinT = wm(S), wm(S)
        w_rope = wm(512).rearrange("p (g m) -> p g m", g=NQ)
        w_swap = wm(512).rearrange("p (g m) -> p g m", g=NQ)
        w_kva = wm(96)
        w_gate1 = wm(9 * I1)
        w_up1 = wm(9 * I1)
        w_down1 = wm(5 * P).rearrange("p (g o) -> p g o", g=5)
        w_rt1 = wm(E)
        wo0 = sb("wo0", [P, NQ, P])
        wo1 = sb("wo1", [P, NQ, P])
        w_lat = sb("w_lat", [P, NQ, P])
        wq0 = sb("wq0", [P, 3, P])
        w_rt0 = sb("w_rt0", [P, E])
        brow = sb("brow", [1, E])
        ones1 = sb("ones1", [1, P])
        colp = sb("colp", [P, 20])
        stage = sb("stage", [P, 4, P])
        wqn = HLw[0:32, 0:2048].rearrange("p (h m) -> p h m", h=H)
        wkb = HLw[0:32, 2048:2560].rearrange("p (h m) -> p h m", h=H)
        won = [x[0:32, :].rearrange("p (h m) -> p h m", h=H // 2) for x in (OS, ON)]

        mean_w = sb("mean_w", [P, P])
        identf = sb("identf", [P, P])
        identb = sb("identb", [P, P], BF16)
        maskqk = sb("maskqk", [P, P], BF16)
        maskkq = sb("maskkq", [P, P], BF16)
        lessall = sb("lessall", [P, P], BF16)
        goon = sb("goon", [P, 256])
        onesb = sb("onesb", [P, P], BF16)
        sel0 = sb("sel0", [P, P])
        sel1 = sb("sel1", [P, P])
        desc = sb("desc", [P, E])
        epsc = sb("epsc", [P, 4])
        BM = sb("BM", [P, 2, QUAD, KT])
        M4 = sb("M4", [P, QUAD * KT])
        CT = sb("CT", [QUAD * KT, P], F16)
        rt = PRf[:, 5120:7680].rearrange("p (n c) -> p n c", n=10)
        ohb = sb("ohb", [P, 256], BF16)
        gT = sb("gT", [P, P])

        def pr_part(o, n):
            return PRf[:, o:o + n]

        NSQ = pr_part(0, 2048).rearrange("p (a t) -> p a t", a=NT)
        NRS = pr_part(2048, 4096).rearrange("p (a b t) -> p a b t", a=NT, b=2)
        GB = pr_part(0, 8192).rearrange("p (a e t) -> p a e t", a=2, e=E)
        GE0 = HLw[:, 0:1536].rearrange("p (a t) -> p a t", a=3)
        HF = HLw[:, 1536:2560].rearrange("p (a t) -> p a t", a=2)
        HH = HLw[:, 2560:3328].bitcast(F16).rearrange("p (a t) -> p a t", a=3)
        HQ = HLw[:, 3328:4096].bitcast(F16).rearrange("p (a t) -> p a t", a=3)
        XH, XL = (YA[:, :].bitcast(F16)[:, i * T:(i + 1) * T] for i in range(2))
        QSh = QS[:, :, :].rearrange("p h s -> p (h s)")
        WIH, WIL = (QSh[:, i * 4096:(i + 1) * 4096].rearrange("p (e f) -> p e f", e=E) for i in range(2))
        WOH, WOL = (QSh[:, 8192 + i * 2048:10240 + i * 2048].rearrange("p (e c o) -> p e c o", e=E, c=2)
                    for i in range(2))
        GE = HLw[:, 0:1024].rearrange("p (a t) -> p a t", a=2)
        HID = HLw[:, 1024:2560].rearrange("p (a t) -> p a t", a=3)
        HGL = HLw[:, 2560:4096].rearrange("p (a t) -> p a t", a=3)
        KH, KL = OS[:, :].bitcast(F16), ON[:, :].bitcast(F16)
        V0 = YA[:, :].rearrange("p (i c) -> p i c", i=NTT)
        VL = sb("VL", [P, NTT, LAT])
        BT = sb("BT", [P, 4, TT])
        XP = QSf[:, 0:2 * (S + 2)].rearrange("p (b s) -> p b s", b=B)
        MX = QSf[:, 2560:2560 + T]
        SG = QSf[:, 5120:5120 + T]
        DTm = KSf[:, 0:T]
        BTm = KSf[:, T:2 * T]
        CTm = KSf[:, 2 * T:3 * T]
        DEC = KSf[:, 3 * T:4 * T]
        ST_ = pr_part(5120, T)
        TMP = BT[:, :, :]
        F1 = QSf[:, 0:2048].rearrange("p (a c t) -> p a c t", a=2, c=2)
        w_inp = sb("w_inp", [P, 2, P])
        w_dbc = sb("w_dbc", [P, 3, P])
        w_outp = sb("w_outp", [P, P])
        w_f1 = sb("w_f1", [P, 2, P])
        w_f2 = sb("w_f2", [P, 2, P])

        ps = [ctx.enter_context(nc.psum_tensor(f"ps{i}", [P, 2, TT], F32)) for i in range(4)]

        def bank(i):
            return ps[i // 2][:, i % 2, :]

        RING = (4, 5)
        OUTP = ps[3]

        gate_d = nc.dram_tensor("gates", (4, E, T), F32, kind="Internal").ap()
        parts_d = nc.dram_tensor("parts", (B, 4, P, S), F16, kind="Internal").ap()

        s_x0 = sem("s_x0")
        s_w = sem("s_w")
        s_wm = sem("s_wm")
        s_wl = sem("s_wl")
        s_const = sem("s_const")
        s_ld = sem("s_ld")
        s_comp = sem("s_comp")
        s_compd = sem("s_compd")
        s_xup = sem("s_xup")
        s_mean, s_xc, s_sq, s_var = sem("s_mean"), sem("s_xc"), sem("s_sq"), sem("s_var")
        s_rs, s_xn, s_lg, s_va = sem("s_rs"), sem("s_xn"), sem("s_lg"), sem("s_va")
        s_rpe, s_rdv, s_rac = sem("s_rpe"), sem("s_rdv"), sem("s_rac")
        s_gw = sem("s_gw")
        s_xh, s_xl = sem("s_xh"), sem("s_xl")
        s_wh, s_wlo = sem("s_wh"), sem("s_wlo")
        s_gg = sem("s_gg")
        s_hf = sem("s_hf")
        s_hh = sem("s_hh")
        s_gb = [sem(f"s_gb{g}") for g in range(4)]
        s_ag, s_ge, s_hid, s_out = sem("s_ag"), sem("s_ge"), sem("s_hid"), sem("s_out")
        s_hg = sem("s_hg")
        s_zero = sem("s_zero")
        s_cdma = sem("s_cdma")
        s_stk = sem("s_stk")
        s_crow = sem("s_crow")
        s_st = sem("s_st")
        s_exp = sem("s_exp")
        s_pv = sem("s_pv")
        s_rr = sem("s_rr")
        s_rd = sem("s_rd")
        s_m4 = sem("s_m4")
        s_vs = sem("s_vs")
        s_wst = sem("s_wst")
        s_den = sem("s_den")
        s_wos = sem("s_wos")
        s_os = sem("s_os")
        s_kb = sem("s_kb")
        s_bnc = sem("s_bnc")
        s_wc = sem("s_wc")
        s_lat = sem("s_lat")
        s_sp, s_sa, s_sd, s_so = sem("s_sp"), sem("s_sa"), sem("s_sd"), sem("s_so")
        s_fin, s_store = sem("s_fin"), sem("s_store")
        s_dve = sem("s_dve")
        s_act = sem("s_act")
        s_pool = sem("s_pool")

        class Chain:

            def __init__(self, eng, s):
                self.eng, self.s, self.n = eng, s, 0

            def up(self, ins):
                ins.then_inc(self.s, 1)
                self.n = self.n + 1

            def wait(self):
                self.eng.wait_ge(self.s, self.n)

            def link(self, ins):
                self.up(ins)
                self.wait()

        (C_L1G, C_L1B, C_INB0, C_INB1, C_DW0, C_DW1, C_DW2, C_DWB, C_DTB, C_BB, C_CB, C_A, C_DSK,
         C_OB, C_L2G, C_L2B, C_F1B0, C_F1B1, C_F2B, C_NA) = range(20)
        colw = sb("colw_sb", [P, 4])

        def tsl(t, n=TT):
            return bass.ds(t * n, n)

        def sp_load(sp):
            sp.dma_start(PRf[:, 0:T].rearrange("p (i d) -> p i d", i=NTT),
                         a["x"].rearrange("(i p) d -> p i d", p=P)).then_inc(s_x0, 16)
            loads = [
                (w_rt0[:, :], a["Wg0"]), (wq0[:, :, :], a["Wqkv0"].rearrange("n p m -> p n m")),
                (wo0[:, :, :], a["WoPad0"].rearrange("g p m -> p g m")),
                (brow[:, :], a["expert_bias"]), (colp[:, 0:19], a["cols"]), (colw[:, 0:2], a["colw"]),
                (w_inp[:, :, :], a["in_W"].rearrange("p (c m) -> p c m", c=2)),
                (w_dbc[:, 0, :], a["dt_W"]), (w_dbc[:, 1, :], a["b_W"]), (w_dbc[:, 2, :], a["c_W"]),
                (w_outp[:, :], a["out_W"]),
                (w_f1[:, :, :], a["f1_W"].rearrange("p (c m) -> p c m", c=2)),
                (w_f2[:, :, :], a["f2_W"].rearrange("(c p) m -> p c m", p=P)),
            ]
            for dst, src in loads:
                sp.dma_start(dst, src).then_inc(s_w, 16)
            load_moe_weights(sp)

            for dst, src in ((wqn, a["wqn"]), (wkb, a["wkb"]), (won[0], a["won"][:, 0:H // 2]),
                             (won[1], a["won"][:, H // 2:H])):
                sp.dma_start(dst, src).then_inc(s_wc, 16)

        N_WFIRST = 16 * 13

        def load_moe_weights(sp):
            sp.dma_start(w_in, a["W_in"].rearrange("e p f -> p e f")).then_inc(s_wm, 16)
            sp.dma_start(w_out, a["W_out"].rearrange("e (c p) o -> p e c o", p=P)).then_inc(s_wm, 16)

        N_CONST = 13

        def pool_const(pool):
            ch = Chain(pool, s_pool)
            for m in (identf, sel0, sel1):
                ch.up(pool.memset(m[:, :], 0.0))
            for m in (identb, maskqk, maskkq):
                ch.up(pool.memset(m[:, :], 0.0))
            ch.up(pool.memset(lessall[:, :], -1.0))
            ch.up(pool.memset(goon[:, :], 1.0))
            ch.wait()
            for m in (identf, identb):
                pool.affine_select(out=m[:, :], in_=m[:, :], compare_op=ALU.not_equal, fill=1.0, base=0,
                                   pattern=[[-1, P]], channel_multiplier=1).then_inc(s_const, 1)
            pool.affine_select(out=maskqk[:, :], in_=maskqk[:, :], compare_op=ALU.is_ge, fill=-BIG, base=0,
                               pattern=[[-1, P]], channel_multiplier=1).then_inc(s_const, 1)
            pool.affine_select(out=maskkq[:, :], in_=maskkq[:, :], compare_op=ALU.is_ge, fill=-BIG, base=0,
                               pattern=[[1, P]], channel_multiplier=-1).then_inc(s_const, 1)
            pool.affine_select(out=lessall[:, :], in_=lessall[:, :], compare_op=ALU.is_ge, fill=0.0, base=0,
                               pattern=[[-1, P]], channel_multiplier=1).then_inc(s_const, 1)
            pool.memset(goon[:, :].rearrange("p (e b) -> p e b", e=E)[:, :, 0:1], 0.0).then_inc(s_const, 1)
            for m, r in ((sel0, HD0), (sel1, LAT)):
                pool.affine_select(out=m[:, :].rearrange("p (j c) -> p j c", j=QUAD),
                                   in_=m[:, :].rearrange("p (j c) -> p j c", j=QUAD),
                                   compare_op=ALU.not_equal, fill=1.0, base=-r,
                                   pattern=[[-32, QUAD], [0, 32]], channel_multiplier=1).then_inc(s_const, 1)
            pool.memset(onesb[:, :], 1.0).then_inc(s_const, 1)
            pool.memset(mean_w[:, :], 1.0 / D).then_inc(s_const, 1)
            pool.memset(ones1[:, :], 1.0).then_inc(s_const, 1)
            pool.memset(BM[:, :, :, :], -3e38).then_inc(s_const, 1)
            for e in range(E):
                ins = pool.memset(desc[:, e:e + 1], float(E - e))
            pool.memset(epsc[:, 0:1], EPS)
            ins = pool.memset(epsc[:, 1:2], EPS * EPS)
            ins.then_inc(s_const, 1)

        def pe_load(pe):
            pe.wait_ge(s_const, N_CONST)
            pe.wait_ge(s_x0, 16)
            for i in range(NTT):
                ins = pe.transpose(bank(i // 4)[:, (i % 4) * P:(i % 4 + 1) * P],
                                   PRf[:, i * P:(i + 1) * P], identf[:, :])
                if i % 4 == 3:
                    ins.then_inc(s_ld, 1)

        def dve_load(dve):
            for t in range(NT):
                dve.wait_ge(s_ld, t + 1)
                dve.tensor_copy(XT[:, t * TT:(t + 1) * TT], bank(t)).then_inc(s_xup, 1)

        def norm_src(mode):
            return YA if mode in ("rms", "ln2") else XT

        def pe_norm(pe, k, mode, ready):
            src = norm_src(mode)
            pe.wait_ge(*ready)
            for t in range(NT):
                pe.matmul(bank(t), mean_w[:, :], src[:, tsl(t)], start=True, stop=True).then_inc(s_mean, 1)
            for t in range(NT):
                pe.wait_ge(s_sq, 4 * k + t + 1)
                pe.matmul(bank(4 + t), mean_w[:, :], NSQ[:, t, :], start=True, stop=True).then_inc(s_var, 1)

        def dve_norm(dve, k, mode, w=None, b=None, ch=None, prev=None):
            src = norm_src(mode)

            def center(t):
                dve.wait_ge(s_mean, 4 * k + t + 1)
                if mode == "rms":
                    dve.tensor_copy(XN[:, tsl(t)], src[:, tsl(t)]).then_inc(s_xc, 1)
                else:
                    dve.tensor_tensor(XN[:, tsl(t)], src[:, tsl(t)], bank(t), ALU.subtract).then_inc(s_xc, 1)

            def scale(t):
                dve.wait_ge(s_rs, 4 * k + t + 1)
                r1, r2 = NRS[:, t, 0, :], NRS[:, t, 1, :]
                if mode == "fused":
                    dve.tensor_tensor(YA[:, tsl(t)], XN[:, tsl(t)], r1, ALU.mult)
                r = r2 if mode == "fused" else r1
                if w is None:
                    dve.tensor_tensor(XN[:, tsl(t)], XN[:, tsl(t)], r, ALU.mult).then_inc(s_xn, 1)
                elif b is None:
                    dve.scalar_tensor_tensor(out=XN[:, tsl(t)], in0=XN[:, tsl(t)], scalar=w, in1=r,
                                             op0=ALU.mult, op1=ALU.mult).then_inc(s_xn, 1)
                else:
                    ch.link(dve.scalar_tensor_tensor(out=XN[:, tsl(t)], in0=XN[:, tsl(t)], scalar=w, in1=r,
                                                     op0=ALU.mult, op1=ALU.mult))
                    dve.tensor_scalar(XN[:, tsl(t)], XN[:, tsl(t)], b, None, ALU.add).then_inc(s_xn, 1)

            for t in range(NT):
                center(t)
            for t in range(NT):
                scale(t)

        def act_norm(act, k, mode, ch):
            n = 2 if mode == "fused" else 1
            for t in range(NT):
                act.wait_ge(s_xc, 4 * k + t + 1)
                act.activation(NSQ[:, t, :], XN[:, tsl(t)], ACT.Square).then_inc(s_sq, 1)
            for t in range(NT):
                act.wait_ge(s_var, 4 * k + t + 1)
                v = bank(4 + t)
                if n == 2:
                    ch.up(act.activation(NRS[:, t, 1, :], v, ACT.Ln, bias=epsc[:, 1:2], scale=1.0 + EPS))
                act.activation(NRS[:, t, 0, :], v, ACT.Ln, bias=epsc[:, 0:1]).then_inc(s_va, 1)
            for t in range(NT):
                act.wait_ge(s_va, 4 * k + t + 1)
                if n == 2:
                    ch.wait()
                act.activation(NRS[:, t, 0:n, :], NRS[:, t, 0:n, :], ACT.Exp, scale=-0.5).then_inc(s_rs, 1)

        def pe_router(pe, r, kn, w, bias, cap):
            for i in range(NTT):
                if i % 4 == 0:
                    pe.wait_ge(s_xn, 4 * kn + i // 4 + 1)
                o = bank(0)[:, i * E:(i + 1) * E]
                ins = pe.matmul(o, XN[:, i * P:(i + 1) * P], w, start=True, stop=not bias)
                if bias:
                    ins = pe.matmul(o, ones1[0:1, :], brow[0:1, :], start=False, stop=True)
            ins.then_inc(s_rpe, 1)
            if cap:
                pe.wait_ge(s_rdv, 3 * r + 2)
                pe.matmul(bank(1)[:, 0:256], lessall[:, :], ohb[:, :], start=True, stop=True)
                pe.matmul(bank(2)[:, 0:256], onesb[:, :], ohb[:, :], start=True, stop=True).then_inc(s_rpe, 1)
            pe.wait_ge(s_rdv, 3 * r + 3)
            ins = pe.transpose(bank(3)[:, 0:P], rt[:, 0, 0:P], identf[:, :])
            ins.then_inc(s_rpe, 1 if cap else 2)

        def act_router(act, r):
            act.wait_ge(s_rdv, 3 * r + 1)
            act.activation(rt[:, 1, 0:P], rt[:, 0, 0:P], ACT.Exp).then_inc(s_rac, 1)

        def dve_router(dve, r, cap, ch):
            def v3(i, o=0):
                return rt[:, i, o:o + P].rearrange("p (i e) -> p i e", e=E)

            def over_e(x):
                return x.unsqueeze(2).to_broadcast([P, NTT, E])

            m = [rt[:, 9, 16 * q:16 * q + 16] for q in range(8)]
            first = desc[:, :].unsqueeze(1).to_broadcast([P, NTT, E])
            dve.wait_ge(s_rpe, 3 * r + 1)
            lg = bank(0)[:, 0:P].rearrange("p (i e) -> p i e", e=E)
            ch.link(dve.tensor_reduce(m[0], lg, AX.X, ALU.max))
            dve.tensor_tensor(v3(0), lg, over_e(m[0]), ALU.subtract).then_inc(s_rdv, 1)
            dve.wait_ge(s_rdv, 3 * r + 1)
            ch.link(dve.scalar_tensor_tensor(out=v3(3), in0=v3(0), scalar=0.0, in1=first,
                                             op0=ALU.is_equal, op1=ALU.mult))
            ch.link(dve.tensor_reduce(m[4], v3(3), AX.X, ALU.max))
            ch.link(dve.tensor_tensor(v3(4, 0), v3(3), over_e(m[4]), ALU.is_equal))
            ch.link(dve.scalar_tensor_tensor(out=v3(5), in0=v3(4, 0), scalar=-BIG, in1=v3(0),
                                             op0=ALU.mult, op1=ALU.add))
            ch.link(dve.tensor_reduce(m[3], v3(5), AX.X, ALU.max))
            ch.link(dve.tensor_tensor(v3(3), v3(5), over_e(m[3]), ALU.is_equal))
            ch.link(dve.tensor_tensor(v3(3), v3(3), first, ALU.mult))
            ch.link(dve.tensor_reduce(m[4], v3(3), AX.X, ALU.max))
            ch.link(dve.tensor_tensor(v3(4, P), v3(3), over_e(m[4]), ALU.is_equal))
            oh = rt[:, 4, :]
            if cap:
                def by_e(x):
                    return x.rearrange("p (b e) -> p e b", e=E)

                def eb(x):
                    return x.rearrange("p (e b) -> p e b", e=E)

                dve.tensor_copy(eb(ohb[:, :]), by_e(oh)).then_inc(s_rdv, 1)
                dve.wait_ge(s_rac, r + 1)
                ch.up(dve.tensor_reduce(m[1], v3(1), AX.X, ALU.add))
                dve.wait_ge(s_rpe, 3 * r + 2)
                ch.link(dve.tensor_tensor_scan(rt[:, 6, :], goon[:, :], bank(2)[:, 0:256], 0.0, ALU.mult, ALU.add))
                ch.link(dve.tensor_tensor(rt[:, 7, :], rt[:, 6, :], bank(1)[:, 0:256], ALU.add))
                ch.link(dve.scalar_tensor_tensor(out=by_e(rt[:, 8, :]), in0=eb(rt[:, 7, :]), scalar=float(CAP),
                                                 in1=by_e(oh), op0=ALU.is_lt, op1=ALU.mult))
                kept = rt[:, 8, :]
            else:
                dve.memset(ohb[:, 0:8], 0.0).then_inc(s_rdv, 1)
                dve.wait_ge(s_rac, r + 1)
                kept = oh
            ch.link(dve.tensor_tensor(rt[:, 5, 0:P], kept[:, 0:P], kept[:, P:256], ALU.add))
            ch.link(dve.tensor_tensor(v3(5), v3(5), v3(1), ALU.mult))
            ch.link(dve.tensor_reduce(m[5], v3(5), AX.X, ALU.add))
            if cap:
                ch.link(dve.scalar_tensor_tensor(out=m[5], in0=m[1], scalar=1e-9, in1=m[5],
                                                 op0=ALU.mult, op1=ALU.max))
            ch.link(dve.reciprocal(m[6], m[5]))
            dve.tensor_tensor(rt[:, 0, 0:P].rearrange("p (e i) -> p i e", e=E), v3(5), over_e(m[6]),
                              ALU.mult).then_inc(s_rdv, 1)
            dve.wait_ge(s_rpe, 3 * r + 3)
            dve.tensor_copy(gT[:, :], bank(3)[:, 0:P]).then_inc(s_hg, 1)

        def sp_gates(sp, r, halves):
            sp.wait_ge(s_hg, r + 1)
            sp.dma_start(gate_d[r].rearrange("e (i t) -> (e i) t", t=P), gT[:, :]).then_inc(s_gw, 16)
            sp.wait_ge(s_gw, 16 * (r + 1))
            for t in range(NT):
                if t >= 2:
                    sp.wait_ge(s_hid if halves else s_gg, ag_base(r) + (t - 1) * (ST1 if halves else ST0))
                for g in range(4):
                    if halves:
                        for h in range(2):
                            src = gate_d[r, 2 * g + h:2 * g + h + 1, t * TT:(t + 1) * TT]
                            sp.dma_start(GB[64 * h:64 * h + 64, t % 2, g, :],
                                         src.to_broadcast([64, TT])).then_inc(s_gb[g], 16)
                    else:
                        src = gate_d[r, 2 * g:2 * g + 2, t * TT:(t + 1) * TT].unsqueeze(0)
                        sp.dma_start(GB[:, t % 2, 2 * g:2 * g + 2, :],
                                     src.to_broadcast([P, 2, TT])).then_inc(s_gb[g], 32)
                for g in range(4):
                    sp.wait_ge(s_gb[g], 32 * (4 * r + t + 1))

        ST0 = 2 * E
        ST1 = 5

        def ag_base(r):
            return (0, NT * ST0, 2 * NT * ST0, 2 * NT * ST0 + NT * ST1)[r]

        def pairbank(u, g):
            return bank(2 + 2 * (u % 3) + g)

        W_UP, H_UP = 2.0 ** 8, 2.0 ** 4
        LAG = 3

        def pool_moe0(pool, r):
            base = ag_base(r)
            for u in range(NT * ST0):
                t, e = u // ST0, u % ST0 // 2
                if u % 4 == 0 and e % 2 == 0:
                    pool.wait_ge(s_gb[e // 2], 32 * (4 * r + t + 1))
                pool.wait_ge(s_ge, base + u + 1)
                pool.tensor_tensor(GE0[:, u % 3, :], GE0[:, u % 3, :], GB[:, t % 2, e, :], ALU.mult).then_inc(s_gg, 1)

        def pe_moe0(pe, r):
            base = ag_base(r)

            def three(dst, wh, wl, xh, xl, start, stop):
                pe.matmul(dst, wh, xh, start=start, stop=False)
                pe.matmul(dst, wl, xh, start=False, stop=False)
                return pe.matmul(dst, wh, xl, start=False, stop=stop)

            def out_mm(v):
                t, e, c = v // ST0, v % ST0 // 2, v % 2
                pe.wait_ge(s_hid, base + v + 1)
                if e == 0 and c == 0 and t >= 2:
                    pe.wait_ge(s_xup, xup_base["moe", r] + t - 1)
                three(bank(t % 2), WOH[:, e, c, :], WOL[:, e, c, :], HH[:, v % 3, :], HQ[:, v % 3, :],
                      v % ST0 == 0, v % ST0 == ST0 - 1).then_inc(s_out, 1)

            pe.wait_ge(s_rdv, 3 * (r + 1))
            for u in range(NT * ST0):
                t, e, c = u // ST0, u % ST0 // 2, u % 2
                if u % ST0 == 0:
                    pe.wait_ge(s_xl, 4 * r + t + 1)
                if t == 0 and c == 0:
                    pe.wait_ge(s_wlo, E * r + e + 1)
                if u >= 3:
                    pe.wait_ge(s_hf, base + u - 2)
                elif u == 0:
                    pe.wait_ge(s_hg, r + 1)
                for g in range(2):
                    fs = slice(g * F0 + c * P, g * F0 + (c + 1) * P)
                    ins = three(pairbank(u, g), WIH[:, e, fs], WIL[:, e, fs], XH[:, tsl(t)], XL[:, tsl(t)], True, True)
                ins.then_inc(s_ag, 1)
                if u >= LAG:
                    out_mm(u - LAG)
            for v in range(NT * ST0 - LAG, NT * ST0):
                out_mm(v)

        def act_moe0(act, r):
            base = ag_base(r)

            def weights(e):
                act.activation(WIH[:, e, :], w_in[:, e, :], ACT.Copy, scale=W_UP)
                act.activation(WOH[:, e, :, :], w_out[:, e, :, :], ACT.Copy, scale=W_UP).then_inc(s_wh, 1)

            def inputs(t):
                act.copy(XH[:, tsl(t)], XN[:, tsl(t)]).then_inc(s_xh, 1)

            def high(v):
                act.wait_ge(s_hf, base + v + 1)
                if v >= 3:
                    act.wait_ge(s_out, base + v - 2)
                act.copy(HH[:, v % 3, :], HF[:, v % 2, :]).then_inc(s_hh, 1)

            act.wait_ge(s_wm, 32)
            inputs(0)
            weights(0)
            weights(1)
            for u in range(NT * ST0):
                t, e, c = u // ST0, u % ST0 // 2, u % 2
                act.wait_ge(s_ag, base + u + 1)
                if u >= 3:
                    act.wait_ge(s_hf, base + u - 2)
                act.activation(GE0[:, u % 3, :], pairbank(u, 0), ACT.Gelu, scale=1.0 / W_UP).then_inc(s_ge, 1)
                if u:
                    high(u - 1)
                if t == 0 and c == 0 and e + 2 < E:
                    weights(e + 2)
                if u % ST0 == 6 and t + 1 < NT:
                    inputs(t + 1)
            high(NT * ST0 - 1)

        def dve_moe0(dve, r):
            base = ag_base(r)

            def weights(e):
                dve.wait_ge(s_wh, E * r + e + 1)
                dve.scalar_tensor_tensor(out=WIL[:, e, :], in0=w_in[:, e, :], scalar=W_UP, in1=WIH[:, e, :],
                                         op0=ALU.mult, op1=ALU.subtract)
                dve.scalar_tensor_tensor(out=WOL[:, e, :, :], in0=w_out[:, e, :, :], scalar=W_UP,
                                         in1=WOH[:, e, :, :], op0=ALU.mult, op1=ALU.subtract).then_inc(s_wlo, 1)

            def inputs(t):
                dve.wait_ge(s_xh, 4 * r + t + 1)
                dve.tensor_tensor(XL[:, tsl(t)], XN[:, tsl(t)], XH[:, tsl(t)], ALU.subtract).then_inc(s_xl, 1)

            def low(v):
                dve.wait_ge(s_hh, base + v + 1)
                if v >= 3:
                    dve.wait_ge(s_out, base + v - 2)
                dve.tensor_tensor(HQ[:, v % 3, :], HF[:, v % 2, :], HH[:, v % 3, :], ALU.subtract).then_inc(s_hid, 1)

            def update(t):
                dve.wait_ge(s_out, base + (t + 1) * ST0)
                dve.scalar_tensor_tensor(out=XT[:, tsl(t)], in0=bank(t % 2), scalar=0.5 / (W_UP * H_UP),
                                         in1=XT[:, tsl(t)], op0=ALU.mult, op1=ALU.add).then_inc(s_xup, 1)

            dve.wait_ge(s_wm, 32)
            inputs(0)
            weights(0)
            weights(1)
            for u in range(NT * ST0):
                t, e, c = u // ST0, u % ST0 // 2, u % 2
                dve.wait_ge(s_gg, base + u + 1)
                if u >= 2:
                    dve.wait_ge(s_hid, base + u - 1)
                dve.scalar_tensor_tensor(out=HF[:, u % 2, :], in0=pairbank(u, 1), scalar=H_UP / W_UP,
                                         in1=GE0[:, u % 3, :], op0=ALU.mult, op1=ALU.mult).then_inc(s_hf, 1)
                if u:
                    low(u - 1)
                if t == 0 and c == 0 and e + 2 < E:
                    weights(e + 2)
                if u % ST0 == 6 and t + 1 < NT:
                    inputs(t + 1)
                if u % ST0 == 4 and t:
                    update(t - 1)
            low(NT * ST0 - 1)
            update(NT - 1)

        def rows1(g):
            return P if g < 4 else I1

        def pe_moe1(pe, r):
            pe.wait_ge(s_hg, r + 1)
            base = ag_base(r)

            def out_mm(v):
                t, g = v // ST1, v % ST1
                pe.wait_ge(s_hid, base + v + 1)
                if g == 0 and t >= 2:
                    pe.wait_ge(s_xup, xup_base["moe", r] + t - 1)
                pe.matmul(bank(t % 2), w_down1[0:rows1(g), g, :], HID[0:rows1(g), v % 3, :], start=(g == 0),
                          stop=(g == ST1 - 1)).then_inc(s_out, 1)

            for u in range(NT * ST1):
                t, g = u // ST1, u % ST1
                if u >= 3:
                    pe.wait_ge(s_hid, base + u - 2)
                n = rows1(g)
                pe.matmul(pairbank(u, 0)[0:n, :], w_gate1[:, g * P:g * P + n], XN[:, tsl(t)], start=True, stop=True)
                pe.matmul(pairbank(u, 1)[0:n, :], w_up1[:, g * P:g * P + n], XN[:, tsl(t)], start=True,
                          stop=True).then_inc(s_ag, 1)
                if u >= 2:
                    out_mm(u - 2)
            out_mm(NT * ST1 - 2)
            out_mm(NT * ST1 - 1)

        def act_moe1(act, r):
            base = ag_base(r)
            for u in range(NT * ST1):
                n = rows1(u % ST1)
                act.wait_ge(s_ag, base + u + 1)
                if u >= 2:
                    act.wait_ge(s_hgl, hgl_base(r) + u - 1)
                act.activation(GE[0:n, u % 2, :], pairbank(u, 0)[0:n, :], ACT.Silu).then_inc(s_ge, 1)

        s_hgl = sem("s_hgl")

        def hgl_base(r):
            return (r - 2) * NT * ST1

        def dve_moe1(dve, r, ch):
            base = ag_base(r)

            def update(t):
                dve.wait_ge(s_out, base + (t + 1) * ST1)
                ch.link(dve.tensor_tensor(YA[:, tsl(t)], YA[:, tsl(t)], bank(t % 2), ALU.add))
                dve.scalar_tensor_tensor(out=XT[:, tsl(t)], in0=YA[:, tsl(t)], scalar=0.5, in1=XT[:, tsl(t)],
                                         op0=ALU.mult, op1=ALU.add).then_inc(s_xup, 1)

            for u in range(NT * ST1):
                n = rows1(u % ST1)
                dve.wait_ge(s_ge, base + u + 1)
                if u >= 3:
                    dve.wait_ge(s_hid, base + u - 2)
                dve.tensor_tensor(HGL[0:n, u % 3, :], GE[0:n, u % 2, :], pairbank(u, 1)[0:n, :],
                                  ALU.mult).then_inc(s_hgl, 1)
                if u % ST1 == 3 and u > ST1:
                    update(u // ST1 - 1)
            update(NT - 1)

        def pool_moe1(pool, r):
            base = ag_base(r)
            for u in range(NT * ST1):
                t, g = u // ST1, u % ST1
                n = rows1(g)
                if g < 4:
                    pool.wait_ge(s_gb[g], 32 * (4 * r + t + 1))
                pool.wait_ge(s_hgl, hgl_base(r) + u + 1)
                if u >= 3:
                    pool.wait_ge(s_out, base + u - 2)
                if g < 4:
                    pool.tensor_tensor(HID[:, u % 3, :], HGL[:, u % 3, :], GB[:, t % 2, g, :],
                                       ALU.mult).then_inc(s_hid, 1)
                else:
                    pool.tensor_copy(HID[0:n, u % 3, :], HGL[0:n, u % 3, :]).then_inc(s_hid, 1)

        def iterations(latent):
            if latent:
                return [(0, 1, False, True, True), (1, NN - 2, True, True, True),
                        (NN - 2, NN - 1, True, True, False), (NN - 1, NN, True, False, False)]
            return [(0, 1, False, True, False), (1, NN - 1, True, True, False), (NN - 1, NN, True, False, False)]

        def quad_builds(m):
            return [(kind, m, h) for h in range(2) for kind in ("rope", "swap", "lat")]

        PROLOGUE = ([("qk", w, 2 * b_ + t) for b_ in range(B) for w in range(2) for t in range(2)]
                    + [("values", 0, t) for t in range(NT)],
                    [("key", 0, 0), ("key", 0, 1)] + quad_builds(0) + [("key", 0, 2), ("key", 0, 3)]
                    + quad_builds(1) + [("values", 0, 0)])

        def pro(k):
            return PROLOGUE[int(k > 0)]

        def pro_end(k, *item):
            return ring_first(k) + pro(k).index(item) + 1

        TAIL = [("den", 0)] + [("spread", h) for h in range(2)] + [("proj", h) for h in range(2)]

        def ring_starts(k):
            lat = k > 0
            n = sum(ring_total(i) for i in range(k)) + len(pro(k)) + len(ring_plan(False, True, False))
            starts = []
            for lo, hi, tail, ahead, build in iterations(lat):
                starts.append(n)
                n += (hi - lo) * len(ring_plan(tail, ahead, build))
            return starts, n

        def ring_total(k):
            lat = k > 0
            n = len(pro(k)) + len(ring_plan(False, True, False)) + len(TAIL)
            for lo, hi, tail, ahead, build in iterations(lat):
                n += (hi - lo) * len(ring_plan(tail, ahead, build))
            return n

        def ring_first(k):
            return sum(ring_total(i) for i in range(k))

        def run(eng, k, body):
            starts, end = ring_starts(k)
            for (lo, hi, tail, ahead, build), r0 in zip(iterations(k > 0), starts):
                per = len(ring_plan(tail, ahead, build))
                if hi - lo == 1:
                    body(lo, r0, tail, ahead, build, lo == 0)
                else:
                    with eng.Fori(0, hi - lo) as i:
                        body(i + lo, i * per + r0, tail, ahead, build, False)
            return end

        def slot(n):
            return (n % NQ) * QUAD

        def seq(n):
            return n // NQ

        STK = (6 * 16, 4 * 16)

        def stk_base(k):
            return NN * STK[0] * min(k, 1) + NN * STK[1] * max(k - 1, 0)

        def pe_unit(pe, k, n, u, bnk):
            qt, c0, w, heads = u
            for o, j in enumerate(heads):
                dst = bnk[:, o * w:(o + 1) * w]
                q = QS[0:CROW, bass.ds(slot(n) + j, 1), qt * P:(qt + 1) * P].squeeze(1)
                if k == 0:
                    key = KS[0:CROW, bass.ds(slot(n) + j, 1), c0:c0 + w].squeeze(1)
                else:
                    key = KS[0:CROW, bass.ds(seq(n), 1), c0:c0 + w].squeeze(1)
                diag = c0 + w == (qt + 1) * P
                ins = pe.matmul(dst, q, key, start=True, stop=not diag)
                if diag:
                    ins = pe.matmul(dst[:, w - P:w], identb[:, :], maskqk[:, :], start=False, stop=True)
            return ins

        def pe_scores(pe, k, n, s):
            kt, heads = STEP[s]
            q0 = kt * P
            for j in heads:
                for lo, hi in halves_of(kt):
                    b0 = lo // TT if len(heads) == 1 else j % 2
                    dst = ps[s % 2][:, b0, lo % TT:lo % TT + hi - lo]
                    diag = lo == q0
                    if k == 0:
                        terms = [(slot(n) + j, CROW + 1)]
                    else:
                        terms = [(seq(n), CROW + 1), (seq(n) + B, CROW)]
                    for i, (ks, rows) in enumerate(terms):
                        ins = pe.matmul(dst, KS[0:rows, bass.ds(ks, 1), q0:q0 + P].squeeze(1),
                                        QS[0:rows, bass.ds(slot(n) + j, 1), lo:hi].squeeze(1),
                                        start=(i == 0), stop=(i == len(terms) - 1 and not diag))
                    if diag:
                        ins = pe.matmul(dst[:, 0:P], identb[:, :], maskkq[:, :], start=False, stop=True)
            ins.then_inc(s_st, 1)

        def pe_pv(pe, k, n, kt, piece, first):
            lo, hi = piece
            if piece == halves_of(kt)[0]:
                pe.wait_ge(s_exp, STEPS * NN * k + n * STEPS + steps_to(kt))
                if kt == 0:
                    pe.wait_ge(s_vs, NN * k + n + 1)
                    if not first:
                        pe.wait_ge(s_os, 2 * NN * k + 2 * n)
            for j in range(QUAD):
                ins = pe.matmul(OUTP[32 * j:32 * j + 32, lo // TT, lo % TT:lo % TT + hi - lo],
                                VS[:, kt, j, :], PR[:, kt % 2, j, lo:hi], start=(kt == 0),
                                stop=(kt == (3 if lo < TT else KT - 1)))
            if piece == halves_of(kt)[-1]:
                ins.then_inc(s_pv, 1)

        def pe_ring(pe, k, n, kind, arg, r, l):
            pe.wait_ge(s_rd, r - 1 if l >= 2 else r)
            bnk = bank(RING[l % 2])
            if kind == "unit":
                ins = pe_unit(pe, k, n + 1, arg, bnk)
            elif kind == "turn":
                pe.wait_ge(s_m4, NN * k + n + 2)
                ins = pe.transpose(bnk[0:QUAD * KT, 0:P], M4[:, :], identf[:, :])
            elif kind == "den":
                pe.wait_ge(s_os, 2 * NN * k + 2 * n)
                pick = (sel1 if k else sel0)[:, :].rearrange("p (j c) -> p j c", j=QUAD)[:, :, 0]
                for c in range(KT):
                    ins = pe.matmul(bnk[:, c * QUAD:(c + 1) * QUAD], OS[:, c * P:(c + 1) * P], pick,
                                    start=True, stop=True)
            elif kind == "spread":
                pe.wait_ge(s_rd, r)
                for i in range(KT // 2):
                    c = arg * (KT // 2) + i
                    ins = pe.matmul(bnk[:, i * P:(i + 1) * P], RX[:, c * P:(c + 1) * P], identf[:, :],
                                    start=True, stop=True)
            elif kind == "proj":
                pe.wait_ge(s_wos, NN * k + n)
                ins = pe.matmul(bnk, stage[:, 3, :], ON[:, arg * TT:(arg + 1) * TT], start=True, stop=True)
            else:
                w = ("rope", "swap", "lat").index(kind)
                if w == 0 and arg == 0:
                    pe.wait_ge(s_wst, NN * (k - 1) + n + 3)
                ins = pe.matmul(bnk, stage[:, w, :], XN[:, bass.ds(seq(n + 2) * S + arg * TT, TT)],
                                start=True, stop=True)
            ins.then_inc(s_rr, 1)

        def pe_attn(pe, k, kn):
            r = ring_first(k)
            pe.wait_ge(s_xn, 4 * (kn + 1))
            pe.wait_ge(s_w, N_WFIRST)
            if k:
                pe.wait_ge(s_wl, N_WL)
            for l, (kind, m, t) in enumerate(pro(k)):
                if l >= 2:
                    pe.wait_ge(s_rd, r + l - 1)
                elif k:
                    pe.wait_ge(s_rd, r)
                o = bank(RING[l % 2])
                if kind == "qk":
                    ins = pe.matmul(o, wq0[:, m, :], XN[:, tsl(t)], start=True, stop=True)
                elif kind == "values" and k == 0:
                    for i in range(4):
                        ins = pe.matmul(o[:, i * P:(i + 1) * P], XN[:, (4 * t + i) * P:(4 * t + i + 1) * P],
                                        wq0[:, 2, :], start=True, stop=True)
                elif kind == "values":
                    for i in range(NTT):
                        ins = pe.matmul(o[:, i * LAT:(i + 1) * LAT], XN[:, i * P:(i + 1) * P], w_kva[:, 0:LAT],
                                        start=True, stop=True)
                elif kind == "key":
                    ins = pe.matmul(o[0:96, :], w_kva, XN[:, tsl(t)], start=True, stop=True)
                else:
                    w = ("rope", "swap", "lat").index(kind)
                    if w == 0 and t == 0:
                        pe.wait_ge(s_wst, NN * (k - 1) + m + 1)
                    ins = pe.matmul(o, stage[:, w, :], XN[:, tsl(t)], start=True, stop=True)
                ins.then_inc(s_rr, 1)
            l = len(pro(k))
            pe.wait_ge(s_stk, stk_base(k) + STK[int(k > 0)])
            pe.wait_ge(s_zero, ZERO[k])
            if k:
                pe.wait_ge(s_kdma, KDMA * (B * (k - 1) + 1))
            else:
                pe.wait_ge(s_cdma, 16 * 2)
            for i, (_, kind, arg) in enumerate(ring_plan(False, True, False)):
                pe_ring(pe, k, -1, kind, arg, r + l, l)
                l += 1

            def body(n, r0, tail, ahead, build, first):
                uses = list(enumerate(ring_plan(tail, ahead, build)))
                pe.wait_ge(s_crow, 16 * (NN * k + n + 1))
                landed = not ahead
                for place, (what, s, piece) in enumerate(WORK):
                    if what == "scores":
                        if not (first and s < 2 and k == 0):
                            pe.wait_ge(s_exp, STEPS * NN * k + n * STEPS + s - 1)
                        pe_scores(pe, k, n, s)
                    else:
                        pe_pv(pe, k, n, s, piece, first)
                    for at_, (after, kind, arg) in uses:
                        if after == place:
                            if kind == "unit" and not landed:
                                pe.wait_ge(s_stk, stk_base(k) + STK[int(k > 0)] * (n + 2))
                                landed = True
                            pe_ring(pe, k, n, kind, arg, r0 + at_, at_)

            if k:
                pe.wait_ge(s_kdma, KDMA * B * k)
            end = run(pe, k, body)
            for i, (kind, arg) in enumerate(TAIL):
                pe_ring(pe, k, NN, kind, arg, end + i, i)

        def act_attn(act, k):
            def body(n, r0, tail, ahead, build, first):
                for s in range(STEPS):
                    kt, heads = STEP[s]
                    q0 = kt * P
                    act.wait_ge(s_st, STEPS * NN * k + n * STEPS + s + 1)
                    if heads[0] == 0 and not (first and kt < 2):
                        act.wait_ge(s_pv, 8 * NN * k + n * KT + kt - 1)
                    if len(heads) == 1:
                        dst = PR[:, kt % 2, heads[0], q0:S]
                        src = ps[s % 2][:, :, :].rearrange("p a t -> p (a t)")[:, q0:S]
                    else:
                        dst = PR[:, kt % 2, heads[0]:heads[-1] + 1, q0:S]
                        src = ps[s % 2][:, :, q0 - TT:TT]
                    act.activation(dst, src, ACT.Exp, scale=0.125 if k else 1.0).then_inc(s_exp, 1)
            run(act, k, body)

        dest = (XT, YA, YA)

        def dve_ring(dve, k, n, kind, arg, r, l):
            dve.wait_ge(s_rr, r + 1)
            bnk = bank(RING[l % 2])
            if kind == "unit":
                qt, c0, w, heads = arg
                dve.tensor_reduce(BM[:, c0 // TT, heads[0]:heads[0] + len(heads), qt],
                                  bnk[:, 0:w * len(heads)].rearrange("p (j w) -> p j w", w=w),
                                  AX.X, ALU.max).then_inc(s_rd, 1)
            elif kind == "turn":
                dve.tensor_copy(CT[:, :], bnk[0:QUAD * KT, 0:P]).then_inc(s_rd, 1)
            elif kind == "den":
                dve.reciprocal(RD[:, :], bnk[:, 0:KT * QUAD]).then_inc(s_den, 1)
                dve.wait_ge(s_den, NN * k + n)
                dve.tensor_copy(RX[:, :].rearrange("p (c r) -> p c r", r=32),
                                RD[:, :].unsqueeze(2).to_broadcast([P, KT * QUAD, 32])).then_inc(s_rd, 1)
            elif kind == "spread":
                hs = slice(arg * TT, (arg + 1) * TT)
                dve.tensor_tensor(ON[:, hs], OS[:, hs], bnk, ALU.mult).then_inc(s_rd, 1)
            elif kind == "proj":
                x = dest[k][:, bass.ds(seq(n - 1) * S + arg * TT, TT)]
                ins = dve.tensor_tensor(x, x, bnk, ALU.add)
                ins.then_inc(s_rd, 1)
            elif kind == "lat":
                m = n + 2
                h = arg
                if not (isinstance(m, int) and m == 0):
                    dve.wait_ge(s_bnc, bnc_base(k) + 16 * m)
                dve.tensor_copy(HL[:, 2, h * TT:(h + 1) * TT], bnk).then_inc(s_lat, 1)
                dve.wait_ge(s_lat, 2 * NN * (k - 1) + 2 * m + h + 1)
                dve.tensor_tensor(HL[:, 3, h * TT:(h + 1) * TT], bnk, HL[:, 2, h * TT:(h + 1) * TT],
                                  ALU.subtract).then_inc(s_rd, 1)
            else:
                w = ("rope", "swap").index(kind)
                m = n + 2
                if w == 0:
                    dve.wait_ge(s_kb, kb_before(k, q_item(m, arg) - 1))
                dve.tensor_tensor(BT[:, 2 * arg + w, :], bnk, (cosT, sinT)[w][:, arg * TT:(arg + 1) * TT],
                                  ALU.mult).then_inc(s_rd, 1)

        def key_item(t):
            return t if t < 2 else t + 2

        def q_item(m, h):
            return 2 + h if isinstance(m, int) and m == 0 else 2 * m + (4 + h)

        def kb_before(k, item):
            return item * 3 + (k - 1) * 3 * (NT + 2 * NN)

        def bnc_base(k):
            return 16 * B * min(k, 1) + 16 * NN * max(k - 1, 0)

        def dve_plan(dve, k, n, plan, r0):
            for i, (_, kind, arg) in enumerate(plan):
                if kind == "turn":
                    dve.wait_ge(s_rd, r0 + i)
                    if not (isinstance(n, int) and k == 0 and n < 0):
                        dve.wait_ge(s_crow, 16 * (NN * k + n + 1))
                    dve.tensor_tensor(M4[:, :], BM[:, 0, :, :].rearrange("p j q -> p (j q)"),
                                      BM[:, 1, :, :].rearrange("p j q -> p (j q)"), ALU.max).then_inc(s_m4, 1)
                dve_ring(dve, k, n, kind, arg, r0 + i, i)

        def dve_copy_out(dve, k, n):
            dve.wait_ge(s_pv, 8 * NN * k + n * KT)
            for h in range(2):
                dve.tensor_copy(OS[:, h * TT:(h + 1) * TT], OUTP[:, h, :]).then_inc(s_os, 1)

        SC0 = float(np.float32(1.0) / np.sqrt(np.float32(HD0)))

        def dve_attn(dve, k, ch):
            r = ring_first(k)
            if k == 0:
                for i, (kind, w, t) in enumerate(pro(0)):
                    bnk = bank(RING[i % 2])
                    dve.wait_ge(s_rr, r + i + 1)
                    if kind == "values":
                        dve.tensor_copy(YA[:, tsl(t)], bnk).then_inc(s_rd, 1)
                        continue
                    sc = (SC0, 1.0)[w]
                    ch.link(dve.tensor_scalar(HL[:, 2 * w, tsl(t)], bnk, sc, None, ALU.mult))
                    dve.scalar_tensor_tensor(out=HL[:, 2 * w + 1, tsl(t)], in0=bnk, scalar=sc,
                                             in1=HL[:, 2 * w, tsl(t)], op0=ALU.mult,
                                             op1=ALU.subtract).then_inc(s_rd, 1)
            else:
                dve.wait_ge(s_wl, N_WL)
                for i, (kind, m, t) in enumerate(pro(k)):
                    bnk = bank(RING[i % 2])
                    if kind == "values":
                        dve.wait_ge(s_rr, r + i + 1)
                        dve.tensor_copy(VL[:, :, :].rearrange("p i c -> p (i c)"),
                                        bnk[:, 0:NTT * LAT]).then_inc(s_rd, 1)
                    elif kind == "key":
                        dve.wait_ge(s_rr, r + i + 1)
                        if t >= 2:
                            dve.wait_ge(s_kb, kb_before(k, key_item(t) - 1))
                        cs = slice((t % 2) * TT, (t % 2 + 1) * TT)
                        a_ = 2 * (t % 2)
                        ch.up(dve.tensor_tensor(BT[32:64, a_, :], bnk[32:64, :], cosT[32:64, cs], ALU.mult))
                        ch.up(dve.tensor_tensor(BT[32:64, a_ + 1, :], bnk[64:96, :], sinT[64:96, cs], ALU.mult))
                        ch.link(dve.tensor_copy(KH[0:32, tsl(t)], bnk[0:32, :]))
                        dve.tensor_tensor(KL[0:32, tsl(t)], bnk[0:32, :], KH[0:32, tsl(t)],
                                          ALU.subtract).then_inc(s_rd, 1)
                    else:
                        dve_ring(dve, k, m - 2, kind, t, r + i, i)
            l = len(pro(k))
            for i, (_, kind, arg) in enumerate(ring_plan(False, True, False)):
                if kind == "turn":
                    dve.wait_ge(s_rd, r + l + i)
                    if k:
                        dve.wait_ge(s_crow, 16 * NN * k)
                    dve.tensor_tensor(M4[:, :], BM[:, 0, :, :].rearrange("p j q -> p (j q)"),
                                      BM[:, 1, :, :].rearrange("p j q -> p (j q)"), ALU.max).then_inc(s_m4, 1)
                dve_ring(dve, k, -1, kind, arg, r + l + i, l + i)

            def body(n, r0, tail, ahead, build, first):
                if tail:
                    dve_copy_out(dve, k, n)
                dve_plan(dve, k, n, ring_plan(tail, ahead, build), r0)

            if k:
                dve.wait_ge(s_kdma, KDMA * B * k)
            end = run(dve, k, body)
            dve_copy_out(dve, k, NN)
            for i, (kind, arg) in enumerate(TAIL):
                dve_ring(dve, k, NN, kind, arg, end + i, i)
            dve.wait_ge(s_rd, end + len(TAIL))
            s_done = s_xup if k == 0 else s_ya
            dve.memset(epsc[:, 2:3], 0.0).then_inc(s_done, 4)

        s_ya = sem("s_ya")
        s_kdma = sem("s_kdma")
        KDMA = 16 * 6
        ZERO = (2 * H + 3, 2 * H + 3 + 3, 2 * H + 3 + 6)

        def pool_attn_setup(pool, k):
            if k:
                pool.wait_ge(s_xup, setup_after[k])
                pool.memset(KS[:, B:2 * B, :].rearrange("p h s -> p (h s)").bitcast(F32), 0.0).then_inc(s_zero, 1)
                pool.wait_ge(s_zero, ZERO[k] - 2)
                pool.memset(KS[CROW:CROW + 1, 0:B, :].rearrange("p h s -> p (h s)"), -1.0).then_inc(s_zero, 1)
                pool.wait_ge(s_zero, ZERO[k] - 1)
                pool.memset(VS[:, :, :, LAT:LAT + 1].rearrange("p a j c -> p (a j) c"), 1.0).then_inc(s_zero, 1)
                pool.wait_ge(s_zero, ZERO[k])
                return
            for h in range(H):
                pool.memset(KS[:, h, :].bitcast(F32), 0.0).then_inc(s_zero, 1)
            pool.memset(VS[:, :, :, :].rearrange("p a j c -> p (a j c)"), 0.0).then_inc(s_zero, 1)
            pool.wait_ge(s_zero, H + 1)
            pool.memset(KS[CROW:CROW + 1, :, :].rearrange("p h s -> p (h s)"), -1.0).then_inc(s_zero, 1)
            pool.wait_ge(s_zero, H + 2)
            pool.memset(VS[:, :, :, HD0:HD0 + 1].rearrange("p a j c -> p (a j) c"), 1.0).then_inc(s_zero, 1)

        def pool_attn(pool, k, ch):
            w_o = wo1 if k else wo0

            def stage_q(m, first):
                if not first:
                    pool.wait_ge(s_lat, 2 * NN * (k - 1) + 2 * m)
                pool.wait_ge(s_const, 1)
                qd = m % NQ
                for i, w in enumerate((w_rope, w_swap, w_lat)):
                    src = w[:, bass.ds(qd, 1), :].squeeze(1)
                    ins = pool.tensor_copy(stage[:, i, :], src)
                    if i < 2:
                        ch.up(ins)
                ins.then_inc(s_wst, 1)
                ch.wait()
                pool.wait_ge(s_wst, NN * (k - 1) + m + 1)

            def rotary(item, rings, rows, buf, hi, lo):
                pool.wait_ge(s_rd, rings)
                if isinstance(item, int) and kb_before(k, item):
                    pool.wait_ge(s_kb, kb_before(k, item))
                b0, b1 = BT[rows, buf, :], BT[rows, buf + 1, :]
                pool.tensor_tensor(hi, b0, b1, ALU.add).then_inc(s_kb, 1)
                pool.tensor_tensor(b0, b0, b1, ALU.add).then_inc(s_kb, 1)
                pool.wait_ge(s_kb, kb_before(k, item) + 2)
                pool.tensor_tensor(lo, b0, hi, ALU.subtract).then_inc(s_kb, 1)

            def parts(m, h, rings):
                hs = slice(h * TT, (h + 1) * TT)
                if not (isinstance(m, int) and m == 0):
                    pool.wait_ge(s_bnc, bnc_base(k) + 16 * m)
                rotary(q_item(m, h), rings, slice(0, P), 2 * h, HL[:, 0, hs], HL[:, 1, hs])

            def keys(t):
                rotary(key_item(t), pro_end(k, "key", 0, t), slice(32, 64), 2 * (t % 2),
                       KH[32:64, tsl(t)], KL[32:64, tsl(t)])

            r = ring_first(k)
            if k:
                pool.wait_ge(s_wl, N_WL)
                stage_q(0, True)
                for m in range(2):
                    keys(2 * m)
                    keys(2 * m + 1)
                    for h in range(2):
                        parts(m, h, pro_end(k, "swap", m, h))
                    if m == 0:
                        stage_q(1, False)

            def stage_v(n, first):
                if first:
                    pool.wait_ge(s_rd, r + len(pro(k)))
                else:
                    pool.wait_ge(s_pv, 8 * NN * k + n * KT)
                pool.wait_ge(s_const, 1)
                if k == 0:
                    src = V0[:, bass.ds(seq(n) * KT, KT), bass.ds((n % NQ) * 32, 32)]
                    pool.tensor_copy(VS[:, :, :, 0:HD0], src.rearrange("p i (j d) -> p i j d", j=QUAD))\
                        .then_inc(s_vs, 1)
                else:
                    src = VL[:, bass.ds(seq(n) * KT, KT), :]
                    for j in range(QUAD):
                        ins = pool.tensor_copy(VS[:, :, j, 0:LAT], src)
                        if j < QUAD - 1:
                            ch.up(ins)
                    ch.wait()
                    ins.then_inc(s_vs, 1)

            def finish(n):
                pool.wait_ge(s_pv, 8 * NN * k + n * KT)
                pool.wait_ge(s_const, 1)
                src = w_o[:, bass.ds((n - 1) % NQ, 1), :].squeeze(1)
                pool.tensor_copy(stage[:, 3, :], src).then_inc(s_wos, 1)

            def body(n, r0, tail, ahead, build, first):
                n_ch = ch.n
                stage_v(n, first)
                if tail:
                    finish(n)
                if build:
                    plan = ring_plan(tail, ahead, build)
                    stage_q(n + 2, False)
                    for h in range(2):
                        at_ = max(i for i, (_, kd, ar) in enumerate(plan) if kd in ("rope", "swap") and ar == h)
                        parts(n + 2, h, r0 + at_ + 1)

            base = ch.n
            starts, end = ring_starts(k)
            for (lo, hi, tail, ahead, build), r0 in zip(iterations(k > 0), starts):
                per = len(ring_plan(tail, ahead, build))
                own = (3 if k else 0) + (2 if build else 0)
                c0 = ch.n
                if hi - lo == 1:
                    body(lo, r0, tail, ahead, build, lo == 0)
                else:
                    with pool.Fori(0, hi - lo) as i:
                        ch.n = i * own + c0
                        body(i + lo, i * per + r0, tail, ahead, build, False)
                ch.n = c0 + own * (hi - lo)
            finish(NN)

        def sp_attn(sp, k):
            r = ring_first(k)

            def send(slot_, b_=None):
                tok = slice(0, S) if b_ is None else slice(b_ * S, (b_ + 1) * S)
                sp.dma_start(parts_d[slot_].rearrange("a p s -> p a s"), HL[:, :, tok]).then_inc(s_bnc, 16)

            Q0, K0 = ((0, 8, 0), (8, 8, 1), (16, 8, 0)), ((0, 8, 2), (8, 8, 2), (16, 8, 3))
            Q1 = ((0, 32, 0), (32, 16, 2), (48, 32, 1), (80, 16, 3))

            def put0(m):
                for st, terms in ((QS, Q0), (KS, K0)):
                    for row, n_, part in terms:
                        h0 = (m % NQ) * QUAD * HD0
                        src = parts_d[m // NQ, part, h0:h0 + QUAD * HD0, :]
                        sp.dma_start(st[row:row + n_, slot(m):slot(m) + QUAD, :],
                                     src.rearrange("(j r) s -> r j s", j=QUAD)).then_inc(s_stk, 16)

            def put1(m):
                for row, n_, part in Q1:
                    src = parts_d[0, part].rearrange("(j r) s -> r j s", j=QUAD)[0:n_]
                    sp.dma_start(QS[row:row + n_, bass.ds(slot(m), QUAD), :], src).then_inc(s_stk, 16)

            def put_keys(b_):
                tok = slice(b_ * S, (b_ + 1) * S)
                for row, n_, sl, src in ((0, 32, b_, KH[32:64, tok]), (48, 32, b_, KH[32:64, tok]),
                                         (32, 16, b_, KH[0:16, tok]), (80, 16, b_, KH[0:16, tok]),
                                         (0, 32, B + b_, KL[32:64, tok]), (32, 16, B + b_, KL[0:16, tok])):
                    sp.dma_start(KS[row:row + n_, sl, :], src).then_inc(s_kdma, 16)

            def crow(m, turned, landed=None):
                sp.wait_ge(s_rd, turned)
                if landed is not None:
                    sp.wait_ge(s_stk, landed)
                sp.dma_start(QS[CROW:CROW + 1, bass.ds(slot(m), QUAD), :], CT[:, :]).then_inc(s_crow, 16)

            first_turned = r + len(pro(k)) + len(ring_plan(False, True, False))
            starts, _ = ring_starts(k)
            if k == 0:
                sp.wait_ge(s_zero, ZERO[0])
                sp.dma_start(QS[24:24 + SLOPE_PIECES, :, :], a["slopes"]).then_inc(s_cdma, 16)
                sp.dma_start(KS[24:24 + SLOPE_PIECES, :, :], a["kpos"]).then_inc(s_cdma, 16)
                for b_ in range(B):
                    sp.wait_ge(s_rd, pro_end(0, "qk", 1, 2 * b_ + 1))
                    send(b_, b_)
                    sp.wait_ge(s_bnc, 16 * (b_ + 1))
                    put0(b_)
                    sp.wait_ge(s_stk, STK[0] * (b_ + 1))
                crow(0, first_turned)
                rr = starts[0]
                for n in range(NN - 1):
                    if n + 2 < NN:
                        if n + 2 >= NQ:
                            sp.wait_ge(s_st, STEPS * (n + 2 - NQ + 1))
                        put0(n + 2)
                        sp.wait_ge(s_stk, STK[0] * (n + 3))
                    rr += len(ring_plan(n > 0, True, False))
                    crow(n + 1, rr)
                return
            sp.wait_ge(s_zero, ZERO[k])
            for m in range(2):
                sp.wait_ge(s_kb, kb_before(k, key_item(2 * m + 1) + 1))
                sp.wait_ge(s_rd, pro_end(k, "key", 0, 2 * m + 1))
                put_keys(m)
                sp.wait_ge(s_kb, kb_before(k, q_item(m, 1) + 1))
                sp.wait_ge(s_rd, pro_end(k, "lat", m, 1))
                send(0)
                sp.wait_ge(s_bnc, bnc_base(k) + 16 * (m + 1))
                put1(m)
                sp.wait_ge(s_kdma, KDMA * (B * (k - 1) + m + 1))
                sp.wait_ge(s_stk, stk_base(k) + STK[1] * (m + 1))
            crow(0, first_turned)
            for (lo, hi, tail, ahead, build), r0 in zip(iterations(True), starts):
                plan = ring_plan(tail, ahead, build)

                def it(n, r0):
                    if build:
                        lat_at = max(i for i, (_, kd, _) in enumerate(plan) if kd == "lat")
                        sp.wait_ge(s_rd, r0 + lat_at + 1)
                        sp.wait_ge(s_kb, kb_before(k, q_item(n + 2, 2)))
                        send(0)
                        sp.wait_ge(s_bnc, bnc_base(k) + 16 * (n + 3))
                        put1(n + 2)
                    if ahead:
                        crow(n + 1, r0 + len(plan), stk_base(k) + STK[1] * (n + 3) if build else None)
                if hi - lo == 1:
                    it(lo, r0)
                else:
                    with sp.Fori(0, hi - lo) as i:
                        it(i + lo, i * len(plan) + r0)

        def sp_last_weights(sp):
            sp.wait_ge(s_xup, xup_base["moe", 1] + 4)
            loads = [(cosT, a["cosT"]), (sinT, a["sinT"]), (w_rope, a["w_rope"].rearrange("p (g m) -> p g m", g=NQ)),
                     (w_swap, a["w_swap"].rearrange("p (g m) -> p g m", g=NQ)), (w_kva, a["w_kva"]),
                     (w_gate1, a["w_gate1"]), (w_up1, a["w_up1"]), (w_down1[:, 0:4, :], a["Wd"].rearrange("(g e) i o -> (e i) g o", e=2)),
                     (w_down1[0:I1, 4, :], a["sWd"]), (w_rt1, a["Wgate"])]
            for dst, src in loads:
                sp.dma_start(dst, src).then_inc(s_wl, 16)

        N_WL = 16 * 10

        def pe_comp(pe):
            pe.wait_ge(s_wc, 64)
            for h in range(H):
                ins = pe.matmul(bank(6)[:, h * 32:(h + 1) * 32], wqn[:, h, :], wkb[:, h, :], start=True, stop=True)
            ins.then_inc(s_comp, 1)
            for h in range(H):
                g, j = divmod(h, QUAD)
                ins = pe.matmul(bank(7)[32 * j:32 * j + 32, g * P:(g + 1) * P], wkb[:, h, :], won[h // 8][:, h % 8, :],
                                start=True, stop=True)
            ins.then_inc(s_comp, 1)

        def act_comp(act):
            act.wait_ge(s_comp, 1)
            act.copy(w_lat[:, :, :].rearrange("p g m -> p (g m)"), bank(6)).then_inc(s_compd, 1)
            act.wait_ge(s_comp, 2)
            act.copy(wo1[:, :, :].rearrange("p g m -> p (g m)"), bank(7)).then_inc(s_compd, 1)

        A_ABS, A_LN, A_DEC, A_FFN = 2 * NT, 3 * NT, 4 * NT, 5 * NT
        s_sg = sem("s_sg")

        def dbc_bank(t, w):
            return bank(2 + 3 * (t % 2) + w)

        def pe_scan(pe, kn):
            for t in range(NT):
                pe.wait_ge(s_xn, 4 * kn + t + 1)
                if t >= 2:
                    pe.wait_ge(s_sa, 2 * (t - 1))
                if t == 0:
                    pe.wait_ge(s_xn, 4 * (kn + 1))
                pe.matmul(bank(2 * (t % 2)), w_inp[:, 0, :], XN[:, tsl(t)], start=True, stop=True)
                pe.matmul(bank(2 * (t % 2) + 1), w_inp[:, 1, :], XN[:, tsl(t)], start=True,
                          stop=True).then_inc(s_sp, 1)
            pe.wait_ge(s_sa, A_ABS)
            for t in range(NT):
                pe.wait_ge(s_sd, 1 + t // 2)
                if t >= 2:
                    pe.wait_ge(s_sa, A_ABS + t - 1)
                for w in range(3):
                    ins = pe.matmul(dbc_bank(t, w), w_dbc[:, w, :], MX[:, tsl(t)], start=True, stop=True)
                ins.then_inc(s_sp, 1)
            for t in range(NT):
                pe.wait_ge(s_sd, 3 + t // 2)
                if t >= 2:
                    pe.wait_ge(s_ya, 4 + t - 1)
                pe.matmul(bank(5 + t % 2), w_outp[:, :], DTm[:, tsl(t)], start=True, stop=True).then_inc(s_sp, 1)

        def act_scan(act, ch):
            for t in range(NT):
                b_, o = divmod(t * TT, S)
                act.wait_ge(s_sp, t + 1)
                act.activation(XP[:, b_, 1 + o:1 + o + TT], bank(2 * (t % 2)), ACT.Identity,
                               bias=colp[:, C_INB0:C_INB0 + 1]).then_inc(s_sa, 1)
                act.activation(SG[:, tsl(t)], bank(2 * (t % 2) + 1), ACT.Sigmoid,
                               bias=colp[:, C_INB1:C_INB1 + 1]).then_inc(s_sa, 1)
            ch.link(act.activation(colw[:, 2:3], colp[:, C_A:C_A + 1], ACT.Exp))
            ch.link(act.mul(colw[:, 3:4], colw[:, 2:3], -1.0))
            for t in range(NT):
                act.wait_ge(s_sp, NT + t + 1)
                act.activation(BTm[:, tsl(t)], dbc_bank(t, 1), ACT.Tanh, bias=colp[:, C_BB:C_BB + 1])
                act.activation(CTm[:, tsl(t)], dbc_bank(t, 2), ACT.Tanh, bias=colp[:, C_CB:C_CB + 1])
                act.wait_ge(s_so, t + 1)
                act.activation(DEC[:, tsl(t)], dbc_bank(t, 0), ACT.Abs,
                               bias=colp[:, C_DTB:C_DTB + 1]).then_inc(s_sa, 1)
                act.wait_ge(s_sa, A_ABS + t + 1)
                ch.up(act.activation(DEC[:, tsl(t)], DEC[:, tsl(t)], ACT.Exp, scale=-1.0))
            ch.wait()
            for t in range(NT):
                act.activation(DEC[:, tsl(t)], DEC[:, tsl(t)], ACT.Ln, bias=1.0).then_inc(s_sa, 1)
            for t in range(NT):
                act.wait_ge(s_so, NT + t + 1)
                act.activation(DEC[:, tsl(t)], DTm[:, tsl(t)], ACT.Exp, scale=colw[:, 3:4]).then_inc(s_sa, 1)

        def pool_scan(pool):
            for t in range(NT):
                if t % 2 == 0:
                    pool.wait_ge(s_sd, 1 + t // 2)
                pool.wait_ge(s_sa, A_ABS + t + 1)
                pool.tensor_tensor(BTm[:, tsl(t)], BTm[:, tsl(t)], MX[:, tsl(t)], ALU.mult)
                pool.tensor_tensor(CTm[:, tsl(t)], CTm[:, tsl(t)], SG[:, tsl(t)], ALU.mult).then_inc(s_sg, 1)
                pool.tensor_tensor(SG[:, tsl(t)], MX[:, tsl(t)], SG[:, tsl(t)], ALU.mult).then_inc(s_sg, 1)

        def dve_scan(dve, kn, ch):
            def col(c):
                return colp[:, c:c + 1]

            dve.wait_ge(s_xn, 4 * (kn + 1))
            for b_ in range(B):
                ch.up(dve.memset(XP[:, b_, 0:1], 0.0))
                ch.up(dve.memset(XP[:, b_, S + 1:S + 2], 0.0))
            for b_ in range(B):
                dve.wait_ge(s_sa, 4 * (b_ + 1))
                ch.wait()
                m = MX[:, b_ * S:(b_ + 1) * S]
                ch.link(dve.tensor_scalar(m, XP[:, b_, 1:S + 1], col(C_DW1), col(C_DWB), ALU.mult, ALU.add))
                ch.link(dve.scalar_tensor_tensor(out=m, in0=XP[:, b_, 0:S], scalar=col(C_DW0), in1=m,
                                                 op0=ALU.mult, op1=ALU.add))
                dve.scalar_tensor_tensor(out=m, in0=XP[:, b_, 2:S + 2], scalar=col(C_DW2), in1=m,
                                         op0=ALU.mult, op1=ALU.add).then_inc(s_sd, 1)
            for t in range(NT):
                dve.wait_ge(s_sp, NT + t + 1)
                dve.tensor_scalar(DTm[:, tsl(t)], dbc_bank(t, 0), col(C_DTB), 0.0, ALU.add,
                                  ALU.max).then_inc(s_so, 1)
            dve.wait_ge(s_so, NT)
            for t in range(NT):
                dve.wait_ge(s_sa, A_LN + t + 1)
                dve.tensor_tensor(DTm[:, tsl(t)], DTm[:, tsl(t)], DEC[:, tsl(t)], ALU.add).then_inc(s_so, 1)
            dve.wait_ge(s_so, 2 * NT)
            for b_ in range(B):
                c = slice(b_ * S, (b_ + 1) * S)
                dve.wait_ge(s_sg, 4 * (b_ + 1))
                ch.link(dve.tensor_tensor(BTm[:, c], BTm[:, c], DTm[:, c], ALU.mult))
                dve.wait_ge(s_sa, A_DEC + 2 * (b_ + 1))
                ch.link(dve.tensor_tensor_scan(ST_[:, c], DEC[:, c], BTm[:, c], 0.0, ALU.mult, ALU.add))
                ch.link(dve.tensor_tensor(ST_[:, c], ST_[:, c], CTm[:, c], ALU.mult))
                dve.scalar_tensor_tensor(out=DTm[:, c], in0=SG[:, c], scalar=col(C_DSK), in1=ST_[:, c],
                                         op0=ALU.mult, op1=ALU.add).then_inc(s_sd, 1)
            for t in range(NT):
                dve.wait_ge(s_sp, 2 * NT + t + 1)
                dve.scalar_tensor_tensor(out=YA[:, tsl(t)], in0=bank(5 + t % 2), scalar=col(C_OB),
                                         in1=YA[:, tsl(t)], op0=ALU.add, op1=ALU.add).then_inc(s_ya, 1)

        def pe_ffn(pe, kn):
            def down(t):
                pe.wait_ge(s_sa, A_FFN + 2 * (t + 1))
                if t >= 2:
                    pe.wait_ge(s_xup, xup_base["scan", 0] + t - 1)
                for c in range(2):
                    ins = pe.matmul(bank(2 + t % 2), w_f2[:, c, :], F1[:, t % 2, c, :], start=(c == 0), stop=(c == 1))
                ins.then_inc(s_sp, 1)

            pe.wait_ge(s_xn, 4 * (kn + 1))
            for t in range(NT):
                if t >= 2:
                    pe.wait_ge(s_sa, A_FFN + 2 * (t - 1))
                for c in range(2):
                    ins = pe.matmul(bank(4 * (t % 2) + c), w_f1[:, c, :], XN[:, tsl(t)], start=True, stop=True)
                ins.then_inc(s_sp, 1)
                if t:
                    down(t - 1)
            down(NT - 1)

        def out_count(t):
            return 3 * NT + (2 * t + 3 if t < NT - 1 else 2 * NT)

        def act_ffn(act):
            for t in range(NT):
                act.wait_ge(s_sp, 3 * NT + 1 if t == 0 else 3 * NT + 2 * t)
                if t >= 2:
                    act.wait_ge(s_sp, out_count(t - 2))
                for c in range(2):
                    act.activation(F1[:, t % 2, c, :], bank(4 * (t % 2) + c), ACT.Gelu,
                                   bias=colp[:, C_F1B0 + c:C_F1B0 + c + 1]).then_inc(s_sa, 1)

        def dve_ffn(dve, ch):
            for t in range(NT):
                dve.wait_ge(s_sp, out_count(t))
                ch.link(dve.scalar_tensor_tensor(out=YA[:, tsl(t)], in0=bank(2 + t % 2),
                                                 scalar=colp[:, C_F2B:C_F2B + 1], in1=YA[:, tsl(t)],
                                                 op0=ALU.add, op1=ALU.add))
                dve.tensor_tensor(XT[:, tsl(t)], XT[:, tsl(t)], YA[:, tsl(t)], ALU.add).then_inc(s_xup, 1)

        def pe_store(pe):
            pe.wait_ge(s_xup, xup_base["end", 0])
            for i in range(NTT):
                ins = pe.transpose(bank(i // 4)[:, (i % 4) * P:(i % 4 + 1) * P], XT[:, i * P:(i + 1) * P], identf[:, :])
                if i % 4 == 3:
                    ins.then_inc(s_ld, 1)

        def dve_store(dve):
            for t in range(NT):
                dve.wait_ge(s_ld, NT + t + 1)
                dve.tensor_copy(XN[:, tsl(t)], bank(t)).then_inc(s_fin, 1)

        def sp_store(sp):
            for t in range(NT):
                sp.wait_ge(s_fin, t + 1)
                sp.dma_start(out.rearrange("(i p) d -> p i d", p=P)[:, 4 * t:4 * t + 4, :],
                             XN[:, tsl(t)].rearrange("p (i d) -> p i d", i=4)).then_inc(s_store, 16)
            sp.wait_ge(s_store, 16 * NT)

        xup_base = {("moe", 0): 4, ("attn", 0): 8, ("moe", 1): 12, ("moe", 2): 16, ("scan", 0): 20,
                    ("moe", 3): 24, ("end", 0): 28}
        setup_after = {1: 16, 2: 24}

        block = ctx.enter_context(nc.Block())

        @block.sync
        def _(sp):
            sp_load(sp)
            sp_gates(sp, 0, False)
            sp_attn(sp, 0)
            sp.wait_ge(s_xup, 12)
            sp_gates(sp, 1, False)
            sp_last_weights(sp)
            sp_attn(sp, 1)
            sp_gates(sp, 2, True)
            sp_attn(sp, 2)
            sp_gates(sp, 3, True)
            sp_store(sp)

        @block.gpsimd
        def _(pool):
            pool_const(pool)
            ch = Chain(pool, s_pool)
            ch.n = 8
            pool_attn_setup(pool, 0)
            pool_moe0(pool, 0)
            pool.wait_ge(s_out, ag_base(1))
            for h in range(H):
                pool.memset(QS[:, h, :].bitcast(F32), 0.0).then_inc(s_zero, 1)
            pool_attn(pool, 0, ch)
            pool_moe0(pool, 1)
            pool_attn_setup(pool, 1)
            pool_attn(pool, 1, ch)
            pool_moe1(pool, 2)
            pool_scan(pool)
            pool_attn_setup(pool, 2)
            pool_attn(pool, 2, ch)
            pool_moe1(pool, 3)

        @block.scalar
        def _(act):
            ch = Chain(act, s_act)
            act.wait_ge(s_const, N_CONST)
            act_norm(act, 0, "plain", ch)
            act_router(act, 0)
            act_comp(act)
            act_moe0(act, 0)
            act_norm(act, 1, "plain", ch)
            act_attn(act, 0)
            act_norm(act, 2, "plain", ch)
            act_router(act, 1)
            act_moe0(act, 1)
            act_norm(act, 3, "fused", ch)
            act_attn(act, 1)
            act_norm(act, 4, "rms", ch)
            act_router(act, 2)
            act_moe1(act, 2)
            act_norm(act, 5, "fused", ch)
            act_scan(act, ch)
            act_norm(act, 6, "ln2", ch)
            act_ffn(act)
            act_norm(act, 7, "fused", ch)
            act_attn(act, 2)
            act_norm(act, 8, "rms", ch)
            act_router(act, 3)
            act_moe1(act, 3)

        @block.tensor
        def _(pe):
            pe_load(pe)
            pe_norm(pe, 0, "plain", (s_xup, 4))
            pe.wait_ge(s_w, N_WFIRST)
            pe_router(pe, 0, 0, w_rt0[:, :], False, True)
            pe_comp(pe)
            pe.wait_ge(s_compd, 2)
            pe_moe0(pe, 0)
            pe_norm(pe, 1, "plain", (s_xup, 8))
            pe_attn(pe, 0, 1)
            pe_norm(pe, 2, "plain", (s_xup, 12))
            pe_router(pe, 1, 2, w_rt0[:, :], False, True)
            pe_moe0(pe, 1)
            pe_norm(pe, 3, "fused", (s_xup, 16))
            pe_attn(pe, 1, 3)
            pe_norm(pe, 4, "rms", (s_ya, 4))
            pe.wait_ge(s_wl, N_WL)
            pe_router(pe, 2, 4, w_rt1, True, False)
            pe_moe1(pe, 2)
            pe_norm(pe, 5, "fused", (s_xup, 20))
            pe_scan(pe, 5)
            pe_norm(pe, 6, "ln2", (s_ya, 8))
            pe_ffn(pe, 6)
            pe_norm(pe, 7, "fused", (s_xup, 24))
            pe_attn(pe, 2, 7)
            pe_norm(pe, 8, "rms", (s_ya, 12))
            pe_router(pe, 3, 8, w_rt1, True, False)
            pe_moe1(pe, 3)
            pe_store(pe)

        @block.vector
        def _(dve):
            ch = Chain(dve, s_dve)
            dve_load(dve)
            dve.wait_ge(s_const, N_CONST)
            dve.wait_ge(s_w, N_WFIRST)
            dve_norm(dve, 0, "plain")
            dve_router(dve, 0, True, ch)
            dve_moe0(dve, 0)
            dve_norm(dve, 1, "plain")
            dve_attn(dve, 0, ch)
            dve_norm(dve, 2, "plain")
            dve_router(dve, 1, True, ch)
            dve_moe0(dve, 1)
            dve_norm(dve, 3, "fused", w=colw[:, 0:1])
            dve_attn(dve, 1, ch)
            dve_norm(dve, 4, "rms", w=colw[:, 1:2])
            dve_router(dve, 2, False, ch)
            dve_moe1(dve, 2, ch)
            dve_norm(dve, 5, "fused", w=colp[:, C_L1G:C_L1G + 1], b=colp[:, C_L1B:C_L1B + 1], ch=ch)
            dve_scan(dve, 5, ch)
            dve_norm(dve, 6, "ln2", w=colp[:, C_L2G:C_L2G + 1], b=colp[:, C_L2B:C_L2B + 1], ch=ch)
            dve_ffn(dve, ch)
            dve_norm(dve, 7, "fused", w=colw[:, 0:1])
            dve_attn(dve, 2, ch)
            dve_norm(dve, 8, "rms", w=colw[:, 1:2])
            dve_router(dve, 3, False, ch)
            dve_moe1(dve, 3, ch)
            dve_store(dve)


def shape_constants():
    f = np.float32
    slopes = f(1.0) / np.power(f(2.0 ** 8), (np.arange(H, dtype=f) + f(1)) / f(H), dtype=f)
    pieces, rest = [], slopes.copy()
    for _ in range(SLOPE_PIECES):
        piece = rest.astype(np.float16)
        pieces.append(piece)
        rest = rest - piece.astype(f)
    slope_rows = np.stack([np.repeat(p[:, None], S, 1) for p in pieces])
    kpos = np.broadcast_to((np.arange(S) - S // 2).astype(np.float16), (SLOPE_PIECES, H, S)).copy()
    freqs = f(1.0) / np.power(100000.0, np.arange(0, ROPE, 2) / ROPE).astype(f)
    ang = np.outer(np.arange(S, dtype=f), freqs).astype(f)
    cos, sin = np.cos(ang).astype(f), np.sin(ang).astype(f)
    c32 = np.repeat(cos.T, 2, 0)
    s32 = np.repeat(sin.T, 2, 0)
    s32[0::2] = -s32[0::2]
    return {"slopes": slope_rows, "kpos": kpos, "cosT": np.tile(c32, (4, 1)), "sinT": np.tile(s32, (4, 1))}


def layouts(i):
    g = {k: np.asarray(v) for k, v in i.items()}
    f = np.float32
    d = {"x": g["L0_attn_x"].reshape(T, D)}
    d["Wg0"], d["W_in"], d["W_out"] = g["L0_ffn_Wg"], g["L0_ffn_W_in"], g["L0_ffn_W_out"]
    d["Wqkv0"] = np.stack([g["L0_attn_W_Q"].T, g["L0_attn_W_K"].T, g["L0_attn_W_V"].T])
    wo = np.zeros((NQ, QUAD, 32, D), f)
    wo[:, :, 0:HD0, :] = g["L0_attn_W_O"].T.reshape(NQ, QUAD, HD0, D)
    d["WoPad0"] = wo.reshape(NQ, P, D)
    d["expert_bias"] = g["L1_ffn_expert_bias"].reshape(1, E)
    n = "L1_attn_"
    dw = g[n + "dw_W"].reshape(D, 3)
    d["cols"] = np.stack([g[n + "ln1_g"], g[n + "ln1_b"], g[n + "in_b"][:D], g[n + "in_b"][D:], dw[:, 0], dw[:, 1],
                          dw[:, 2], g[n + "dw_b"], g[n + "dt_b"], g[n + "b_b"], g[n + "c_b"], g[n + "a_log"],
                          g[n + "d_skip"], g[n + "out_b"], g[n + "ln2_g"], g[n + "ln2_b"], g[n + "f1_b"][:D],
                          g[n + "f1_b"][D:], g[n + "f2_b"]], axis=1)
    d["colw"] = np.stack([g["L1_ffn_w_ln1"], g["L1_ffn_w_ln2"]], axis=1)
    for k in ("in_W", "dt_W", "b_W", "c_W", "out_W", "f1_W", "f2_W"):
        d[k] = g[n + k]
    wq = g["L1_ffn_Wq"].reshape(D, H, 64)
    d["w_rope"] = wq[:, :, NOPE:].reshape(D, H * ROPE)
    d["w_swap"] = wq[:, :, NOPE:].reshape(D, H, ROPE // 2, 2)[..., ::-1].reshape(D, H * ROPE)
    kva = g["L1_ffn_Wkva"]
    pad = np.zeros((D, 16), f)
    d["w_kva"] = np.concatenate([kva[:, :LAT], pad, kva[:, LAT:],
                                 kva[:, LAT:].reshape(D, ROPE // 2, 2)[..., ::-1].reshape(D, ROPE)], axis=1)
    d["wqn"] = wq[:, :, :NOPE].transpose(2, 1, 0)
    kb = np.zeros((NOPE, H, 32), f)
    kb[:, :, :LAT] = g["L1_ffn_Wkvb"].reshape(LAT, H, NOPE).transpose(2, 1, 0)
    d["wkb"] = kb
    d["won"] = g["L1_ffn_Wo"].reshape(H, 64, D)[:, :NOPE].transpose(1, 0, 2)
    for k, w, s in (("w_gate1", "Wg", "sWg"), ("w_up1", "Wu", "sWu")):
        d[k] = np.concatenate([g["L1_ffn_" + w].transpose(1, 0, 2).reshape(D, E * I1), g["L1_ffn_" + s][0]], axis=1)
    d["Wd"], d["sWd"], d["Wgate"] = g["L1_ffn_Wd"], g["L1_ffn_sWd"][0], g["L1_ffn_Wgate"]
    d.update(shape_constants())
    return {k: np.ascontiguousarray(v) for k, v in d.items()}


def kernel(**inputs):
    import concourse.bacc as bacc
    from concourse.bass_utils import run_bass_kernel_spmd

    arrays = layouts(inputs)
    nc = bacc.Bacc("TRN2", target_bir_lowering=False, num_devices=1)
    aps = {k: nc.dram_tensor(k, v.shape, mybir.dt.from_np(v.dtype), kind="ExternalInput").ap()
           for k, v in arrays.items()}
    out = nc.dram_tensor("out", (T, D), F32, kind="ExternalOutput").ap()
    build_program(nc, aps, out)
    r = run_bass_kernel_spmd(nc, [arrays], core_ids=[0])
    return r.results[0]["out"].reshape(B, S, D)
```

```python
from contextlib import ExitStack

import numpy as np

import concourse.bass as bass
from concourse import mybir

F32 = mybir.dt.float32
F16 = mybir.dt.float16
BF16 = mybir.dt.bfloat16
ALU = mybir.AluOpType
ACT = mybir.ActivationFunctionType
AX = mybir.AxisListType

P = 128
B, S, D = 2, 1024, 128
T = B * S
TT = 512
NT = T // TT
NTT = T // P
H = 16
QUAD = 4
NQ = H // QUAD
NN = B * NQ
KT = S // P
HD0 = D // H
E = 8
F0 = 256
CAP = -(-2 * T * 5 // (E * 4))
ROPE, NOPE, LAT = 32, 32, 16
I1 = 64
EPS = 1e-5
BIG = 1e30
CROW = 96
STEP = [(kt, heads) for kt in range(KT)
        for heads in ([(j,) for j in range(QUAD)] if kt * P < TT else [(0, 1), (2, 3)])]
STEPS = len(STEP)


def steps_to(kt):
    return sum(1 for t, _ in STEP if t <= kt)


SLOPE_PIECES = 3

UNITS = []
for _qt in range(KT):
    _n = (_qt + 1) * P
    for _c0 in range(0, _n, TT):
        _w = min(TT, _n - _c0)
        _per = max(1, min(QUAD, TT // _w))
        _per = {3: 2}.get(_per, _per)
        for _j in range(0, QUAD, _per):
            UNITS.append((_qt, _c0, _w, tuple(range(_j, _j + _per))))


def halves_of(kt):
    q0 = kt * P
    return [(lo, hi) for lo, hi in ((q0, TT), (max(q0, TT), S)) if lo < hi]


WORK = []
for _s in range(STEPS):
    WORK.append(("scores", _s, None))
    _kt = STEP[_s][0]
    if _kt and _s == steps_to(_kt - 1) + 1:
        WORK += [("pv", _kt - 1, piece) for piece in halves_of(_kt - 1)]
WORK += [("pv", KT - 1, piece) for piece in halves_of(KT - 1)]


def ring_plan(tail, ahead, build, terms=2):
    pe_cost = {"den": 0.9, "spread": 0.9, "proj": 0.9, "rope": 0.9, "swap": 0.9, "lat": 0.9, "unit": 0.24, "turn": 0.1}
    dve_cost = {"den": 1.0, "spread": 0.65, "proj": 0.65, "rope": 0.65, "swap": 0.65, "lat": 1.3, "unit": 0.58,
                "turn": 0.3}
    own = []
    if tail:
        own += [(3.5, "den", 0)] + [(0, "spread", h) for h in range(2)] + [(0, "proj", h) for h in range(2)]
    if build:
        own += [(12.0, kind, h) for h in range(2) for kind in ("rope", "swap", "lat")]
    units = [("unit", u) for u in UNITS] if ahead else []
    plan, t, exp_end, dve, bank_free = [], 0.0, [0.0, 0.0], 1.5 if tail else 0.0, [0.0, 0.0]
    since = 0
    for place, (what, s, piece) in enumerate(WORK):
        if what == "scores":
            cols = (S - STEP[s][0] * P) * len(STEP[s][1])
            t = max(t, exp_end[-2] + 0.1) + 0.1 + terms * cols * 0.00042
            exp_end.append(max(exp_end[-1], t + 0.2) + 0.2 + cols * 0.0007)
        else:
            t += QUAD * (piece[1] - piece[0]) * 0.0008
        while (own or units) and bank_free[len(plan) % 2] <= t:
            if own and own[0][0] <= t and (not units or since >= 0 or own[0][1] in ("den", "spread", "proj")):
                _, kind, arg = own.pop(0)
                since = 0
            elif units:
                kind, arg = units.pop(0)
                since += 1
            else:
                break
            l = len(plan)
            plan.append((place, kind, arg))
            t += pe_cost[kind]
            dve = max(dve, t + 0.15) + dve_cost[kind]
            bank_free[l % 2] = dve + 0.1
            if kind == "den":
                own = [(dve + 0.1 if kd == "spread" else at, kd, ar) for at, kd, ar in own]
    last = len(WORK) - 1
    plan += [(last, kind, arg) for _, kind, arg in own] + [(last, kind, arg) for kind, arg in units]
    if ahead:
        plan.append((min(last, max(TURN, plan[-1][0] + 1)), "turn", 0))
    return plan


TURN = WORK.index(("scores", STEPS - 4, None))


def build_program(nc, a, out):
    with ExitStack() as ctx:
        def sb(name, shape, dt=F32):
            return ctx.enter_context(nc.sbuf_tensor(name, shape, dt))

        def sem(name):
            return ctx.enter_context(nc.semaphore(name))

        XT = sb("XT", [P, T])
        XN = sb("XN", [P, T])
        YA = sb("YA", [P, T])
        QS = sb("QS", [P, H, S], F16)
        KS = sb("KS", [P, H, S], F16)
        PR = sb("PR", [P, 2, QUAD, S])
        VS = sb("VS", [P, KT, QUAD, 32])
        OS = sb("OS", [P, S])
        ON = sb("ON", [P, S])
        RD = sb("RD", [P, KT * QUAD])
        RX = sb("RX", [P, S])
        HL = sb("HL", [P, 4, T], F16)
        WM = sb("WM", [P, 6144])
        QSf = QS[:, :, :].rearrange("p h s -> p (h s)").bitcast(F32)
        KSf = KS[:, :, :].rearrange("p h s -> p (h s)").bitcast(F32)
        PRf = PR[:, :, :, :].rearrange("p a j s -> p (a j s)")

        HLw = HL[:, :, :].rearrange("p a t -> p (a t)").bitcast(F32)
        w_in = WM[:, 0:4096].rearrange("p (e f) -> p e f", e=E)
        w_out = WM[:, 4096:6144].rearrange("p (e c o) -> p e c o", e=E, c=2)
        at = [0]

        def wm(n):
            at[0] += n
            assert at[0] <= 6144
            return WM[:, at[0] - n:at[0]]

        cosT, sinT = wm(S), wm(S)
        w_rope = wm(512).rearrange("p (g m) -> p g m", g=NQ)
        w_swap = wm(512).rearrange("p (g m) -> p g m", g=NQ)
        w_kva = wm(96)
        w_gate1 = wm(9 * I1)
        w_up1 = wm(9 * I1)
        w_down1 = wm(5 * P).rearrange("p (g o) -> p g o", g=5)
        w_rt1 = wm(E)
        wo0 = sb("wo0", [P, NQ, P])
        wo1 = sb("wo1", [P, NQ, P])
        w_lat = sb("w_lat", [P, NQ, P])
        wq0 = sb("wq0", [P, 3, P])
        w_rt0 = sb("w_rt0", [P, E])
        brow = sb("brow", [P, E])
        colp = sb("colp", [P, 20])
        stage = sb("stage", [P, P])
        wqn = HLw[0:32, 0:2048].rearrange("p (h m) -> p h m", h=H)
        wkb = HLw[0:32, 2048:2560].rearrange("p (h m) -> p h m", h=H)
        won = [x[0:32, :].rearrange("p (h m) -> p h m", h=H // 2) for x in (OS, ON)]

        mean_w = sb("mean_w", [P, P])
        identf = sb("identf", [P, P])
        identb = sb("identb", [P, P], BF16)
        maskqk = sb("maskqk", [P, P], BF16)
        maskkq = sb("maskkq", [P, P], BF16)
        lessall = sb("lessall", [P, P], BF16)
        goon = sb("goon", [P, 256])
        onesb = sb("onesb", [P, P], BF16)
        sel0 = sb("sel0", [P, P])
        sel1 = sb("sel1", [P, P])
        desc = sb("desc", [P, E])
        epsc = sb("epsc", [P, 5])
        BM = sb("BM", [P, 2, QUAD, KT])
        M4 = sb("M4", [P, QUAD * KT])
        CT = sb("CT", [QUAD * KT, P], F16)
        rt = PRf[:, 5120:7680].rearrange("p (n c) -> p n c", n=10)
        ohb = sb("ohb", [P, 256], BF16)
        gT = sb("gT", [P, P])

        def pr_part(o, n):
            return PRf[:, o:o + n]

        NSQ = pr_part(0, 2048).rearrange("p (a t) -> p a t", a=NT)
        NRS = pr_part(2048, 4096).rearrange("p (a b t) -> p a b t", a=NT, b=2)
        GB = pr_part(0, 8192).rearrange("p (a e t) -> p a e t", a=2, e=E)
        GE0 = HLw[:, 0:1536].rearrange("p (a t) -> p a t", a=3)
        HF = HLw[:, 1536:2560].rearrange("p (a t) -> p a t", a=2)
        HH = HLw[:, 2560:3328].bitcast(F16).rearrange("p (a t) -> p a t", a=3)
        HQ = HLw[:, 3328:4096].bitcast(F16).rearrange("p (a t) -> p a t", a=3)
        XH, XL = (YA[:, :].bitcast(F16)[:, i * T:(i + 1) * T] for i in range(2))
        QSh = QS[:, :, :].rearrange("p h s -> p (h s)")
        WIH, WIL = (QSh[:, i * 4096:(i + 1) * 4096].rearrange("p (e f) -> p e f", e=E) for i in range(2))
        WOH, WOL = (QSh[:, 8192 + i * 2048:10240 + i * 2048].rearrange("p (e c o) -> p e c o", e=E, c=2)
                    for i in range(2))
        WGUH, WGUL = (QSh[:, i * 1152:(i + 1) * 1152].rearrange("p (w f) -> p w f", w=2) for i in range(2))
        WDH, WDL = (QSh[:, 2304 + i * 640:2944 + i * 640].rearrange("p (g o) -> p g o", g=5) for i in range(2))
        KH, KL = OS[:, :].bitcast(F16), ON[:, :].bitcast(F16)
        V0 = YA[:, :].rearrange("p (i c) -> p i c", i=NTT)
        VL = sb("VL", [P, NTT, LAT])
        KSh = KS[:, :, :].rearrange("p h s -> p (h s)")
        XQH, XQL = (KSh[:, i:i + T] for i in (4 * S, 4 * S + T))
        WQH, WQL = (KSh[:, 12 * S + i * 1536:12 * S + (i + 1) * 1536].rearrange("p (w m) -> p w m", w=3)
                    for i in range(2))
        BT = sb("BT", [P, 4, TT])
        XP = QSf[:, 0:2 * (S + 2)].rearrange("p (b s) -> p b s", b=B)
        MX = QSf[:, 2560:2560 + T]
        SG = QSf[:, 5120:5120 + T]
        DTm = KSf[:, 0:T]
        BTm = KSf[:, T:2 * T]
        CTm = KSf[:, 2 * T:3 * T]
        DEC = KSf[:, 3 * T:4 * T]
        ST_ = pr_part(5120, T)
        TMP = BT[:, :, :]
        F1 = QSf[:, 0:2048].rearrange("p (a c t) -> p a c t", a=2, c=2)
        w_inp = sb("w_inp", [P, 2, P])
        w_dbc = sb("w_dbc", [P, 3, P])
        w_outp = sb("w_outp", [P, P])
        w_f1 = sb("w_f1", [P, 2, P])
        w_f2 = sb("w_f2", [P, 2, P])

        ps = [ctx.enter_context(nc.psum_tensor(f"ps{i}", [P, 2, TT], F32)) for i in range(4)]

        def bank(i):
            return ps[i // 2][:, i % 2, :]

        RING = (4, 5)
        OUTP = ps[3]

        gate_d = nc.dram_tensor("gates", (4, E, T), F32, kind="Internal").ap()
        parts_d = nc.dram_tensor("parts", (B, 4, P, S), F16, kind="Internal").ap()

        s_x0 = sem("s_x0")
        s_w = sem("s_w")
        s_wm = sem("s_wm")
        s_wl = sem("s_wl")
        s_const = sem("s_const")
        s_ld = sem("s_ld")
        s_comp = sem("s_comp")
        s_compd = sem("s_compd")
        s_xup = sem("s_xup")
        s_mean, s_xc, s_sq, s_var = sem("s_mean"), sem("s_xc"), sem("s_sq"), sem("s_var")
        s_rs, s_xn, s_va = sem("s_rs"), sem("s_xn"), sem("s_va")
        s_r1 = sem("s_r1")
        s_y1 = sem("s_y1")
        s_rpe, s_rdv, s_rac = sem("s_rpe"), sem("s_rdv"), sem("s_rac")
        s_gw = sem("s_gw")
        s_xh, s_xl = sem("s_xh"), sem("s_xl")
        s_wh, s_wlo = sem("s_wh"), sem("s_wlo")
        s_gg = sem("s_gg")
        s_hf = sem("s_hf")
        s_hh = sem("s_hh")
        s_gb = [sem(f"s_gb{g}") for g in range(4)]
        s_ag, s_ge, s_hid, s_out = sem("s_ag"), sem("s_ge"), sem("s_hid"), sem("s_out")
        s_hg = sem("s_hg")
        s_zero = sem("s_zero")
        s_cdma = sem("s_cdma")
        s_stk = sem("s_stk")
        s_crow = sem("s_crow")
        s_st = sem("s_st")
        s_exp = sem("s_exp")
        s_pv = sem("s_pv")
        s_rr = sem("s_rr")
        s_rd = sem("s_rd")
        s_m4 = sem("s_m4")
        s_vs = sem("s_vs")
        s_wqh, s_wql = sem("s_wqh"), sem("s_wql")
        s_xqh, s_xql = sem("s_xqh"), sem("s_xql")
        s_den = sem("s_den")
        s_wos = sem("s_wos")
        s_os = sem("s_os")
        s_kb = sem("s_kb")
        s_bnc = sem("s_bnc")
        s_wc = sem("s_wc")
        s_lat = sem("s_lat")
        s_sp, s_sa, s_sd, s_so = sem("s_sp"), sem("s_sa"), sem("s_sd"), sem("s_so")
        s_fin, s_store = sem("s_fin"), sem("s_store")
        s_dve = sem("s_dve")
        s_act = sem("s_act")
        s_pool = sem("s_pool")

        class Chain:

            def __init__(self, eng, s):
                self.eng, self.s, self.n = eng, s, 0

            def up(self, ins):
                ins.then_inc(self.s, 1)
                self.n = self.n + 1

            def wait(self):
                self.eng.wait_ge(self.s, self.n)

            def link(self, ins):
                self.up(ins)
                self.wait()

        (C_L1G, C_L1B, C_INB0, C_INB1, C_DW0, C_DW1, C_DW2, C_DWB, C_DTB, C_BB, C_CB, C_A, C_DSK,
         C_OB, C_L2G, C_L2B, C_F1B0, C_F1B1, C_F2B, C_NA) = range(20)
        colw = sb("colw_sb", [P, 4])

        def tsl(t, n=TT):
            return bass.ds(t * n, n)

        def sp_load(sp):
            sp.dma_start(PRf[:, 0:T].rearrange("p (i d) -> p i d", i=NTT),
                         a["x"].rearrange("(i p) d -> p i d", p=P)).then_inc(s_x0, 16)
            loads = [
                (w_rt0[:, :], a["Wg0"]), (wq0[:, :, :], a["Wqkv0"].rearrange("n p m -> p n m")),
                (wo0[:, :, :], a["WoPad0"].rearrange("g p m -> p g m")),
                (brow[:, :], a["expert_bias"].to_broadcast([P, E])), (colp[:, 0:19], a["cols"]), (colw[:, 0:2], a["colw"]),
                (w_inp[:, :, :], a["in_W"].rearrange("p (c m) -> p c m", c=2)),
                (w_dbc[:, 0, :], a["dt_W"]), (w_dbc[:, 1, :], a["b_W"]), (w_dbc[:, 2, :], a["c_W"]),
                (w_outp[:, :], a["out_W"]),
                (w_f1[:, :, :], a["f1_W"].rearrange("p (c m) -> p c m", c=2)),
                (w_f2[:, :, :], a["f2_W"].rearrange("(c p) m -> p c m", p=P)),
            ]
            for dst, src in loads:
                sp.dma_start(dst, src).then_inc(s_w, 16)
            load_moe_weights(sp)

            for dst, src in ((wqn, a["wqn"]), (wkb, a["wkb"]), (won[0], a["won"][:, 0:H // 2]),
                             (won[1], a["won"][:, H // 2:H])):
                sp.dma_start(dst, src).then_inc(s_wc, 16)

        N_WFIRST = 16 * 13

        def load_moe_weights(sp):
            sp.dma_start(w_in, a["W_in"].rearrange("e p f -> p e f")).then_inc(s_wm, 16)
            sp.dma_start(w_out, a["W_out"].rearrange("e (c p) o -> p e c o", p=P)).then_inc(s_wm, 16)

        N_CONST = 12

        def pool_const(pool):
            ch = Chain(pool, s_pool)
            for m in (identf, sel0, sel1):
                ch.up(pool.memset(m[:, :], 0.0))
            for m in (identb, maskqk, maskkq):
                ch.up(pool.memset(m[:, :], 0.0))
            ch.up(pool.memset(lessall[:, :], -1.0))
            ch.up(pool.memset(goon[:, :], 1.0))
            ch.wait()
            for m in (identf, identb):
                pool.affine_select(out=m[:, :], in_=m[:, :], compare_op=ALU.not_equal, fill=1.0, base=0,
                                   pattern=[[-1, P]], channel_multiplier=1).then_inc(s_const, 1)
            pool.affine_select(out=maskqk[:, :], in_=maskqk[:, :], compare_op=ALU.is_ge, fill=-BIG, base=0,
                               pattern=[[-1, P]], channel_multiplier=1).then_inc(s_const, 1)
            pool.affine_select(out=maskkq[:, :], in_=maskkq[:, :], compare_op=ALU.is_ge, fill=-BIG, base=0,
                               pattern=[[1, P]], channel_multiplier=-1).then_inc(s_const, 1)
            pool.affine_select(out=lessall[:, :], in_=lessall[:, :], compare_op=ALU.is_ge, fill=0.0, base=0,
                               pattern=[[-1, P]], channel_multiplier=1).then_inc(s_const, 1)
            pool.memset(goon[:, :].rearrange("p (e b) -> p e b", e=E)[:, :, 0:1], 0.0).then_inc(s_const, 1)
            for m, r in ((sel0, HD0), (sel1, LAT)):
                pool.affine_select(out=m[:, :].rearrange("p (j c) -> p j c", j=QUAD),
                                   in_=m[:, :].rearrange("p (j c) -> p j c", j=QUAD),
                                   compare_op=ALU.not_equal, fill=1.0, base=-r,
                                   pattern=[[-32, QUAD], [0, 32]], channel_multiplier=1).then_inc(s_const, 1)
            pool.memset(onesb[:, :], 1.0).then_inc(s_const, 1)
            pool.memset(mean_w[:, :], 1.0 / D).then_inc(s_const, 1)
            pool.memset(BM[:, :, :, :], -3e38).then_inc(s_const, 1)
            for e in range(E):
                ins = pool.memset(desc[:, e:e + 1], float(E - e))
            pool.memset(epsc[:, 0:1], EPS)
            ins = pool.memset(epsc[:, 1:2], EPS * EPS)
            ins.then_inc(s_const, 1)

        def pe_load(pe):
            pe.wait_ge(s_const, N_CONST)
            pe.wait_ge(s_x0, 16)
            for i in range(NTT):
                ins = pe.transpose(bank(i // 4)[:, (i % 4) * P:(i % 4 + 1) * P],
                                   PRf[:, i * P:(i + 1) * P], identf[:, :])
                if i % 4 == 3:
                    ins.then_inc(s_ld, 1)

        def dve_load(dve):
            for t in range(NT):
                dve.wait_ge(s_ld, t + 1)
                dve.tensor_copy(XT[:, t * TT:(t + 1) * TT], bank(t)).then_inc(s_xup, 1)

        def norm_src(mode):
            return YA if mode in ("rms", "ln2") else XT

        def pe_norm(pe, k, mode, ready):
            src = norm_src(mode)
            pe.wait_ge(*ready)
            for t in range(NT):
                pe.matmul(bank(t), mean_w[:, :], src[:, tsl(t)], start=True, stop=True).then_inc(s_mean, 1)
            for t in range(NT):
                pe.wait_ge(s_sq, 4 * k + t + 1)
                pe.matmul(bank(4 + t), mean_w[:, :], NSQ[:, t, :], start=True, stop=True).then_inc(s_var, 1)

        def dve_norm(dve, k, mode, w=None, b=None, ch=None, prev=None):
            src = norm_src(mode)

            centred = YA if mode == "fused" else XN

            def center(t):
                dve.wait_ge(s_mean, 4 * k + t + 1)
                if mode == "rms":
                    dve.tensor_copy(XN[:, tsl(t)], src[:, tsl(t)]).then_inc(s_xc, 1)
                else:
                    dve.tensor_tensor(centred[:, tsl(t)], src[:, tsl(t)], bank(t), ALU.subtract).then_inc(s_xc, 1)

            def scale(t):
                dve.wait_ge(s_rs, 4 * k + t + 1)
                r = NRS[:, t, 1 if mode == "fused" else 0, :]
                if w is None:
                    dve.tensor_tensor(XN[:, tsl(t)], XN[:, tsl(t)], r, ALU.mult).then_inc(s_xn, 1)
                elif b is None:
                    dve.scalar_tensor_tensor(out=XN[:, tsl(t)], in0=centred[:, tsl(t)], scalar=w, in1=r,
                                             op0=ALU.mult, op1=ALU.mult).then_inc(s_xn, 1)
                else:
                    ch.link(dve.scalar_tensor_tensor(out=XN[:, tsl(t)], in0=centred[:, tsl(t)], scalar=w, in1=r,
                                                     op0=ALU.mult, op1=ALU.mult))
                    dve.tensor_scalar(XN[:, tsl(t)], XN[:, tsl(t)], b, None, ALU.add).then_inc(s_xn, 1)

            for t in range(NT):
                center(t)
            for t in range(NT):
                scale(t)

        FUSED = (3, 5, 7)

        def act_norm(act, k, mode, ch):
            act.activation(epsc[:, 4:5], epsc[:, 0:1], ACT.Ln)
            sq = YA if mode == "fused" else XN
            for t in range(NT):
                act.wait_ge(s_xc, 4 * k + t + 1)
                act.activation(NSQ[:, t, :], sq[:, tsl(t)], ACT.Square).then_inc(s_sq, 1)
            w = 1 if mode == "fused" else 0
            for t in range(NT):
                act.wait_ge(s_var, 4 * k + t + 1)
                act.activation(NRS[:, t, w, :], bank(4 + t), ACT.Ln, bias=epsc[:, w:w + 1],
                               scale=1.0 + EPS if w else 1.0).then_inc(s_va, 1)
                if w:
                    ch.up(act.copy(NRS[:, t, 0, :], bank(4 + t)))
            for t in range(NT):
                act.wait_ge(s_va, 4 * k + t + 1)
                act.activation(NRS[:, t, w, :], NRS[:, t, w, :], ACT.Exp, scale=-0.5).then_inc(s_rs, 1)

        def act_first_factor(act, ch):
            ch.wait()
            for t in range(NT):
                ch.up(act.activation(NRS[:, t, 0, :], NRS[:, t, 0, :], ACT.Ln, bias=epsc[:, 0:1]))
            ch.wait()
            for t in range(NT):
                act.activation(NRS[:, t, 0, :], NRS[:, t, 0, :], ACT.Exp, scale=-0.5).then_inc(s_r1, 1)

        def pool_first_norm(pool, k):
            pool.wait_ge(s_xn, 4 * (k + 1))
            for t in range(NT):
                pool.wait_ge(s_r1, NT * FUSED.index(k) + t + 1)
                pool.tensor_tensor(YA[:, tsl(t)], YA[:, tsl(t)], NRS[:, t, 0, :], ALU.mult).then_inc(s_y1, 1)

        def pe_router(pe, r, kn, w, cap):
            for i in range(NTT):
                if i % 4 == 0:
                    pe.wait_ge(s_xn, 4 * kn + i // 4 + 1)
                o = bank(0)[:, i * E:(i + 1) * E]
                ins = pe.matmul(o, XN[:, i * P:(i + 1) * P], w, start=True, stop=True)
            ins.then_inc(s_rpe, 1)
            if cap:
                pe.wait_ge(s_rdv, 3 * r + 2)
                pe.matmul(bank(1)[:, 0:256], lessall[:, :], ohb[:, :], start=True, stop=True)
                pe.matmul(bank(2)[:, 0:256], onesb[:, :], ohb[:, :], start=True, stop=True).then_inc(s_rpe, 1)
            pe.wait_ge(s_rdv, 3 * r + 3)
            ins = pe.transpose(bank(3)[:, 0:P], rt[:, 0, 0:P], identf[:, :])
            ins.then_inc(s_rpe, 1 if cap else 2)

        def act_router(act, r):
            act.wait_ge(s_rdv, 3 * r + 1)
            act.activation(rt[:, 1, 0:P], rt[:, 0, 0:P], ACT.Exp).then_inc(s_rac, 1)

        def dve_router(dve, r, cap, ch):
            def v3(i, o=0):
                return rt[:, i, o:o + P].rearrange("p (i e) -> p i e", e=E)

            def over_e(x):
                return x.unsqueeze(2).to_broadcast([P, NTT, E])

            m = [rt[:, 9, 16 * q:16 * q + 16] for q in range(8)]
            first = desc[:, :].unsqueeze(1).to_broadcast([P, NTT, E])
            dve.wait_ge(s_rpe, 3 * r + 1)
            lg = bank(0)[:, 0:P].rearrange("p (i e) -> p i e", e=E)
            if not cap:
                ch.link(dve.tensor_tensor(v3(2), lg, brow[:, :].unsqueeze(1).to_broadcast([P, NTT, E]), ALU.add))
                lg = v3(2)
            ch.link(dve.tensor_reduce(m[0], lg, AX.X, ALU.max))
            dve.tensor_tensor(v3(0), lg, over_e(m[0]), ALU.subtract).then_inc(s_rdv, 1)
            dve.wait_ge(s_rdv, 3 * r + 1)
            ch.link(dve.scalar_tensor_tensor(out=v3(3), in0=v3(0), scalar=0.0, in1=first,
                                             op0=ALU.is_equal, op1=ALU.mult))
            ch.link(dve.tensor_reduce(m[4], v3(3), AX.X, ALU.max))
            ch.link(dve.tensor_tensor(v3(4, 0), v3(3), over_e(m[4]), ALU.is_equal))
            ch.link(dve.scalar_tensor_tensor(out=v3(5), in0=v3(4, 0), scalar=-BIG, in1=v3(0),
                                             op0=ALU.mult, op1=ALU.add))
            ch.link(dve.tensor_reduce(m[3], v3(5), AX.X, ALU.max))
            ch.link(dve.tensor_tensor(v3(3), v3(5), over_e(m[3]), ALU.is_equal))
            ch.link(dve.tensor_tensor(v3(3), v3(3), first, ALU.mult))
            ch.link(dve.tensor_reduce(m[4], v3(3), AX.X, ALU.max))
            ch.link(dve.tensor_tensor(v3(4, P), v3(3), over_e(m[4]), ALU.is_equal))
            oh = rt[:, 4, :]
            if cap:
                def by_e(x):
                    return x.rearrange("p (b e) -> p e b", e=E)

                def eb(x):
                    return x.rearrange("p (e b) -> p e b", e=E)

                dve.tensor_copy(eb(ohb[:, :]), by_e(oh)).then_inc(s_rdv, 1)
                dve.wait_ge(s_rac, r + 1)
                ch.up(dve.tensor_reduce(m[1], v3(1), AX.X, ALU.add))
                dve.wait_ge(s_rpe, 3 * r + 2)
                ch.link(dve.tensor_tensor_scan(rt[:, 6, :], goon[:, :], bank(2)[:, 0:256], 0.0, ALU.mult, ALU.add))
                ch.link(dve.tensor_tensor(rt[:, 7, :], rt[:, 6, :], bank(1)[:, 0:256], ALU.add))
                ch.link(dve.scalar_tensor_tensor(out=by_e(rt[:, 8, :]), in0=eb(rt[:, 7, :]), scalar=float(CAP),
                                                 in1=by_e(oh), op0=ALU.is_lt, op1=ALU.mult))
                kept = rt[:, 8, :]
            else:
                dve.memset(ohb[:, 0:8], 0.0).then_inc(s_rdv, 1)
                dve.wait_ge(s_rac, r + 1)
                kept = oh
            ch.link(dve.tensor_tensor(rt[:, 5, 0:P], kept[:, 0:P], kept[:, P:256], ALU.add))
            ch.link(dve.tensor_tensor(v3(5), v3(5), v3(1), ALU.mult))
            ch.link(dve.tensor_reduce(m[5], v3(5), AX.X, ALU.add))
            if cap:
                ch.link(dve.scalar_tensor_tensor(out=m[5], in0=m[1], scalar=1e-9, in1=m[5],
                                                 op0=ALU.mult, op1=ALU.max))
            ch.link(dve.reciprocal(m[6], m[5]))
            dve.tensor_tensor(rt[:, 0, 0:P].rearrange("p (e i) -> p i e", e=E), v3(5), over_e(m[6]),
                              ALU.mult).then_inc(s_rdv, 1)
            dve.wait_ge(s_rpe, 3 * r + 3)
            dve.tensor_copy(gT[:, :], bank(3)[:, 0:P]).then_inc(s_hg, 1)

        def sp_gates(sp, r, halves):
            sp.wait_ge(s_hg, r + 1)
            sp.dma_start(gate_d[r].rearrange("e (i t) -> (e i) t", t=P), gT[:, :]).then_inc(s_gw, 16)
            sp.wait_ge(s_gw, 16 * (r + 1))
            for t in range(NT):
                if t >= 2:
                    sp.wait_ge(s_gg, ag_base(r) + (t - 1) * (ST1 if halves else ST0))
                for g in range(4):
                    if halves:
                        for h in range(2):
                            src = gate_d[r, 2 * g + h:2 * g + h + 1, t * TT:(t + 1) * TT]
                            sp.dma_start(GB[64 * h:64 * h + 64, t % 2, g, :],
                                         src.to_broadcast([64, TT])).then_inc(s_gb[g], 16)
                    else:
                        src = gate_d[r, 2 * g:2 * g + 2, t * TT:(t + 1) * TT].unsqueeze(0)
                        sp.dma_start(GB[:, t % 2, 2 * g:2 * g + 2, :],
                                     src.to_broadcast([P, 2, TT])).then_inc(s_gb[g], 32)
                for g in range(4):
                    sp.wait_ge(s_gb[g], 32 * (4 * r + t + 1))

        ST0 = 2 * E
        ST1 = 5

        def ag_base(r):
            return (0, NT * ST0, 2 * NT * ST0, 2 * NT * ST0 + NT * ST1)[r]

        def pairbank(u, g):
            return bank(2 + 2 * (u % 3) + g)

        W_UP, H_UP = 2.0 ** 8, 2.0 ** 4
        LAG = 3

        def moe_plan(r):
            steps = []
            if r < 2:
                for e in range(E):
                    for c in range(2):
                        fs = [slice(g * F0 + c * P, g * F0 + (c + 1) * P) for g in range(2)]
                        steps.append((P, e, e, [(WIH[:, e, f], WIL[:, e, f]) for f in fs],
                                      (WOH[:, e, c, :], WOL[:, e, c, :])))
                return steps
            for g in range(ST1):
                n = P if g < 4 else I1
                fs = slice(g * P, g * P + n)
                steps.append((n, g, g if g < 4 else None, [(WGUH[:, w, fs], WGUL[:, w, fs]) for w in range(2)],
                              (WDH[0:n, g, :], WDL[0:n, g, :])))
            return steps

        def moe_chunk(r, c):
            if r < 2:
                return [(w_in[:, c, :], WIH[:, c, :], WIL[:, c, :]),
                        (w_out[:, c, :, :], WOH[:, c, :, :], WOL[:, c, :, :])]
            n = P if c < 4 else I1
            fs = slice(c * P, c * P + n)
            return [(w_gate1[:, fs], WGUH[:, 0, fs], WGUL[:, 0, fs]), (w_up1[:, fs], WGUH[:, 1, fs], WGUL[:, 1, fs]),
                    (w_down1[0:n, c, :], WDH[0:n, c, :], WDL[0:n, c, :])]

        def moe_chunks(r):
            return E if r < 2 else ST1

        def chunk_base(r):
            return sum(moe_chunks(i) for i in range(r))

        def moe_schedule(r):
            plan = moe_plan(r)
            per = len(plan)
            each = per // moe_chunks(r)
            rows = []
            for u in range(NT * per):
                t, i = divmod(u, per)
                chunk = i // each + 2
                rows.append((u, t, plan[i], chunk if t == 0 and i % each == 0 and chunk < moe_chunks(r) else None,
                             t + 1 if i == per // 2 and t + 1 < NT else None))
            return rows

        def moe_parts(r):
            return (XH, XL) if r < 2 else (XQH, XQL)

        def pool_moe(pool, r):
            base, per = ag_base(r), len(moe_plan(r))
            for u, t, (n, _, gate, _, _), _, _ in moe_schedule(r):
                if gate is None:
                    pool.memset(epsc[:, 3:4], 0.0).then_inc(s_gg, 1)
                    continue
                pool.wait_ge(s_gb[gate // 2 if r < 2 else gate], 32 * (4 * r + t + 1))
                pool.wait_ge(s_ge, base + u + 1)
                pool.tensor_tensor(GE0[:, u % 3, :], GE0[:, u % 3, :], GB[:, t % 2, gate, :], ALU.mult).then_inc(s_gg, 1)

        def pe_moe(pe, r):
            base, plan = ag_base(r), moe_plan(r)
            per, (xh, xl) = len(plan), moe_parts(r)

            def three(dst, w, x, start, stop):
                pe.matmul(dst, w[0], x[0], start=start, stop=False)
                pe.matmul(dst, w[1], x[0], start=False, stop=False)
                return pe.matmul(dst, w[0], x[1], start=False, stop=stop)

            def out_mm(v):
                t, i = divmod(v, per)
                n, _, _, _, down = plan[i]
                pe.wait_ge(s_hid, base + v + 1)
                if i == 0 and t >= 2:
                    pe.wait_ge(s_xup, xup_base["moe", r] + t - 1)
                three(bank(t % 2), down, (HH[0:n, v % 3, :], HQ[0:n, v % 3, :]), i == 0,
                      i == per - 1).then_inc(s_out, 1)

            pe.wait_ge(s_rdv, 3 * (r + 1))
            pe.wait_ge(s_hg, r + 1)
            for u, t, (n, chunk, _, ws, _), _, _ in moe_schedule(r):
                if u % per == 0:
                    pe.wait_ge(s_xl, 4 * r + t + 1)
                if t == 0:
                    pe.wait_ge(s_wlo, chunk_base(r) + chunk + 1)
                if u >= 3:
                    pe.wait_ge(s_hf, base + u - 2)
                for g in range(2):
                    ins = three(pairbank(u, g)[0:n, :], ws[g], (xh[:, tsl(t)], xl[:, tsl(t)]), True, True)
                ins.then_inc(s_ag, 1)
                if u >= LAG:
                    out_mm(u - LAG)
            for v in range(NT * per - LAG, NT * per):
                out_mm(v)

        def act_moe(act, r):
            base, plan = ag_base(r), moe_plan(r)
            per, (xh, _) = len(plan), moe_parts(r)

            def weights(c):
                for w, high_, _ in moe_chunk(r, c):
                    ins = act.activation(high_, w, ACT.Copy, scale=W_UP)
                ins.then_inc(s_wh, 1)

            def inputs(t):
                act.copy(xh[:, tsl(t)], XN[:, tsl(t)]).then_inc(s_xh, 1)

            def high(v):
                n = plan[v % per][0]
                act.wait_ge(s_hf, base + v + 1)
                if v >= 3:
                    act.wait_ge(s_out, base + v - 2)
                act.copy(HH[0:n, v % 3, :], HF[0:n, v % 2, :]).then_inc(s_hh, 1)

            act.wait_ge(s_wm if r < 2 else s_wl, 32 if r < 2 else N_WL)
            inputs(0)
            weights(0)
            weights(1)
            for u, t, (n, _, _, _, _), chunk, tile in moe_schedule(r):
                act.wait_ge(s_ag, base + u + 1)
                if u >= 3:
                    act.wait_ge(s_hf, base + u - 2)
                act.activation(GE0[0:n, u % 3, :], pairbank(u, 0)[0:n, :], ACT.Gelu if r < 2 else ACT.Silu,
                               scale=1.0 / W_UP).then_inc(s_ge, 1)
                if u:
                    high(u - 1)
                if chunk is not None:
                    weights(chunk)
                if tile is not None:
                    inputs(tile)
            high(NT * per - 1)

        def dve_moe(dve, r, ch):
            base, plan = ag_base(r), moe_plan(r)
            per, (xh, xl) = len(plan), moe_parts(r)

            def weights(c):
                dve.wait_ge(s_wh, chunk_base(r) + c + 1)
                for w, high_, low_ in moe_chunk(r, c):
                    ins = dve.scalar_tensor_tensor(out=low_, in0=w, scalar=W_UP, in1=high_,
                                                   op0=ALU.mult, op1=ALU.subtract)
                ins.then_inc(s_wlo, 1)

            def inputs(t):
                dve.wait_ge(s_xh, 4 * r + t + 1)
                dve.tensor_tensor(xl[:, tsl(t)], XN[:, tsl(t)], xh[:, tsl(t)], ALU.subtract).then_inc(s_xl, 1)

            def low(v):
                n = plan[v % per][0]
                dve.wait_ge(s_hh, base + v + 1)
                if v >= 3:
                    dve.wait_ge(s_out, base + v - 2)
                dve.tensor_tensor(HQ[0:n, v % 3, :], HF[0:n, v % 2, :], HH[0:n, v % 3, :],
                                  ALU.subtract).then_inc(s_hid, 1)

            def update(t):
                dve.wait_ge(s_out, base + (t + 1) * per)
                down = 1.0 / (W_UP * H_UP)
                if r < 2:
                    dve.scalar_tensor_tensor(out=XT[:, tsl(t)], in0=bank(t % 2), scalar=0.5 * down,
                                             in1=XT[:, tsl(t)], op0=ALU.mult, op1=ALU.add).then_inc(s_xup, 1)
                else:
                    ch.link(dve.scalar_tensor_tensor(out=YA[:, tsl(t)], in0=bank(t % 2), scalar=down,
                                                     in1=YA[:, tsl(t)], op0=ALU.mult, op1=ALU.add))
                    dve.scalar_tensor_tensor(out=XT[:, tsl(t)], in0=YA[:, tsl(t)], scalar=0.5, in1=XT[:, tsl(t)],
                                             op0=ALU.mult, op1=ALU.add).then_inc(s_xup, 1)

            dve.wait_ge(s_wm if r < 2 else s_wl, 32 if r < 2 else N_WL)
            inputs(0)
            weights(0)
            weights(1)
            for u, t, (n, _, _, _, _), chunk, tile in moe_schedule(r):
                dve.wait_ge(s_gg, base + u + 1)
                dve.wait_ge(s_ge, base + u + 1)
                if u >= 2:
                    dve.wait_ge(s_hid, base + u - 1)
                dve.scalar_tensor_tensor(out=HF[0:n, u % 2, :], in0=pairbank(u, 1)[0:n, :], scalar=H_UP / W_UP,
                                         in1=GE0[0:n, u % 3, :], op0=ALU.mult, op1=ALU.mult).then_inc(s_hf, 1)
                if u:
                    low(u - 1)
                if chunk is not None:
                    weights(chunk)
                if tile is not None:
                    inputs(tile)
                if u % per == LAG + 1 and t:
                    update(t - 1)
            low(NT * per - 1)
            update(NT - 1)

        def iterations(latent):
            if latent:
                return [(0, 1, False, True, True), (1, NN - 2, True, True, True),
                        (NN - 2, NN - 1, True, True, False), (NN - 1, NN, True, False, False)]
            return [(0, 1, False, True, False), (1, NN - 1, True, True, False), (NN - 1, NN, True, False, False)]

        def quad_builds(m):
            return [(kind, m, h) for h in range(2) for kind in ("rope", "swap", "lat")]

        PROLOGUE = ([("qk", w, 2 * b_ + t) for b_ in range(B) for w in range(2) for t in range(2)]
                    + [("values", 0, t) for t in range(NT)],
                    [("key", 0, 0), ("key", 0, 1)] + quad_builds(0) + [("key", 0, 2), ("key", 0, 3)]
                    + quad_builds(1) + [("values", 0, 0)])

        def pro(k):
            return PROLOGUE[int(k > 0)]

        def pro_end(k, *item):
            return ring_first(k) + pro(k).index(item) + 1

        TAIL = [("den", 0)] + [("spread", h) for h in range(2)] + [("proj", h) for h in range(2)]

        def ring_starts(k):
            lat = k > 0
            n = sum(ring_total(i) for i in range(k)) + len(pro(k)) + len(ring_plan(False, True, False))
            starts = []
            for lo, hi, tail, ahead, build in iterations(lat):
                starts.append(n)
                n += (hi - lo) * len(ring_plan(tail, ahead, build))
            return starts, n

        def ring_total(k):
            lat = k > 0
            n = len(pro(k)) + len(ring_plan(False, True, False)) + len(TAIL)
            for lo, hi, tail, ahead, build in iterations(lat):
                n += (hi - lo) * len(ring_plan(tail, ahead, build))
            return n

        def ring_first(k):
            return sum(ring_total(i) for i in range(k))

        def run(eng, k, body):
            starts, end = ring_starts(k)
            for (lo, hi, tail, ahead, build), r0 in zip(iterations(k > 0), starts):
                per = len(ring_plan(tail, ahead, build))
                if hi - lo == 1:
                    body(lo, r0, tail, ahead, build, lo == 0)
                else:
                    with eng.Fori(0, hi - lo) as i:
                        body(i + lo, i * per + r0, tail, ahead, build, False)
            return end

        def slot(n):
            return (n % NQ) * QUAD

        def seq(n):
            return n // NQ

        STK = (6 * 16, 4 * 16)

        def stk_base(k):
            return NN * STK[0] * min(k, 1) + NN * STK[1] * max(k - 1, 0)

        def pe_unit(pe, k, n, u, bnk):
            qt, c0, w, heads = u
            for o, j in enumerate(heads):
                dst = bnk[:, o * w:(o + 1) * w]
                q = QS[0:CROW, bass.ds(slot(n) + j, 1), qt * P:(qt + 1) * P].squeeze(1)
                if k == 0:
                    key = KS[0:CROW, bass.ds(slot(n) + j, 1), c0:c0 + w].squeeze(1)
                else:
                    key = KS[0:CROW, bass.ds(seq(n), 1), c0:c0 + w].squeeze(1)
                diag = c0 + w == (qt + 1) * P
                ins = pe.matmul(dst, q, key, start=True, stop=not diag)
                if diag:
                    ins = pe.matmul(dst[:, w - P:w], identb[:, :], maskqk[:, :], start=False, stop=True)
            return ins

        def pe_scores(pe, k, n, s):
            kt, heads = STEP[s]
            q0 = kt * P
            for j in heads:
                for lo, hi in halves_of(kt):
                    b0 = lo // TT if len(heads) == 1 else j % 2
                    dst = ps[s % 2][:, b0, lo % TT:lo % TT + hi - lo]
                    diag = lo == q0
                    if k == 0:
                        terms = [(slot(n) + j, CROW + 1)]
                    else:
                        terms = [(seq(n), CROW + 1), (seq(n) + B, CROW)]
                    for i, (ks, rows) in enumerate(terms):
                        ins = pe.matmul(dst, KS[0:rows, bass.ds(ks, 1), q0:q0 + P].squeeze(1),
                                        QS[0:rows, bass.ds(slot(n) + j, 1), lo:hi].squeeze(1),
                                        start=(i == 0), stop=(i == len(terms) - 1 and not diag))
                    if diag:
                        ins = pe.matmul(dst[:, 0:P], identb[:, :], maskkq[:, :], start=False, stop=True)
            ins.then_inc(s_st, 1)

        def pe_pv(pe, k, n, kt, piece, first):
            lo, hi = piece
            if piece == halves_of(kt)[0]:
                pe.wait_ge(s_exp, STEPS * NN * k + n * STEPS + steps_to(kt))
                if kt == 0:
                    pe.wait_ge(s_vs, NN * k + n + 1)
                    if not first:
                        pe.wait_ge(s_os, 2 * NN * k + 2 * n)
            for j in range(QUAD):
                ins = pe.matmul(OUTP[32 * j:32 * j + 32, lo // TT, lo % TT:lo % TT + hi - lo],
                                VS[:, kt, j, :], PR[:, kt % 2, j, lo:hi], start=(kt == 0),
                                stop=(kt == (3 if lo < TT else KT - 1)))
            if piece == halves_of(kt)[-1]:
                ins.then_inc(s_pv, 1)

        def pe_build(pe, bnk, kind, m, h):
            w = ("rope", "swap", "lat").index(kind)
            wq, x = bass.ds((m % NQ) * P, P), bass.ds(seq(m) * S + h * TT, TT)
            pe.matmul(bnk, WQH[:, w, wq], XQH[:, x], start=True, stop=False)
            pe.matmul(bnk, WQL[:, w, wq], XQH[:, x], start=False, stop=False)
            return pe.matmul(bnk, WQH[:, w, wq], XQL[:, x], start=False, stop=True)

        def pe_ring(pe, k, n, kind, arg, r, l):
            pe.wait_ge(s_rd, r - 1 if l >= 2 else r)
            bnk = bank(RING[l % 2])
            if kind == "unit":
                ins = pe_unit(pe, k, n + 1, arg, bnk)
            elif kind == "turn":
                pe.wait_ge(s_m4, NN * k + n + 2)
                ins = pe.transpose(bnk[0:QUAD * KT, 0:P], M4[:, :], identf[:, :])
            elif kind == "den":
                pe.wait_ge(s_os, 2 * NN * k + 2 * n)
                pick = (sel1 if k else sel0)[:, :].rearrange("p (j c) -> p j c", j=QUAD)[:, :, 0]
                for c in range(KT):
                    ins = pe.matmul(bnk[:, c * QUAD:(c + 1) * QUAD], OS[:, c * P:(c + 1) * P], pick,
                                    start=True, stop=True)
            elif kind == "spread":
                pe.wait_ge(s_rd, r)
                for i in range(KT // 2):
                    c = arg * (KT // 2) + i
                    ins = pe.matmul(bnk[:, i * P:(i + 1) * P], RX[:, c * P:(c + 1) * P], identf[:, :],
                                    start=True, stop=True)
            elif kind == "proj":
                pe.wait_ge(s_wos, NN * k + n)
                ins = pe.matmul(bnk, stage[:, :], ON[:, arg * TT:(arg + 1) * TT], start=True, stop=True)
            else:
                ins = pe_build(pe, bnk, kind, n + 2, arg)
            ins.then_inc(s_rr, 1)

        def pe_attn(pe, k, kn):
            r = ring_first(k)
            pe.wait_ge(s_xn, 4 * (kn + 1))
            pe.wait_ge(s_w, N_WFIRST)
            if k:
                pe.wait_ge(s_wl, N_WL)
            for l, (kind, m, t) in enumerate(pro(k)):
                if l >= 2:
                    pe.wait_ge(s_rd, r + l - 1)
                elif k:
                    pe.wait_ge(s_rd, r)
                o = bank(RING[l % 2])
                if kind == "qk":
                    ins = pe.matmul(o, wq0[:, m, :], XN[:, tsl(t)], start=True, stop=True)
                elif kind == "values" and k == 0:
                    for i in range(4):
                        ins = pe.matmul(o[:, i * P:(i + 1) * P], XN[:, (4 * t + i) * P:(4 * t + i + 1) * P],
                                        wq0[:, 2, :], start=True, stop=True)
                elif kind == "values":
                    for i in range(NTT):
                        ins = pe.matmul(o[:, i * LAT:(i + 1) * LAT], XN[:, i * P:(i + 1) * P], w_kva[:, 0:LAT],
                                        start=True, stop=True)
                elif kind == "key":
                    ins = pe.matmul(o[0:96, :], w_kva, XN[:, tsl(t)], start=True, stop=True)
                else:
                    if kind == "rope":
                        pe.wait_ge(s_wql, k)
                        pe.wait_ge(s_xql, NT * (k - 1) + t + 1)
                    ins = pe_build(pe, o, kind, m, t)
                ins.then_inc(s_rr, 1)
            l = len(pro(k))
            pe.wait_ge(s_stk, stk_base(k) + STK[int(k > 0)])
            pe.wait_ge(s_zero, ZERO[k])
            if k:
                pe.wait_ge(s_kdma, KDMA * (B * (k - 1) + 1))
            else:
                pe.wait_ge(s_cdma, 16 * 2)
            for i, (_, kind, arg) in enumerate(ring_plan(False, True, False)):
                pe_ring(pe, k, -1, kind, arg, r + l, l)
                l += 1

            def body(n, r0, tail, ahead, build, first):
                uses = list(enumerate(ring_plan(tail, ahead, build)))
                pe.wait_ge(s_crow, 16 * (NN * k + n + 1))
                landed = not ahead
                for place, (what, s, piece) in enumerate(WORK):
                    if what == "scores":
                        if not (first and s < 2 and k == 0):
                            pe.wait_ge(s_exp, STEPS * NN * k + n * STEPS + s - 1)
                        pe_scores(pe, k, n, s)
                    else:
                        pe_pv(pe, k, n, s, piece, first)
                    for at_, (after, kind, arg) in uses:
                        if after == place:
                            if kind == "unit" and not landed:
                                pe.wait_ge(s_stk, stk_base(k) + STK[int(k > 0)] * (n + 2))
                                landed = True
                            pe_ring(pe, k, n, kind, arg, r0 + at_, at_)

            if k:
                pe.wait_ge(s_kdma, KDMA * B * k)
                pe.wait_ge(s_xql, NT * k)
            end = run(pe, k, body)
            for i, (kind, arg) in enumerate(TAIL):
                pe_ring(pe, k, NN, kind, arg, end + i, i)

        def act_attn(act, k, ch):
            if k:
                act.wait_ge(s_wl, N_WL)
                for w, m in enumerate((w_rope, w_swap, w_lat[:, :, :])):
                    ins = act.activation(WQH[:, w, :].rearrange("p (g m) -> p g m", g=NQ), m, ACT.Copy, scale=W_UP)
                ins.then_inc(s_wqh, 1)
                for t in range(NT):
                    act.wait_ge(s_xn, 4 * NORM_OF[k] + t + 1)
                    act.copy(XQH[:, tsl(t)], XN[:, tsl(t)]).then_inc(s_xqh, 1)
                act_first_factor(act, ch)
                act.wait_ge(s_y1, NT * (FUSED.index(NORM_OF[k]) + 1))
            def body(n, r0, tail, ahead, build, first):
                for s in range(STEPS):
                    kt, heads = STEP[s]
                    q0 = kt * P
                    act.wait_ge(s_st, STEPS * NN * k + n * STEPS + s + 1)
                    if heads[0] == 0 and not (first and kt < 2):
                        act.wait_ge(s_pv, 8 * NN * k + n * KT + kt - 1)
                    if len(heads) == 1:
                        dst = PR[:, kt % 2, heads[0], q0:S]
                        src = ps[s % 2][:, :, :].rearrange("p a t -> p (a t)")[:, q0:S]
                    else:
                        dst = PR[:, kt % 2, heads[0]:heads[-1] + 1, q0:S]
                        src = ps[s % 2][:, :, q0 - TT:TT]
                    act.activation(dst, src, ACT.Exp, scale=0.125 if k else 1.0).then_inc(s_exp, 1)
            run(act, k, body)

        dest = (XT, YA, YA)
        NORM_OF = (1, 3, 7)

        def dve_ring(dve, k, n, kind, arg, r, l):
            dve.wait_ge(s_rr, r + 1)
            bnk = bank(RING[l % 2])
            if kind == "unit":
                qt, c0, w, heads = arg
                dve.tensor_reduce(BM[:, c0 // TT, heads[0]:heads[0] + len(heads), qt],
                                  bnk[:, 0:w * len(heads)].rearrange("p (j w) -> p j w", w=w),
                                  AX.X, ALU.max).then_inc(s_rd, 1)
            elif kind == "turn":
                dve.tensor_copy(CT[:, :], bnk[0:QUAD * KT, 0:P]).then_inc(s_rd, 1)
            elif kind == "den":
                dve.reciprocal(RD[:, :], bnk[:, 0:KT * QUAD]).then_inc(s_den, 1)
                dve.wait_ge(s_den, NN * k + n)
                dve.tensor_copy(RX[:, :].rearrange("p (c r) -> p c r", r=32),
                                RD[:, :].unsqueeze(2).to_broadcast([P, KT * QUAD, 32])).then_inc(s_rd, 1)
            elif kind == "spread":
                hs = slice(arg * TT, (arg + 1) * TT)
                dve.tensor_tensor(ON[:, hs], OS[:, hs], bnk, ALU.mult).then_inc(s_rd, 1)
            elif kind == "proj":
                x = dest[k][:, bass.ds(seq(n - 1) * S + arg * TT, TT)]
                ins = dve.tensor_tensor(x, x, bnk, ALU.add)
                ins.then_inc(s_rd, 1)
            elif kind == "lat":
                m = n + 2
                h = arg
                if not (isinstance(m, int) and m == 0):
                    dve.wait_ge(s_bnc, bnc_base(k) + 16 * m)
                dve.tensor_scalar(HL[:, 2, h * TT:(h + 1) * TT], bnk, 1.0 / W_UP, None, ALU.mult).then_inc(s_lat, 1)
                dve.wait_ge(s_lat, 2 * NN * (k - 1) + 2 * m + h + 1)
                dve.scalar_tensor_tensor(out=HL[:, 3, h * TT:(h + 1) * TT], in0=bnk, scalar=1.0 / W_UP,
                                         in1=HL[:, 2, h * TT:(h + 1) * TT], op0=ALU.mult,
                                         op1=ALU.subtract).then_inc(s_rd, 1)
            else:
                w = ("rope", "swap").index(kind)
                m = n + 2
                if w == 0:
                    dve.wait_ge(s_kb, kb_before(k, q_item(m, arg) - 1))
                dve.scalar_tensor_tensor(out=BT[:, 2 * arg + w, :], in0=bnk, scalar=1.0 / W_UP,
                                         in1=(cosT, sinT)[w][:, arg * TT:(arg + 1) * TT],
                                         op0=ALU.mult, op1=ALU.mult).then_inc(s_rd, 1)

        def key_item(t):
            return t if t < 2 else t + 2

        def q_item(m, h):
            return 2 + h if isinstance(m, int) and m == 0 else 2 * m + (4 + h)

        def kb_before(k, item):
            return item * 3 + (k - 1) * 3 * (NT + 2 * NN)

        def bnc_base(k):
            return 16 * B * min(k, 1) + 16 * NN * max(k - 1, 0)

        def dve_plan(dve, k, n, plan, r0):
            for i, (_, kind, arg) in enumerate(plan):
                if kind == "turn":
                    dve.wait_ge(s_rd, r0 + i)
                    if not (isinstance(n, int) and k == 0 and n < 0):
                        dve.wait_ge(s_crow, 16 * (NN * k + n + 1))
                    dve.tensor_tensor(M4[:, :], BM[:, 0, :, :].rearrange("p j q -> p (j q)"),
                                      BM[:, 1, :, :].rearrange("p j q -> p (j q)"), ALU.max).then_inc(s_m4, 1)
                dve_ring(dve, k, n, kind, arg, r0 + i, i)

        def dve_copy_out(dve, k, n):
            dve.wait_ge(s_pv, 8 * NN * k + n * KT)
            for h in range(2):
                dve.tensor_copy(OS[:, h * TT:(h + 1) * TT], OUTP[:, h, :]).then_inc(s_os, 1)

        SC0 = float(np.float32(1.0) / np.sqrt(np.float32(HD0)))

        def dve_attn(dve, k, ch):
            r = ring_first(k)
            if k == 0:
                for i, (kind, w, t) in enumerate(pro(0)):
                    bnk = bank(RING[i % 2])
                    dve.wait_ge(s_rr, r + i + 1)
                    if kind == "values":
                        dve.tensor_copy(YA[:, tsl(t)], bnk).then_inc(s_rd, 1)
                        continue
                    sc = (SC0, 1.0)[w]
                    ch.link(dve.tensor_scalar(HL[:, 2 * w, tsl(t)], bnk, sc, None, ALU.mult))
                    dve.scalar_tensor_tensor(out=HL[:, 2 * w + 1, tsl(t)], in0=bnk, scalar=sc,
                                             in1=HL[:, 2 * w, tsl(t)], op0=ALU.mult,
                                             op1=ALU.subtract).then_inc(s_rd, 1)
            else:
                dve.wait_ge(s_wl, N_WL)
                dve.wait_ge(s_wqh, k)
                for w, m in enumerate((w_rope, w_swap, w_lat[:, :, :])):
                    g3 = (WQL[:, w, :].rearrange("p (g m) -> p g m", g=NQ), WQH[:, w, :].rearrange("p (g m) -> p g m", g=NQ))
                    ins = dve.scalar_tensor_tensor(out=g3[0], in0=m, scalar=W_UP, in1=g3[1],
                                                   op0=ALU.mult, op1=ALU.subtract)
                ins.then_inc(s_wql, 1)
                for i, (kind, m, t) in enumerate(pro(k)):
                    bnk = bank(RING[i % 2])
                    if kind == "values":
                        dve.wait_ge(s_rr, r + i + 1)
                        dve.tensor_copy(VL[:, :, :].rearrange("p i c -> p (i c)"),
                                        bnk[:, 0:NTT * LAT]).then_inc(s_rd, 1)
                    elif kind == "key":
                        dve.wait_ge(s_rr, r + i + 1)
                        if t >= 2:
                            dve.wait_ge(s_kb, kb_before(k, key_item(t) - 1))
                        cs = slice((t % 2) * TT, (t % 2 + 1) * TT)
                        a_ = 2 * (t % 2)
                        ch.up(dve.tensor_tensor(BT[32:64, a_, :], bnk[32:64, :], cosT[32:64, cs], ALU.mult))
                        ch.up(dve.tensor_tensor(BT[32:64, a_ + 1, :], bnk[64:96, :], sinT[64:96, cs], ALU.mult))
                        ch.link(dve.tensor_copy(KH[0:32, tsl(t)], bnk[0:32, :]))
                        dve.tensor_tensor(KL[0:32, tsl(t)], bnk[0:32, :], KH[0:32, tsl(t)],
                                          ALU.subtract).then_inc(s_rd, 1)
                    else:
                        dve_ring(dve, k, m - 2, kind, t, r + i, i)
            l = len(pro(k))
            for i, (_, kind, arg) in enumerate(ring_plan(False, True, False)):
                if kind == "turn":
                    dve.wait_ge(s_rd, r + l + i)
                    if k:
                        dve.wait_ge(s_crow, 16 * NN * k)
                    dve.tensor_tensor(M4[:, :], BM[:, 0, :, :].rearrange("p j q -> p (j q)"),
                                      BM[:, 1, :, :].rearrange("p j q -> p (j q)"), ALU.max).then_inc(s_m4, 1)
                dve_ring(dve, k, -1, kind, arg, r + l + i, l + i)

            def body(n, r0, tail, ahead, build, first):
                if tail:
                    dve_copy_out(dve, k, n)
                dve_plan(dve, k, n, ring_plan(tail, ahead, build), r0)

            if k:
                dve.wait_ge(s_kdma, KDMA * B * k)
                dve.wait_ge(s_y1, NT * (FUSED.index(NORM_OF[k]) + 1))
            end = run(dve, k, body)
            dve_copy_out(dve, k, NN)
            for i, (kind, arg) in enumerate(TAIL):
                dve_ring(dve, k, NN, kind, arg, end + i, i)
            dve.wait_ge(s_rd, end + len(TAIL))
            s_done = s_xup if k == 0 else s_ya
            dve.memset(epsc[:, 2:3], 0.0).then_inc(s_done, 4)

        s_ya = sem("s_ya")
        s_kdma = sem("s_kdma")
        KDMA = 16 * 6
        ZERO = (2 * H + 3, 2 * H + 3 + 3, 2 * H + 3 + 6)

        def pool_attn_setup(pool, k):
            if k:
                pool.wait_ge(s_xup, setup_after[k])
                pool.memset(KS[:, B:2 * B, :].rearrange("p h s -> p (h s)").bitcast(F32), 0.0).then_inc(s_zero, 1)
                pool.wait_ge(s_zero, ZERO[k] - 2)
                pool.memset(KS[CROW:CROW + 1, 0:B, :].rearrange("p h s -> p (h s)"), -1.0).then_inc(s_zero, 1)
                pool.wait_ge(s_zero, ZERO[k] - 1)
                pool.memset(VS[:, :, :, LAT:LAT + 1].rearrange("p a j c -> p (a j) c"), 1.0).then_inc(s_zero, 1)
                pool.wait_ge(s_zero, ZERO[k])
                return
            for h in range(H):
                pool.memset(KS[:, h, :].bitcast(F32), 0.0).then_inc(s_zero, 1)
            pool.memset(VS[:, :, :, :].rearrange("p a j c -> p (a j c)"), 0.0).then_inc(s_zero, 1)
            pool.wait_ge(s_zero, H + 1)
            pool.memset(KS[CROW:CROW + 1, :, :].rearrange("p h s -> p (h s)"), -1.0).then_inc(s_zero, 1)
            pool.wait_ge(s_zero, H + 2)
            pool.memset(VS[:, :, :, HD0:HD0 + 1].rearrange("p a j c -> p (a j) c"), 1.0).then_inc(s_zero, 1)

        def pool_attn(pool, k, ch):
            w_o = wo1 if k else wo0

            def input_low(t):
                pool.wait_ge(s_xqh, NT * (k - 1) + t + 1)
                pool.tensor_tensor(XQL[:, tsl(t)], XN[:, tsl(t)], XQH[:, tsl(t)], ALU.subtract).then_inc(s_xql, 1)

            def rotary(item, rings, rows, buf, hi, lo):
                pool.wait_ge(s_rd, rings)
                if isinstance(item, int) and kb_before(k, item):
                    pool.wait_ge(s_kb, kb_before(k, item))
                b0, b1 = BT[rows, buf, :], BT[rows, buf + 1, :]
                pool.tensor_tensor(hi, b0, b1, ALU.add).then_inc(s_kb, 1)
                pool.tensor_tensor(b0, b0, b1, ALU.add).then_inc(s_kb, 1)
                pool.wait_ge(s_kb, kb_before(k, item) + 2)
                pool.tensor_tensor(lo, b0, hi, ALU.subtract).then_inc(s_kb, 1)

            def parts(m, h, rings):
                hs = slice(h * TT, (h + 1) * TT)
                if not (isinstance(m, int) and m == 0):
                    pool.wait_ge(s_bnc, bnc_base(k) + 16 * m)
                rotary(q_item(m, h), rings, slice(0, P), 2 * h, HL[:, 0, hs], HL[:, 1, hs])

            def keys(t):
                rotary(key_item(t), pro_end(k, "key", 0, t), slice(32, 64), 2 * (t % 2),
                       KH[32:64, tsl(t)], KL[32:64, tsl(t)])

            r = ring_first(k)
            if k:
                pool.wait_ge(s_wl, N_WL)
                input_low(0)
                input_low(1)
                pool.wait_ge(s_xql, NT * (k - 1) + 2)
                for m in range(2):
                    keys(2 * m)
                    keys(2 * m + 1)
                    for h in range(2):
                        parts(m, h, pro_end(k, "swap", m, h))
                input_low(2)
                input_low(3)
                pool_first_norm(pool, NORM_OF[k])

            def stage_v(n, first):
                if first:
                    pool.wait_ge(s_rd, r + len(pro(k)))
                else:
                    pool.wait_ge(s_pv, 8 * NN * k + n * KT)
                pool.wait_ge(s_const, 1)
                if k == 0:
                    src = V0[:, bass.ds(seq(n) * KT, KT), bass.ds((n % NQ) * 32, 32)]
                    pool.tensor_copy(VS[:, :, :, 0:HD0], src.rearrange("p i (j d) -> p i j d", j=QUAD))\
                        .then_inc(s_vs, 1)
                else:
                    src = VL[:, bass.ds(seq(n) * KT, KT), :]
                    for j in range(QUAD):
                        ins = pool.tensor_copy(VS[:, :, j, 0:LAT], src)
                        if j < QUAD - 1:
                            ch.up(ins)
                    ch.wait()
                    ins.then_inc(s_vs, 1)

            def finish(n):
                pool.wait_ge(s_pv, 8 * NN * k + n * KT)
                pool.wait_ge(s_const, 1)
                src = w_o[:, bass.ds((n - 1) % NQ, 1), :].squeeze(1)
                pool.tensor_copy(stage[:, :], src).then_inc(s_wos, 1)

            def body(n, r0, tail, ahead, build, first):
                n_ch = ch.n
                stage_v(n, first)
                if tail:
                    finish(n)
                if build:
                    plan = ring_plan(tail, ahead, build)
                    for h in range(2):
                        at_ = max(i for i, (_, kd, ar) in enumerate(plan) if kd in ("rope", "swap") and ar == h)
                        parts(n + 2, h, r0 + at_ + 1)

            base = ch.n
            starts, end = ring_starts(k)
            for (lo, hi, tail, ahead, build), r0 in zip(iterations(k > 0), starts):
                per = len(ring_plan(tail, ahead, build))
                own = 3 if k else 0
                c0 = ch.n
                if hi - lo == 1:
                    body(lo, r0, tail, ahead, build, lo == 0)
                else:
                    with pool.Fori(0, hi - lo) as i:
                        ch.n = i * own + c0
                        body(i + lo, i * per + r0, tail, ahead, build, False)
                ch.n = c0 + own * (hi - lo)
            finish(NN)

        def sp_attn(sp, k):
            r = ring_first(k)

            def send(slot_, b_=None):
                tok = slice(0, S) if b_ is None else slice(b_ * S, (b_ + 1) * S)
                sp.dma_start(parts_d[slot_].rearrange("a p s -> p a s"), HL[:, :, tok]).then_inc(s_bnc, 16)

            Q0, K0 = ((0, 8, 0), (8, 8, 1), (16, 8, 0)), ((0, 8, 2), (8, 8, 2), (16, 8, 3))
            Q1 = ((0, 32, 0), (32, 16, 2), (48, 32, 1), (80, 16, 3))

            def put0(m):
                for st, terms in ((QS, Q0), (KS, K0)):
                    for row, n_, part in terms:
                        h0 = (m % NQ) * QUAD * HD0
                        src = parts_d[m // NQ, part, h0:h0 + QUAD * HD0, :]
                        sp.dma_start(st[row:row + n_, slot(m):slot(m) + QUAD, :],
                                     src.rearrange("(j r) s -> r j s", j=QUAD)).then_inc(s_stk, 16)

            def put1(m):
                for row, n_, part in Q1:
                    src = parts_d[0, part].rearrange("(j r) s -> r j s", j=QUAD)[0:n_]
                    sp.dma_start(QS[row:row + n_, bass.ds(slot(m), QUAD), :], src).then_inc(s_stk, 16)

            def put_keys(b_):
                tok = slice(b_ * S, (b_ + 1) * S)
                for row, n_, sl, src in ((0, 32, b_, KH[32:64, tok]), (48, 32, b_, KH[32:64, tok]),
                                         (32, 16, b_, KH[0:16, tok]), (80, 16, b_, KH[0:16, tok]),
                                         (0, 32, B + b_, KL[32:64, tok]), (32, 16, B + b_, KL[0:16, tok])):
                    sp.dma_start(KS[row:row + n_, sl, :], src).then_inc(s_kdma, 16)

            def crow(m, turned, landed=None):
                sp.wait_ge(s_rd, turned)
                if landed is not None:
                    sp.wait_ge(s_stk, landed)
                sp.dma_start(QS[CROW:CROW + 1, bass.ds(slot(m), QUAD), :], CT[:, :]).then_inc(s_crow, 16)

            first_turned = r + len(pro(k)) + len(ring_plan(False, True, False))
            starts, _ = ring_starts(k)
            if k == 0:
                sp.wait_ge(s_zero, ZERO[0])
                sp.dma_start(QS[24:24 + SLOPE_PIECES, :, :], a["slopes"]).then_inc(s_cdma, 16)
                sp.dma_start(KS[24:24 + SLOPE_PIECES, :, :], a["kpos"]).then_inc(s_cdma, 16)
                for b_ in range(B):
                    sp.wait_ge(s_rd, pro_end(0, "qk", 1, 2 * b_ + 1))
                    send(b_, b_)
                    sp.wait_ge(s_bnc, 16 * (b_ + 1))
                    put0(b_)
                    sp.wait_ge(s_stk, STK[0] * (b_ + 1))
                crow(0, first_turned)
                rr = starts[0]
                for n in range(NN - 1):
                    if n + 2 < NN:
                        if n + 2 >= NQ:
                            sp.wait_ge(s_st, STEPS * (n + 2 - NQ + 1))
                        put0(n + 2)
                        sp.wait_ge(s_stk, STK[0] * (n + 3))
                    rr += len(ring_plan(n > 0, True, False))
                    crow(n + 1, rr)
                return
            sp.wait_ge(s_zero, ZERO[k])
            for m in range(2):
                sp.wait_ge(s_kb, kb_before(k, key_item(2 * m + 1) + 1))
                sp.wait_ge(s_rd, pro_end(k, "key", 0, 2 * m + 1))
                put_keys(m)
                sp.wait_ge(s_kb, kb_before(k, q_item(m, 1) + 1))
                sp.wait_ge(s_rd, pro_end(k, "lat", m, 1))
                send(0)
                sp.wait_ge(s_bnc, bnc_base(k) + 16 * (m + 1))
                put1(m)
                sp.wait_ge(s_kdma, KDMA * (B * (k - 1) + m + 1))
                sp.wait_ge(s_stk, stk_base(k) + STK[1] * (m + 1))
            crow(0, first_turned)
            for (lo, hi, tail, ahead, build), r0 in zip(iterations(True), starts):
                plan = ring_plan(tail, ahead, build)

                def it(n, r0):
                    if build:
                        lat_at = max(i for i, (_, kd, _) in enumerate(plan) if kd == "lat")
                        sp.wait_ge(s_rd, r0 + lat_at + 1)
                        sp.wait_ge(s_kb, kb_before(k, q_item(n + 2, 2)))
                        send(0)
                        sp.wait_ge(s_bnc, bnc_base(k) + 16 * (n + 3))
                        put1(n + 2)
                    if ahead:
                        crow(n + 1, r0 + len(plan), stk_base(k) + STK[1] * (n + 3) if build else None)
                if hi - lo == 1:
                    it(lo, r0)
                else:
                    with sp.Fori(0, hi - lo) as i:
                        it(i + lo, i * len(plan) + r0)

        def sp_last_weights(sp):
            sp.wait_ge(s_xup, xup_base["moe", 1] + 4)
            loads = [(cosT, a["cosT"]), (sinT, a["sinT"]), (w_rope, a["w_rope"].rearrange("p (g m) -> p g m", g=NQ)),
                     (w_swap, a["w_swap"].rearrange("p (g m) -> p g m", g=NQ)), (w_kva, a["w_kva"]),
                     (w_gate1, a["w_gate1"]), (w_up1, a["w_up1"]), (w_down1[:, 0:4, :], a["Wd"].rearrange("(g e) i o -> (e i) g o", e=2)),
                     (w_down1[0:I1, 4, :], a["sWd"]), (w_rt1, a["Wgate"])]
            for dst, src in loads:
                sp.dma_start(dst, src).then_inc(s_wl, 16)

        N_WL = 16 * 10

        def pe_comp(pe):
            pe.wait_ge(s_wc, 64)
            for h in range(H):
                ins = pe.matmul(bank(6)[:, h * 32:(h + 1) * 32], wqn[:, h, :], wkb[:, h, :], start=True, stop=True)
            ins.then_inc(s_comp, 1)
            for h in range(H):
                g, j = divmod(h, QUAD)
                ins = pe.matmul(bank(7)[32 * j:32 * j + 32, g * P:(g + 1) * P], wkb[:, h, :], won[h // 8][:, h % 8, :],
                                start=True, stop=True)
            ins.then_inc(s_comp, 1)

        def act_comp(act):
            act.wait_ge(s_comp, 1)
            act.copy(w_lat[:, :, :].rearrange("p g m -> p (g m)"), bank(6)).then_inc(s_compd, 1)
            act.wait_ge(s_comp, 2)
            act.copy(wo1[:, :, :].rearrange("p g m -> p (g m)"), bank(7)).then_inc(s_compd, 1)

        A_ABS, A_LN, A_DEC, A_FFN = 2 * NT, 3 * NT, 4 * NT, 5 * NT
        s_sg = sem("s_sg")

        def dbc_bank(t, w):
            return bank(2 + 3 * (t % 2) + w)

        def pe_scan(pe, kn):
            for t in range(NT):
                pe.wait_ge(s_xn, 4 * kn + t + 1)
                if t >= 2:
                    pe.wait_ge(s_sa, 2 * (t - 1))
                if t == 0:
                    pe.wait_ge(s_xn, 4 * (kn + 1))
                pe.matmul(bank(2 * (t % 2)), w_inp[:, 0, :], XN[:, tsl(t)], start=True, stop=True)
                pe.matmul(bank(2 * (t % 2) + 1), w_inp[:, 1, :], XN[:, tsl(t)], start=True,
                          stop=True).then_inc(s_sp, 1)
            pe.wait_ge(s_sa, A_ABS)
            for t in range(NT):
                pe.wait_ge(s_sd, 1 + t // 2)
                if t >= 2:
                    pe.wait_ge(s_sa, A_ABS + t - 1)
                for w in range(3):
                    ins = pe.matmul(dbc_bank(t, w), w_dbc[:, w, :], MX[:, tsl(t)], start=True, stop=True)
                ins.then_inc(s_sp, 1)
            for t in range(NT):
                pe.wait_ge(s_sd, 3 + t // 2)
                if t >= 2:
                    pe.wait_ge(s_ya, 4 + t - 1)
                pe.matmul(bank(5 + t % 2), w_outp[:, :], DTm[:, tsl(t)], start=True, stop=True).then_inc(s_sp, 1)

        def act_scan(act, ch):
            for t in range(NT):
                b_, o = divmod(t * TT, S)
                act.wait_ge(s_sp, t + 1)
                act.activation(XP[:, b_, 1 + o:1 + o + TT], bank(2 * (t % 2)), ACT.Identity,
                               bias=colp[:, C_INB0:C_INB0 + 1]).then_inc(s_sa, 1)
                act.activation(SG[:, tsl(t)], bank(2 * (t % 2) + 1), ACT.Sigmoid,
                               bias=colp[:, C_INB1:C_INB1 + 1]).then_inc(s_sa, 1)
            act_first_factor(act, ch)
            ch.link(act.activation(colw[:, 2:3], colp[:, C_A:C_A + 1], ACT.Exp))
            ch.link(act.mul(colw[:, 3:4], colw[:, 2:3], -1.0))
            for t in range(NT):
                act.wait_ge(s_sp, NT + t + 1)
                act.activation(BTm[:, tsl(t)], dbc_bank(t, 1), ACT.Tanh, bias=colp[:, C_BB:C_BB + 1])
                act.activation(CTm[:, tsl(t)], dbc_bank(t, 2), ACT.Tanh, bias=colp[:, C_CB:C_CB + 1])
                act.wait_ge(s_so, t + 1)
                act.activation(DEC[:, tsl(t)], dbc_bank(t, 0), ACT.Abs,
                               bias=colp[:, C_DTB:C_DTB + 1]).then_inc(s_sa, 1)
                act.wait_ge(s_sa, A_ABS + t + 1)
                ch.up(act.activation(DEC[:, tsl(t)], DEC[:, tsl(t)], ACT.Exp, scale=-1.0))
            ch.wait()
            for t in range(NT):
                act.activation(DEC[:, tsl(t)], DEC[:, tsl(t)], ACT.Ln, bias=1.0).then_inc(s_sa, 1)
            for t in range(NT):
                act.wait_ge(s_so, NT + t + 1)
                act.activation(DEC[:, tsl(t)], DTm[:, tsl(t)], ACT.Exp, scale=colw[:, 3:4]).then_inc(s_sa, 1)

        def pool_scan(pool):
            pool_first_norm(pool, 5)
            for t in range(NT):
                if t % 2 == 0:
                    pool.wait_ge(s_sd, 1 + t // 2)
                pool.wait_ge(s_sa, A_ABS + t + 1)
                pool.tensor_tensor(BTm[:, tsl(t)], BTm[:, tsl(t)], MX[:, tsl(t)], ALU.mult)
                pool.tensor_tensor(CTm[:, tsl(t)], CTm[:, tsl(t)], SG[:, tsl(t)], ALU.mult).then_inc(s_sg, 1)
                pool.tensor_tensor(SG[:, tsl(t)], MX[:, tsl(t)], SG[:, tsl(t)], ALU.mult).then_inc(s_sg, 1)

        def dve_scan(dve, kn, ch):
            def col(c):
                return colp[:, c:c + 1]

            dve.wait_ge(s_xn, 4 * (kn + 1))
            for b_ in range(B):
                ch.up(dve.memset(XP[:, b_, 0:1], 0.0))
                ch.up(dve.memset(XP[:, b_, S + 1:S + 2], 0.0))
            for b_ in range(B):
                dve.wait_ge(s_sa, 4 * (b_ + 1))
                ch.wait()
                m = MX[:, b_ * S:(b_ + 1) * S]
                ch.link(dve.tensor_scalar(m, XP[:, b_, 1:S + 1], col(C_DW1), col(C_DWB), ALU.mult, ALU.add))
                ch.link(dve.scalar_tensor_tensor(out=m, in0=XP[:, b_, 0:S], scalar=col(C_DW0), in1=m,
                                                 op0=ALU.mult, op1=ALU.add))
                dve.scalar_tensor_tensor(out=m, in0=XP[:, b_, 2:S + 2], scalar=col(C_DW2), in1=m,
                                         op0=ALU.mult, op1=ALU.add).then_inc(s_sd, 1)
            for t in range(NT):
                dve.wait_ge(s_sp, NT + t + 1)
                dve.tensor_scalar(DTm[:, tsl(t)], dbc_bank(t, 0), col(C_DTB), 0.0, ALU.add,
                                  ALU.max).then_inc(s_so, 1)
            dve.wait_ge(s_so, NT)
            for t in range(NT):
                dve.wait_ge(s_sa, A_LN + t + 1)
                dve.tensor_tensor(DTm[:, tsl(t)], DTm[:, tsl(t)], DEC[:, tsl(t)], ALU.add).then_inc(s_so, 1)
            dve.wait_ge(s_so, 2 * NT)
            for b_ in range(B):
                c = slice(b_ * S, (b_ + 1) * S)
                dve.wait_ge(s_sg, 4 * (b_ + 1))
                ch.link(dve.tensor_tensor(BTm[:, c], BTm[:, c], DTm[:, c], ALU.mult))
                dve.wait_ge(s_sa, A_DEC + 2 * (b_ + 1))
                ch.link(dve.tensor_tensor_scan(ST_[:, c], DEC[:, c], BTm[:, c], 0.0, ALU.mult, ALU.add))
                ch.link(dve.tensor_tensor(ST_[:, c], ST_[:, c], CTm[:, c], ALU.mult))
                dve.scalar_tensor_tensor(out=DTm[:, c], in0=SG[:, c], scalar=col(C_DSK), in1=ST_[:, c],
                                         op0=ALU.mult, op1=ALU.add).then_inc(s_sd, 1)
            dve.wait_ge(s_y1, NT * (FUSED.index(5) + 1))
            for t in range(NT):
                dve.wait_ge(s_sp, 2 * NT + t + 1)
                dve.scalar_tensor_tensor(out=YA[:, tsl(t)], in0=bank(5 + t % 2), scalar=col(C_OB),
                                         in1=YA[:, tsl(t)], op0=ALU.add, op1=ALU.add).then_inc(s_ya, 1)

        def pe_ffn(pe, kn):
            def down(t):
                pe.wait_ge(s_sa, A_FFN + 2 * (t + 1))
                if t >= 2:
                    pe.wait_ge(s_xup, xup_base["scan", 0] + t - 1)
                for c in range(2):
                    ins = pe.matmul(bank(2 + t % 2), w_f2[:, c, :], F1[:, t % 2, c, :], start=(c == 0), stop=(c == 1))
                ins.then_inc(s_sp, 1)

            pe.wait_ge(s_xn, 4 * (kn + 1))
            for t in range(NT):
                if t >= 2:
                    pe.wait_ge(s_sa, A_FFN + 2 * (t - 1))
                for c in range(2):
                    ins = pe.matmul(bank(4 * (t % 2) + c), w_f1[:, c, :], XN[:, tsl(t)], start=True, stop=True)
                ins.then_inc(s_sp, 1)
                if t:
                    down(t - 1)
            down(NT - 1)

        def out_count(t):
            return 3 * NT + (2 * t + 3 if t < NT - 1 else 2 * NT)

        def act_ffn(act):
            for t in range(NT):
                act.wait_ge(s_sp, 3 * NT + 1 if t == 0 else 3 * NT + 2 * t)
                if t >= 2:
                    act.wait_ge(s_sp, out_count(t - 2))
                for c in range(2):
                    act.activation(F1[:, t % 2, c, :], bank(4 * (t % 2) + c), ACT.Gelu,
                                   bias=colp[:, C_F1B0 + c:C_F1B0 + c + 1]).then_inc(s_sa, 1)

        def dve_ffn(dve, ch):
            for t in range(NT):
                dve.wait_ge(s_sp, out_count(t))
                ch.link(dve.scalar_tensor_tensor(out=YA[:, tsl(t)], in0=bank(2 + t % 2),
                                                 scalar=colp[:, C_F2B:C_F2B + 1], in1=YA[:, tsl(t)],
                                                 op0=ALU.add, op1=ALU.add))
                dve.tensor_tensor(XT[:, tsl(t)], XT[:, tsl(t)], YA[:, tsl(t)], ALU.add).then_inc(s_xup, 1)

        def pe_store(pe):
            pe.wait_ge(s_xup, xup_base["end", 0])
            for i in range(NTT):
                ins = pe.transpose(bank(i // 4)[:, (i % 4) * P:(i % 4 + 1) * P], XT[:, i * P:(i + 1) * P], identf[:, :])
                if i % 4 == 3:
                    ins.then_inc(s_ld, 1)

        def dve_store(dve):
            for t in range(NT):
                dve.wait_ge(s_ld, NT + t + 1)
                dve.tensor_copy(XN[:, tsl(t)], bank(t)).then_inc(s_fin, 1)

        def sp_store(sp):
            for t in range(NT):
                sp.wait_ge(s_fin, t + 1)
                sp.dma_start(out.rearrange("(i p) d -> p i d", p=P)[:, 4 * t:4 * t + 4, :],
                             XN[:, tsl(t)].rearrange("p (i d) -> p i d", i=4)).then_inc(s_store, 16)
            sp.wait_ge(s_store, 16 * NT)

        xup_base = {("moe", 0): 4, ("attn", 0): 8, ("moe", 1): 12, ("moe", 2): 16, ("scan", 0): 20,
                    ("moe", 3): 24, ("end", 0): 28}
        setup_after = {1: 16, 2: 24}

        block = ctx.enter_context(nc.Block())

        @block.sync
        def _(sp):
            sp_load(sp)
            sp_gates(sp, 0, False)
            sp_attn(sp, 0)
            sp.wait_ge(s_xup, 12)
            sp_gates(sp, 1, False)
            sp_last_weights(sp)
            sp_attn(sp, 1)
            sp_gates(sp, 2, True)
            sp_attn(sp, 2)
            sp_gates(sp, 3, True)
            sp_store(sp)

        @block.gpsimd
        def _(pool):
            pool_const(pool)
            ch = Chain(pool, s_pool)
            ch.n = 8
            pool_attn_setup(pool, 0)
            pool_moe(pool, 0)
            pool.wait_ge(s_out, ag_base(1))
            for h in range(H):
                pool.memset(QS[:, h, :].bitcast(F32), 0.0).then_inc(s_zero, 1)
            pool_attn(pool, 0, ch)
            pool_moe(pool, 1)
            pool_attn_setup(pool, 1)
            pool_attn(pool, 1, ch)
            pool_moe(pool, 2)
            pool_scan(pool)
            pool_attn_setup(pool, 2)
            pool_attn(pool, 2, ch)
            pool_moe(pool, 3)

        @block.scalar
        def _(act):
            ch = Chain(act, s_act)
            act.wait_ge(s_const, N_CONST)
            act_norm(act, 0, "plain", ch)
            act_router(act, 0)
            act_comp(act)
            act_moe(act, 0)
            act_norm(act, 1, "plain", ch)
            act_attn(act, 0, ch)
            act_norm(act, 2, "plain", ch)
            act_router(act, 1)
            act_moe(act, 1)
            act_norm(act, 3, "fused", ch)
            act_attn(act, 1, ch)
            act_norm(act, 4, "rms", ch)
            act_router(act, 2)
            act_moe(act, 2)
            act_norm(act, 5, "fused", ch)
            act_scan(act, ch)
            act_norm(act, 6, "ln2", ch)
            act_ffn(act)
            act_norm(act, 7, "fused", ch)
            act_attn(act, 2, ch)
            act_norm(act, 8, "rms", ch)
            act_router(act, 3)
            act_moe(act, 3)

        @block.tensor
        def _(pe):
            pe_load(pe)
            pe_norm(pe, 0, "plain", (s_xup, 4))
            pe.wait_ge(s_w, N_WFIRST)
            pe_router(pe, 0, 0, w_rt0[:, :], True)
            pe_comp(pe)
            pe.wait_ge(s_compd, 2)
            pe_moe(pe, 0)
            pe_norm(pe, 1, "plain", (s_xup, 8))
            pe_attn(pe, 0, 1)
            pe_norm(pe, 2, "plain", (s_xup, 12))
            pe_router(pe, 1, 2, w_rt0[:, :], True)
            pe_moe(pe, 1)
            pe_norm(pe, 3, "fused", (s_xup, 16))
            pe_attn(pe, 1, 3)
            pe_norm(pe, 4, "rms", (s_ya, 4))
            pe.wait_ge(s_wl, N_WL)
            pe_router(pe, 2, 4, w_rt1, False)
            pe_moe(pe, 2)
            pe_norm(pe, 5, "fused", (s_xup, 20))
            pe_scan(pe, 5)
            pe_norm(pe, 6, "ln2", (s_ya, 8))
            pe_ffn(pe, 6)
            pe_norm(pe, 7, "fused", (s_xup, 24))
            pe_attn(pe, 2, 7)
            pe_norm(pe, 8, "rms", (s_ya, 12))
            pe_router(pe, 3, 8, w_rt1, False)
            pe_moe(pe, 3)
            pe_store(pe)

        @block.vector
        def _(dve):
            ch = Chain(dve, s_dve)
            dve_load(dve)
            dve.wait_ge(s_const, N_CONST)
            dve.wait_ge(s_w, N_WFIRST)
            dve_norm(dve, 0, "plain")
            dve_router(dve, 0, True, ch)
            dve_moe(dve, 0, ch)
            dve_norm(dve, 1, "plain")
            dve_attn(dve, 0, ch)
            dve_norm(dve, 2, "plain")
            dve_router(dve, 1, True, ch)
            dve_moe(dve, 1, ch)
            dve_norm(dve, 3, "fused", w=colw[:, 0:1])
            dve_attn(dve, 1, ch)
            dve_norm(dve, 4, "rms", w=colw[:, 1:2])
            dve_router(dve, 2, False, ch)
            dve_moe(dve, 2, ch)
            dve_norm(dve, 5, "fused", w=colp[:, C_L1G:C_L1G + 1], b=colp[:, C_L1B:C_L1B + 1], ch=ch)
            dve_scan(dve, 5, ch)
            dve_norm(dve, 6, "ln2", w=colp[:, C_L2G:C_L2G + 1], b=colp[:, C_L2B:C_L2B + 1], ch=ch)
            dve_ffn(dve, ch)
            dve_norm(dve, 7, "fused", w=colw[:, 0:1])
            dve_attn(dve, 2, ch)
            dve_norm(dve, 8, "rms", w=colw[:, 1:2])
            dve_router(dve, 3, False, ch)
            dve_moe(dve, 3, ch)
            dve_store(dve)


def shape_constants():
    f = np.float32
    slopes = f(1.0) / np.power(f(2.0 ** 8), (np.arange(H, dtype=f) + f(1)) / f(H), dtype=f)
    pieces, rest = [], slopes.copy()
    for _ in range(SLOPE_PIECES):
        piece = rest.astype(np.float16)
        pieces.append(piece)
        rest = rest - piece.astype(f)
    slope_rows = np.stack([np.repeat(p[:, None], S, 1) for p in pieces])
    kpos = np.broadcast_to((np.arange(S) - S // 2).astype(np.float16), (SLOPE_PIECES, H, S)).copy()
    freqs = f(1.0) / np.power(100000.0, np.arange(0, ROPE, 2) / ROPE).astype(f)
    ang = np.outer(np.arange(S, dtype=f), freqs).astype(f)
    cos, sin = np.cos(ang).astype(f), np.sin(ang).astype(f)
    c32 = np.repeat(cos.T, 2, 0)
    s32 = np.repeat(sin.T, 2, 0)
    s32[0::2] = -s32[0::2]
    return {"slopes": slope_rows, "kpos": kpos, "cosT": np.tile(c32, (4, 1)), "sinT": np.tile(s32, (4, 1))}


def layouts(i):
    g = {k: np.asarray(v) for k, v in i.items()}
    f = np.float32
    d = {"x": g["L0_attn_x"].reshape(T, D)}
    d["Wg0"], d["W_in"], d["W_out"] = g["L0_ffn_Wg"], g["L0_ffn_W_in"], g["L0_ffn_W_out"]
    d["Wqkv0"] = np.stack([g["L0_attn_W_Q"].T, g["L0_attn_W_K"].T, g["L0_attn_W_V"].T])
    wo = np.zeros((NQ, QUAD, 32, D), f)
    wo[:, :, 0:HD0, :] = g["L0_attn_W_O"].T.reshape(NQ, QUAD, HD0, D)
    d["WoPad0"] = wo.reshape(NQ, P, D)
    d["expert_bias"] = g["L1_ffn_expert_bias"].reshape(1, E)
    n = "L1_attn_"
    dw = g[n + "dw_W"].reshape(D, 3)
    d["cols"] = np.stack([g[n + "ln1_g"], g[n + "ln1_b"], g[n + "in_b"][:D], g[n + "in_b"][D:], dw[:, 0], dw[:, 1],
                          dw[:, 2], g[n + "dw_b"], g[n + "dt_b"], g[n + "b_b"], g[n + "c_b"], g[n + "a_log"],
                          g[n + "d_skip"], g[n + "out_b"], g[n + "ln2_g"], g[n + "ln2_b"], g[n + "f1_b"][:D],
                          g[n + "f1_b"][D:], g[n + "f2_b"]], axis=1)
    d["colw"] = np.stack([g["L1_ffn_w_ln1"], g["L1_ffn_w_ln2"]], axis=1)
    for k in ("in_W", "dt_W", "b_W", "c_W", "out_W", "f1_W", "f2_W"):
        d[k] = g[n + k]
    wq = g["L1_ffn_Wq"].reshape(D, H, 64)
    d["w_rope"] = wq[:, :, NOPE:].reshape(D, H * ROPE)
    d["w_swap"] = wq[:, :, NOPE:].reshape(D, H, ROPE // 2, 2)[..., ::-1].reshape(D, H * ROPE)
    kva = g["L1_ffn_Wkva"]
    pad = np.zeros((D, 16), f)
    d["w_kva"] = np.concatenate([kva[:, :LAT], pad, kva[:, LAT:],
                                 kva[:, LAT:].reshape(D, ROPE // 2, 2)[..., ::-1].reshape(D, ROPE)], axis=1)
    d["wqn"] = wq[:, :, :NOPE].transpose(2, 1, 0)
    kb = np.zeros((NOPE, H, 32), f)
    kb[:, :, :LAT] = g["L1_ffn_Wkvb"].reshape(LAT, H, NOPE).transpose(2, 1, 0)
    d["wkb"] = kb
    d["won"] = g["L1_ffn_Wo"].reshape(H, 64, D)[:, :NOPE].transpose(1, 0, 2)
    for k, w, s in (("w_gate1", "Wg", "sWg"), ("w_up1", "Wu", "sWu")):
        d[k] = np.concatenate([g["L1_ffn_" + w].transpose(1, 0, 2).reshape(D, E * I1), g["L1_ffn_" + s][0]], axis=1)
    d["Wd"], d["sWd"], d["Wgate"] = g["L1_ffn_Wd"], g["L1_ffn_sWd"][0], g["L1_ffn_Wgate"]
    d.update(shape_constants())
    return {k: np.ascontiguousarray(v) for k, v in d.items()}


def kernel(**inputs):
    import concourse.bacc as bacc
    from concourse.bass_utils import run_bass_kernel_spmd

    arrays = layouts(inputs)
    nc = bacc.Bacc("TRN2", target_bir_lowering=False, num_devices=1)
    aps = {k: nc.dram_tensor(k, v.shape, mybir.dt.from_np(v.dtype), kind="ExternalInput").ap()
           for k, v in arrays.items()}
    out = nc.dram_tensor("out", (T, D), F32, kind="ExternalOutput").ap()
    build_program(nc, aps, out)
    r = run_bass_kernel_spmd(nc, [arrays], core_ids=[0])
    return r.results[0]["out"].reshape(B, S, D)
```
